# Optimizing a Trainium2 kernel written in Bass

```python
import numpy as np
import jax
import jax.numpy as jnp

def _softmax(x, axis=-1):
    return jax.nn.softmax(x, axis=axis)

def _gelu(x):
    return jax.nn.gelu(x, approximate=True)

def _silu(x):
    return jax.nn.silu(x)

def _sigmoid(x):
    return jax.nn.sigmoid(x)

def _layernorm(x, axis=-1, eps=1e-05):
    m = jnp.mean(x, axis=axis, keepdims=True)
    v = jnp.var(x, axis=axis, keepdims=True)
    return (x - m) / jnp.sqrt(v + eps)

def _scatter_add(tgt, idx, src, axis=0):
    return tgt.at[idx].add(src)

def _segment_sum(src, seg, n):
    return jax.ops.segment_sum(src, seg, n)
kernel_name = 'mk_perceiver_d1_seqx_r4_1b18ce'

def setup_inputs(seed: int=0):
    np.random.seed(seed)
    _w = jnp.asarray

    def _rec_inputs():
        import jax
        import jax.numpy as jnp
        _rk = jax.random.key(seed)
        x = -0.0002928 + 1 * jax.random.normal(jax.random.fold_in(_rk, 1), (16, 64, 256), jnp.float32)
        _lenS = 64 - jax.random.randint(jax.random.fold_in(_rk, 7), (16,), 0, max(1, 64 // 4) + 1, jnp.int32)
        _lenS2 = 1601 - jax.random.randint(jax.random.fold_in(_rk, 8), (16,), 0, max(1, 1601 // 4) + 1, jnp.int32)
        _ctx_1024P = jax.random.normal(jax.random.fold_in(_rk, 11), (16, 16, 256), jnp.float32)
        _ctx_1024c = jax.random.dirichlet(jax.random.fold_in(_rk, 511), 0.3 * jnp.ones((16,), jnp.float32), (16, 1601))
        _ctx_1024t = jnp.einsum('bsk,bkd->bsd', _ctx_1024c, _ctx_1024P)
        _ctx_1024t = _ctx_1024t * jax.lax.rsqrt(jnp.mean(jnp.square(_ctx_1024t)) + 1e-12) * 0.953939
        ctx_1024 = -1.39393e-06 + 0.999914 * (_ctx_1024t + 0.3 * jax.random.normal(jax.random.fold_in(_rk, 611), (16, 1601, 256), jnp.float32))
        return (x, ctx_1024)
    x, ctx_1024 = _rec_inputs()

    def _L0_xattn_setup():
        import jax, jax.numpy as jnp
        import numpy as np
        import math
        D_MODEL = 256
        N_HEADS = 16
        D_HEAD = D_MODEL // N_HEADS
        key = jax.random.key(seed)
        ks = jax.random.split(key, 11)
        N, L, S = (2, 512, 512)
        inp = {'queries': jax.random.normal(ks[0], (N, L, D_MODEL), dtype=jnp.float32), 'keys': jax.random.normal(ks[1], (N, S, D_MODEL), dtype=jnp.float32), 'values': jax.random.normal(ks[2], (N, S, D_MODEL), dtype=jnp.float32), 'Wq': jax.random.normal(ks[3], (D_MODEL, N_HEADS * D_HEAD), dtype=jnp.float32) / math.sqrt(D_MODEL), 'bq': jnp.zeros((N_HEADS * D_HEAD,), dtype=jnp.float32), 'Wk': jax.random.normal(ks[4], (D_MODEL, N_HEADS * D_HEAD), dtype=jnp.float32) / math.sqrt(D_MODEL), 'bk': jnp.zeros((N_HEADS * D_HEAD,), dtype=jnp.float32), 'Wv': jax.random.normal(ks[5], (D_MODEL, N_HEADS * D_HEAD), dtype=jnp.float32) / math.sqrt(D_MODEL), 'bv': jnp.zeros((N_HEADS * D_HEAD,), dtype=jnp.float32), 'Wo': jax.random.normal(ks[6], (N_HEADS * D_HEAD, D_MODEL), dtype=jnp.float32) / math.sqrt(N_HEADS * D_HEAD), 'bo': jnp.zeros((D_MODEL,), dtype=jnp.float32)}
        return inp
    _L0_xattn_all = _L0_xattn_setup()
    _L0_xattn_in = {k: v for k, v in _L0_xattn_all.items() if k in ('Wq', 'bq', 'Wk', 'bk', 'Wv', 'bv', 'Wo', 'bo')}
    del _L0_xattn_all

    def _L0_attn_setup():
        import jax, jax.numpy as jnp
        import numpy as np
        DIM = 256
        D_STATE = 64
        D_CONV = 4
        EXPAND = 2
        D_INNER = DIM * EXPAND
        N_HEADS = D_INNER // 64
        HEAD_DIM = D_INNER // N_HEADS
        B_SZ = 1
        SEQ = 256
        D_IN_PROJ = 2 * D_INNER + 2 * D_STATE + N_HEADS
        EPS = 1e-06
        key = jax.random.key(seed)
        ks = jax.random.split(key, 9)
        x = jax.random.normal(ks[0], (B_SZ, SEQ, DIM), jnp.float32)
        W_in = jax.random.normal(ks[1], (D_IN_PROJ, DIM), jnp.float32) / np.sqrt(DIM)
        W_conv = jax.random.normal(ks[2], (D_INNER, 1, D_CONV), jnp.float32) / np.sqrt(D_CONV)
        b_conv = 0.01 * jax.random.normal(ks[3], (D_INNER,), jnp.float32)
        A_log = jnp.log(jnp.arange(1, D_STATE + 1, dtype=jnp.float32)) * jnp.ones((N_HEADS, HEAD_DIM, D_STATE), jnp.float32)
        D = jnp.ones((N_HEADS, HEAD_DIM), jnp.float32) + 0.01 * jax.random.normal(ks[4], (N_HEADS, HEAD_DIM), jnp.float32)
        dt_bias = 0.1 * jax.random.normal(ks[5], (N_HEADS,), jnp.float32)
        norm_w = jnp.ones((D_INNER,), jnp.float32) + 0.01 * jax.random.normal(ks[6], (D_INNER,), jnp.float32)
        W_out = jax.random.normal(ks[7], (DIM, D_INNER), jnp.float32) / np.sqrt(D_INNER)
        return {'x': x, 'W_in': W_in, 'W_conv': W_conv, 'b_conv': b_conv, 'A_log': A_log, 'D': D, 'dt_bias': dt_bias, 'norm_w': norm_w, 'W_out': W_out}
    _L0_attn_all = _L0_attn_setup()
    _L0_attn_in = {k: v for k, v in _L0_attn_all.items() if k in ('W_in', 'W_conv', 'b_conv', 'A_log', 'D', 'dt_bias', 'norm_w', 'W_out')}
    del _L0_attn_all

    def _L0_ffn_setup():
        import jax, jax.numpy as jnp
        import numpy as np
        D = 256
        E = 12
        HS = 2 * D
        HR = 3 * D
        TAU = 1.5

        def _geglu(h):
            a, g = jnp.split(h, 2, axis=-1)
            return a * jax.nn.gelu(g, approximate=False)
        key = jax.random.key(seed)
        ks = jax.random.split(key, 12)

        def xavier(k, shape):
            fan_in, fan_out = (shape[-2], shape[-1])
            lim = jnp.sqrt(6.0 / (fan_in + fan_out))
            return jax.random.uniform(k, shape, jnp.float32, -lim, lim)
        x = jax.random.normal(ks[0], (2, 256, D), jnp.float32)
        Ws1 = xavier(ks[1], (D, 2 * HS))
        bs1 = jnp.zeros((2 * HS,), jnp.float32)
        Ws2 = xavier(ks[2], (HS, D))
        bs2 = jnp.zeros((D,), jnp.float32)
        We1 = xavier(ks[3], (E, D, 2 * HR))
        be1 = jnp.zeros((E, 2 * HR), jnp.float32)
        We2 = xavier(ks[4], (E, HR, D))
        be2 = jnp.zeros((E, D), jnp.float32)
        Wr = xavier(ks[5], (D, E))
        br = jnp.zeros((E,), jnp.float32)
        return {'x': x, 'Ws1': Ws1, 'bs1': bs1, 'Ws2': Ws2, 'bs2': bs2, 'We1': We1, 'be1': be1, 'We2': We2, 'be2': be2, 'Wr': Wr, 'br': br}
    _L0_ffn_all = _L0_ffn_setup()
    _L0_ffn_in = {k: v for k, v in _L0_ffn_all.items() if k in ('Ws1', 'bs1', 'Ws2', 'bs2', 'We1', 'be1', 'We2', 'be2', 'Wr', 'br')}
    del _L0_ffn_all
    return {'x': x, 'ctx_1024': ctx_1024, 'L0_xattn_Wq': _L0_xattn_in['Wq'], 'L0_xattn_bq': _L0_xattn_in['bq'], 'L0_xattn_Wk': _L0_xattn_in['Wk'], 'L0_xattn_bk': _L0_xattn_in['bk'], 'L0_xattn_Wv': _L0_xattn_in['Wv'], 'L0_xattn_bv': _L0_xattn_in['bv'], 'L0_xattn_Wo': _L0_xattn_in['Wo'], 'L0_xattn_bo': _L0_xattn_in['bo'], 'L0_attn_W_in': _L0_attn_in['W_in'], 'L0_attn_W_conv': _L0_attn_in['W_conv'], 'L0_attn_b_conv': _L0_attn_in['b_conv'], 'L0_attn_A_log': _L0_attn_in['A_log'], 'L0_attn_D': _L0_attn_in['D'], 'L0_attn_dt_bias': _L0_attn_in['dt_bias'], 'L0_attn_norm_w': _L0_attn_in['norm_w'], 'L0_attn_W_out': _L0_attn_in['W_out'], 'L0_ffn_Ws1': _L0_ffn_in['Ws1'], 'L0_ffn_bs1': _L0_ffn_in['bs1'], 'L0_ffn_Ws2': _L0_ffn_in['Ws2'], 'L0_ffn_bs2': _L0_ffn_in['bs2'], 'L0_ffn_We1': _L0_ffn_in['We1'], 'L0_ffn_be1': _L0_ffn_in['be1'], 'L0_ffn_We2': _L0_ffn_in['We2'], 'L0_ffn_be2': _L0_ffn_in['be2'], 'L0_ffn_Wr': _L0_ffn_in['Wr'], 'L0_ffn_br': _L0_ffn_in['br']}

def reference(x, ctx_1024, L0_xattn_Wq, L0_xattn_bq, L0_xattn_Wk, L0_xattn_bk, L0_xattn_Wv, L0_xattn_bv, L0_xattn_Wo, L0_xattn_bo, L0_attn_W_in, L0_attn_W_conv, L0_attn_b_conv, L0_attn_A_log, L0_attn_D, L0_attn_dt_bias, L0_attn_norm_w, L0_attn_W_out, L0_ffn_Ws1, L0_ffn_bs1, L0_ffn_Ws2, L0_ffn_bs2, L0_ffn_We1, L0_ffn_be1, L0_ffn_We2, L0_ffn_be2, L0_ffn_Wr, L0_ffn_br):
    import jax
    import jax.numpy as jnp

    def _L0_xattn_ref(queries, keys, values, Wq, bq, Wk, bk, Wv, bv, Wo, bo):
        import jax, jax.numpy as jnp
        import numpy as np
        import math
        D_MODEL = 256
        N_HEADS = 16
        D_HEAD = D_MODEL // N_HEADS
        N, L, _ = queries.shape
        S = keys.shape[1]
        H, D = (N_HEADS, D_HEAD)
        q = (queries @ Wq + bq).reshape(N, L, H, D)
        k = (keys @ Wk + bk).reshape(N, S, H, D)
        v = (values @ Wv + bv).reshape(N, S, H, D)
        sm = jnp.einsum('nlhd,nshd->nlhs', q, k) / math.sqrt(D)
        sm = jax.nn.softmax(sm, axis=1)
        attn = jnp.einsum('nlhs,nshd->nlhd', sm, v).reshape(N, L, H * D)
        return attn @ Wo + bo

    def _L0_attn_ref(x, W_in, W_conv, b_conv, A_log, D, dt_bias, norm_w, W_out):
        import jax, jax.numpy as jnp
        import numpy as np
        DIM = 256
        D_STATE = 64
        D_CONV = 4
        EXPAND = 2
        D_INNER = DIM * EXPAND
        N_HEADS = D_INNER // 64
        HEAD_DIM = D_INNER // N_HEADS
        B_SZ = 1
        SEQ = 256
        D_IN_PROJ = 2 * D_INNER + 2 * D_STATE + N_HEADS
        EPS = 1e-06
        Bsz, L, _ = x.shape
        zxBCdt = x @ W_in.T
        z, xin, Bm, Cm, dt = jnp.split(zxBCdt, [D_INNER, 2 * D_INNER, 2 * D_INNER + D_STATE, 2 * D_INNER + 2 * D_STATE], axis=-1)
        xc = jnp.transpose(xin, (0, 2, 1))
        xc = jax.lax.conv_general_dilated(xc, W_conv, window_strides=(1,), padding=[(D_CONV - 1, 0)], feature_group_count=D_INNER, dimension_numbers=('NCH', 'OIH', 'NCH'))
        xc = xc + b_conv[None, :, None]
        xin = jax.nn.silu(jnp.transpose(xc, (0, 2, 1)))
        xh = xin.reshape(Bsz, L, N_HEADS, HEAD_DIM)
        A = -jnp.exp(A_log)
        dt = jax.nn.softplus(dt + dt_bias)

        def step(h_state, ins):
            x_t, dt_t, B_t, C_t = ins
            a = jnp.exp(dt_t[:, :, None, None] * A[None])
            h_state = a * h_state + B_t[:, None, None, :] * x_t[..., None]
            y_t = jnp.einsum('bhdn,bn->bhd', h_state, C_t)
            return (h_state, y_t)
        h0 = jnp.zeros((Bsz, N_HEADS, HEAD_DIM, D_STATE), x.dtype)
        xs = (jnp.moveaxis(xh, 1, 0), jnp.moveaxis(dt, 1, 0), jnp.moveaxis(Bm, 1, 0), jnp.moveaxis(Cm, 1, 0))
        _, ys = jax.lax.scan(step, h0, xs)
        y = jnp.moveaxis(ys, 0, 1)
        y = y + xh * D[None, None]
        y = y.reshape(Bsz, L, D_INNER)
        y = y * jax.nn.silu(z)
        rms = jnp.sqrt(jnp.mean(y * y, axis=-1, keepdims=True) + EPS)
        y = y / rms * norm_w
        return y @ W_out.T

    def _L0_ffn_ref(x, Ws1, bs1, Ws2, bs2, We1, be1, We2, be2, Wr, br):
        import jax, jax.numpy as jnp
        import numpy as np
        D = 256
        E = 12
        HS = 2 * D
        HR = 3 * D
        TAU = 1.5

        def _geglu(h):
            a, g = jnp.split(h, 2, axis=-1)
            return a * jax.nn.gelu(g, approximate=False)
        B, T, Dm = x.shape
        xf = x.reshape(-1, Dm)
        ys = _geglu(xf @ Ws1 + bs1) @ Ws2 + bs2
        logits = (xf @ Wr + br) / TAU
        top_val, top_idx = jax.lax.top_k(logits, 2)
        top_w = jax.nn.softmax(top_val, axis=-1)
        onehot = jax.nn.one_hot(top_idx, E, dtype=x.dtype)
        w = jnp.einsum('nke,nk->ne', onehot, top_w)
        h = jnp.einsum('nd,edh->enh', xf, We1) + be1[:, None, :]
        act = _geglu(h)
        yE = jnp.einsum('enh,ehd->end', act, We2) + be2[:, None, :]
        yr = jnp.einsum('end,ne->nd', yE, w)
        return (ys + yr).reshape(B, T, Dm)
    x = x + _L0_xattn_ref(_layernorm(x, axis=-1), ctx_1024, ctx_1024, L0_xattn_Wq, L0_xattn_bq, L0_xattn_Wk, L0_xattn_bk, L0_xattn_Wv, L0_xattn_bv, L0_xattn_Wo, L0_xattn_bo)
    x = x + _L0_attn_ref(_layernorm(x, axis=-1), L0_attn_W_in, L0_attn_W_conv, L0_attn_b_conv, L0_attn_A_log, L0_attn_D, L0_attn_dt_bias, L0_attn_norm_w, L0_attn_W_out)
    x = x + _L0_ffn_ref(_layernorm(x, axis=-1), L0_ffn_Ws1, L0_ffn_bs1, L0_ffn_Ws2, L0_ffn_bs2, L0_ffn_We1, L0_ffn_be1, L0_ffn_We2, L0_ffn_be2, L0_ffn_Wr, L0_ffn_br)
    return x

_drawn_inputs = setup_inputs


def setup_inputs(seed=0):
    import zlib

    import numpy as np

    out = dict(_drawn_inputs(seed))
    spreads = {'L0_xattn_bq': (0.0, 2.0),
     'L0_xattn_bk': (0.0, 0.1),
     'L0_xattn_bv': (0.0, 0.1),
     'L0_xattn_bo': (0.0, 0.8),
     'L0_ffn_bs1': (0.0, 0.8),
     'L0_ffn_bs2': (0.0, 2.0),
     'L0_ffn_be1': (0.0, 0.8),
     'L0_ffn_be2': (0.0, 2.0),
     'L0_ffn_br': (0.0, 0.8)}
    factors = {'L0_attn_b_conv': 8.0,
     'L0_attn_D': 8.0,
     'L0_attn_dt_bias': 8.0,
     'L0_attn_norm_w': 8.0,
     'L0_ffn_Ws1': 3.128,
     'L0_ffn_Ws2': 3.169,
     'L0_ffn_We1': 5.673,
     'L0_ffn_We2': 5.657,
     'L0_ffn_Wr': 5.595}
    for name, (base, spread) in spreads.items():
        noise = np.random.default_rng([zlib.crc32(name.encode()), seed]).standard_normal(out[name].shape)
        drawn = base * np.exp(spread * noise) if base else spread * noise
        out[name] = jnp.asarray(drawn.astype(out[name].dtype))
    for name, factor in factors.items():
        out[name] = (out[name] * factor).astype(out[name].dtype)
    return out
```

```python
from contextlib import ExitStack

import numpy as np

import concourse.bass as bass
from concourse import mybir

F32 = mybir.dt.float32
BF16 = mybir.dt.bfloat16
U32 = mybir.dt.uint32
ALU = mybir.AluOpType
ACT = mybir.ActivationFunctionType
AX_X = mybir.AxisListType.X

P = 128
NB, L, D = 16, 64, 256
TOK = NB * L
TT = TOK // P
KD = D // P
LN_EPS = 1e-5

S = 1601
H, DH = 16, 16
ROWS = [P] * (S // P) + [S % P]
NT = len(ROWS)
HC = P // DH
KCH = [(0, 401), (401, 400), (801, 400), (1201, 400)]
NK = KD * len(KCH)
SLOTS = 4
SLOT = [k for _ in range(6) for k in range(3)] + [k for _ in range(2) for k in range(4)]
LAG = 2

DI, NS, NH, HD = 512, 64, 8, 64
XC = DI // P
UNITS = P // 2
RMS_EPS = 1e-6
FAR = 2.0 ** 100
A_MIN = 1e-25

E, HR, HS = 12, 768, 512
TAU = 1.5


class Chain:

    def __init__(self, eng, sem):
        self.eng, self.sem, self.n = eng, sem, 0

    def did(self, ins):
        self.n += 1
        ins.then_inc(self.sem, 1)
        return self.n

    def wait(self):
        self.eng.wait_ge(self.sem, self.n)

    def link(self, ins):
        self.did(ins)
        self.wait()


def load_inputs(nc, d, sb):
    with ExitStack() as ctx:
        loaded = ctx.enter_context(nc.semaphore("l_loaded"))
        made = ctx.enter_context(nc.semaphore("l_made"))
        chain = ctx.enter_context(nc.semaphore("l_chain"))
        block = ctx.enter_context(nc.Block())

        @block.sync
        def _(sp):
            sp.dma_start(sb["x"][:, :, :], d["x"].rearrange("(t p) d -> p t d", p=P)).then_inc(loaded, 16)
            sp.wait_ge(loaded, 16)

        @block.gpsimd
        def _(pool):
            c = Chain(pool, made)
            c.link(pool.memset(sb["ident"][:, :], 0.0))
            c.link(pool.memset(sb["hmask"][:, :], 1.0))
            c.link(pool.memset(sb["minus_half"][:, :], -0.5))
            c.link(pool.affine_select(out=sb["ident"][:, :], in_=sb["ident"][:, :], compare_op=ALU.not_equal,
                                     fill=1.0, base=0, pattern=[[-1, P]], channel_multiplier=1))
            c.link(pool.affine_select(out=sb["hmask"][:, :], in_=sb["hmask"][:, :], compare_op=ALU.is_ge,
                                      fill=0.0, base=0, pattern=[[-DH, HC]], channel_multiplier=1))
            c.link(pool.affine_select(out=sb["hmask"][:, :], in_=sb["hmask"][:, :], compare_op=ALU.is_ge,
                                      fill=0.0, base=DH - 1, pattern=[[DH, HC]], channel_multiplier=-1))

        @block.vector
        def _(dve):
            dve.wait_ge(made, 6)
            for i in range(2):
                ins = nc.vector.tensor_reduce(sb["pmask"][:, i:i + 1], sb["hmask"][:, i::2], AX_X, ALU.add)
            ins.then_inc(chain, 1)


def layer_norm(nc, sb, tag):
    with ExitStack() as ctx:
        stats = ctx.enter_context(nc.sbuf_tensor(f"{tag}_stats", [P, TT, 6], F32))
        mv = ctx.enter_context(nc.sbuf_tensor(f"{tag}_mv", [P, TT, 2], F32))
        vare = ctx.enter_context(nc.sbuf_tensor(f"{tag}_vare", [P, TT], F32))
        rstd = ctx.enter_context(nc.sbuf_tensor(f"{tag}_rstd", [P, TT], F32))
        xln = ctx.enter_context(nc.sbuf_tensor(f"{tag}_xln", [P, TT, D], F32))
        ps = ctx.enter_context(nc.psum_tensor(f"{tag}_ps", [P, 4, 512], F32))
        chain = ctx.enter_context(nc.semaphore(f"{tag}_chain"))
        var_ready = ctx.enter_context(nc.semaphore(f"{tag}_var_ready"))
        rstd_ready = ctx.enter_context(nc.semaphore(f"{tag}_rstd_ready"))
        xln_ready = ctx.enter_context(nc.semaphore(f"{tag}_xln_ready"))
        turned = ctx.enter_context(nc.semaphore(f"{tag}_turned"))
        copied = ctx.enter_context(nc.semaphore(f"{tag}_copied"))
        block = ctx.enter_context(nc.Block())

        @block.vector
        def _(dve):
            c = Chain(dve, chain)
            for t in range(TT):
                c.did(nc.vector.bn_stats(stats[:, t, :], sb["x"][:, t, :]))
            c.wait()
            for t in range(TT):
                c.did(nc.vector.bn_aggr(mv[:, t, :], stats[:, t, :]))
            c.wait()
            nc.vector.tensor_scalar(vare[:, :], mv[:, :, 1], LN_EPS, None, ALU.add).then_inc(var_ready, 1)
            dve.wait_ge(rstd_ready, 1)
            for t in range(TT):
                nc.vector.tensor_scalar(xln[:, t, :], sb["x"][:, t, :], mv[:, t, 0:1], rstd[:, t:t + 1],
                                        ALU.subtract, ALU.mult).then_inc(xln_ready, 1)

        @block.gpsimd
        def _(pool):
            pool.wait_ge(var_ready, 1)
            pool.tensor_tensor(rstd[:, :], vare[:, :], sb["minus_half"][:, :], ALU.pow).then_inc(rstd_ready, 1)

        @block.tensor
        def _(pe):
            for t in range(TT):
                pe.wait_ge(xln_ready, t + 1)
                if t >= 4:
                    pe.wait_ge(copied, t - 3)
                for c in range(KD):
                    ins = nc.tensor.transpose(ps[:, t % 4, c * P:(c + 1) * P], xln[:, t, c * P:(c + 1) * P],
                                              sb["ident"][:, :])
                ins.then_inc(turned, 1)

        @block.scalar
        def _(act):
            for t in range(TT):
                act.wait_ge(turned, t + 1)
                nc.scalar.copy(sb["xlnT"][:, :, t * P:(t + 1) * P],
                               ps[:, t % 4, 0:KD * P].rearrange("p (c s) -> p c s", c=KD)).then_inc(copied, 1)


def query_projection(nc, d, sb, a):
    with ExitStack() as ctx:
        wq = ctx.enter_context(nc.sbuf_tensor("wq", [P, KD, D], F32))
        bq = ctx.enter_context(nc.sbuf_tensor("bq", [P, KD], F32))
        bqs = ctx.enter_context(nc.sbuf_tensor("bqs", [P, KD], F32))
        ps = ctx.enter_context(nc.psum_tensor("q_ps", [P, 4, 512], F32))
        loaded = ctx.enter_context(nc.semaphore("q_loaded"))
        rest = ctx.enter_context(nc.semaphore("q_rest"))
        scaled = ctx.enter_context(nc.semaphore("q_scaled"))
        done = ctx.enter_context(nc.semaphore("q_done"))
        block = ctx.enter_context(nc.Block())

        @block.sync
        def _(sp):
            sp.dma_start(wq[:, :, :], d["wq"].rearrange("(c p) n -> p c n", p=P)).then_inc(loaded, 16)
            sp.dma_start(bq[:, :], d["bq"]).then_inc(loaded, 16)
            for name, t in (("wk", a["wk"]), ("wv", a["wv"]), ("wo", a["wo"])):
                sp.dma_start(t[:, :, :], d[name].rearrange("(c p) n -> p c n", p=P)).then_inc(rest, 16)
            sp.dma_start(a["bk"][:, :], d["bk"]).then_inc(rest, 16)
            sp.dma_start(a["bv"][:, :], d["bv"].partition_broadcast(P)).then_inc(rest, 16)
            sp.dma_start(a["bo"][:, :], d["bo"].partition_broadcast(P)).then_inc(rest, 16)
            sp.wait_ge(rest, 96)

        @block.tensor
        def _(pe):
            pe.wait_ge(loaded, 32)
            for m in range(KD):
                for n in range(2):
                    for k in range(KD):
                        ins = nc.tensor.matmul(ps[:, 2 * m + n, :], wq[:, k, m * P:(m + 1) * P],
                                               sb["xlnT"][:, k, n * 512:(n + 1) * 512],
                                               start=(k == 0), stop=(k == KD - 1))
                    ins.then_inc(done, 1)

        @block.scalar
        def _(act):
            act.wait_ge(loaded, 32)
            nc.scalar.mul(bqs[:, :], bq[:, :], DH ** -0.5).then_inc(scaled, 1)
            act.wait_ge(scaled, 1)
            for j in range(2 * KD):
                m, n = j // 2, j % 2
                act.wait_ge(done, j + 1)
                nc.scalar.activation(a["qT"][:, m, n * 512:(n + 1) * 512], ps[:, j, :], ACT.Identity,
                                     bias=bqs[:, m:m + 1], scale=DH ** -0.5)


def attention(nc, d, sb, a):
    with ExitStack() as ctx:
        def sbuf(name, shape, dt=F32):
            return ctx.enter_context(nc.sbuf_tensor(name, shape, dt))

        def sem(name):
            return ctx.enter_context(nc.semaphore(name))

        ctxT = [sbuf(f"ctxT{b}", [P, KD, S]) for b in range(2)]
        kT = [sbuf(f"kT{b}", [P, KD, S]) for b in range(2)]
        qbd = [sbuf(f"qbd{b}", [P, KD, HC, L]) for b in range(2)]
        prob = sbuf("prob", [P, SLOTS, H, L])
        mx = sbuf("mx", [P, SLOTS, H])
        vb = sbuf("vb", [P, SLOTS, D])
        half = sbuf("half", [P, 2, H, L // 2])
        z = sbuf("z", [P, 2, H])
        rz = sbuf("rz", [P, 2, H])
        vn = sbuf("vn", [P, 2, D])
        otmp = sbuf("otmp", [P, KD, L])

        ps_s = [ctx.enter_context(nc.psum_tensor(f"ps_s{i}", [P, 2, 512], F32)) for i in range(2)]
        ps_v = [ctx.enter_context(nc.psum_tensor(f"ps_v{i}", [P, 512], F32)) for i in range(2)]
        ps_k = ctx.enter_context(nc.psum_tensor("ps_k", [P, 512], F32))
        ps_o = ctx.enter_context(nc.psum_tensor("ps_o", [P, 512], F32))

        ctx_loaded = [sem("ctx_loaded0"), sem("ctx_loaded1")]
        qbd_ready = sem("qbd_ready")
        k_product = sem("k_product")
        kT_ready = sem("kT_ready")
        v_product = sem("v_product")
        vb_ready = sem("vb_ready")
        scores_ready = sem("scores_ready")
        max_ready = sem("max_ready")
        sub_ready = sem("sub_ready")
        exp_ready = sem("exp_ready")
        half_ready = sem("half_ready")
        z_ready = sem("z_ready")
        rz_ready = sem("rz_ready")
        vn_ready = sem("vn_ready")
        pv_done = sem("pv_done")
        o_ready = sem("o_ready")
        o_half = sem("o_half")
        o_read = sem("o_read")
        block = ctx.enter_context(nc.Block())

        def pairs(eng, batch, tail=None):
            for par in range(2):
                batch(par, par)
            with eng.Fori(1, NB // 2 - 1) as it:
                for par in range(2):
                    batch(it * 2 + par, par)
            for par in range(2):
                batch(NB - 2 + par, par)
            if tail:
                tail()

        def is_first(n):
            return isinstance(n, int) and n == 0

        def is_last(n):
            return isinstance(n, int) and n == NB - 1

        def before(t, par, back):
            i = (NT * par + t - back) % (2 * NT)
            return ROWS[i % NT], SLOT[i], i % 2

        @block.sync
        def _(sp):
            def batch(n, par):
                if not (isinstance(n, int) and n < 2):
                    sp.wait_ge(v_product, (n - 1) * NT)
                sp.dma_start(ctxT[par][:, :, :], d["ctxT"][n].rearrange("(c p) s -> p c s", p=P))\
                  .then_inc(ctx_loaded[par], 16)

            pairs(sp, batch)

        @block.gpsimd
        def _(pool):
            def spread(n, par):
                for c in range(KD):
                    pool.tensor_tensor(
                        qbd[par][:, c, :, :],
                        a["qT"][:, c, bass.ds(n * L, L)].unsqueeze(1).broadcast_to([P, HC, L]),
                        sb["hmask"][:, :].unsqueeze(2).broadcast_to([P, HC, L]), ALU.mult).then_inc(qbd_ready, 1)

            def scale_values(g, par, t, back=1):
                rows, slot, i = before(t, par, back)
                pool.wait_ge(rz_ready, g + 1)
                pool.wait_ge(vb_ready, g + 1)
                if not (isinstance(g, int) and g < 2):
                    pool.wait_ge(pv_done, g - 1)
                pool.tensor_tensor(vn[0:rows, i, :].rearrange("p (h e) -> p h e", h=H),
                                   vb[0:rows, slot, :].rearrange("p (h e) -> p h e", h=H),
                                   rz[0:rows, i, :].unsqueeze(2).broadcast_to([rows, H, DH]), ALU.mult)\
                    .then_inc(vn_ready, 1)

            def batch(n, par):
                if is_first(n):
                    spread(0, 0)
                for t in range(NT):
                    g = n * NT + t
                    rows, slot, i = before(t, par, 0)
                    pool.wait_ge(exp_ready, g + 1)
                    if not (isinstance(g, int) and g < 2):
                        pool.wait_ge(z_ready, g - 1)
                    pool.tensor_tensor(half[0:rows, i, :, :], prob[0:rows, slot, :, 0:L // 2],
                                       prob[0:rows, slot, :, L // 2:L], ALU.add).then_inc(half_ready, 1)
                    if not (isinstance(g, int) and g < 1):
                        scale_values(g - 1, par, t)
                    if t == 4 and not is_last(n):
                        spread(n + 1, 1 - par)

            pairs(pool, batch, lambda: scale_values(NB * NT - 1, 0, 0))

        @block.scalar
        def _(act):
            def keys(n, par, j):
                m, (s0, w) = j % KD, KCH[j // KD]
                act.wait_ge(k_product, n * NK + j + 1)
                nc.scalar.activation(kT[par][:, m, s0:s0 + w], ps_k[:, 0:w], ACT.Identity,
                                     bias=a["bk"][:, m:m + 1]).then_inc(kT_ready, 1)

            def batch(n, par):
                if is_first(n):
                    for j in range(NK):
                        keys(0, 0, j)
                for t in range(NT):
                    g = n * NT + t
                    rows, slot, _ = before(t, par, 0)
                    if t < NK and not is_last(n):
                        keys(n + 1, 1 - par, t)
                    act.wait_ge(sub_ready, g + 1)
                    nc.scalar.activation(prob[0:rows, slot, :, :], prob[0:rows, slot, :, :], ACT.Exp)\
                        .then_inc(exp_ready, 1)

            pairs(act, batch)

        @block.tensor
        def _(pe):
            def keys(n, par, j):
                m, (s0, w) = j % KD, KCH[j // KD]
                if j == 0:
                    pe.wait_ge(ctx_loaded[par], (n - par) * 8 + 16)
                if not (is_first(n) and j == 0):
                    pe.wait_ge(kT_ready, n * NK + j)
                for k in range(KD):
                    ins = nc.tensor.matmul(ps_k[:, 0:w], a["wk"][:, k, m * P:(m + 1) * P],
                                           ctxT[par][:, k, s0:s0 + w], start=(k == 0), stop=(k == KD - 1))
                ins.then_inc(k_product, 1)

            def values_product(g, n, par, t, back):
                rows, slot, i = before(t, par, back)
                tile = (NT * par + t - back) % NT
                pe.wait_ge(vn_ready, g + 1)
                if tile == 0 and not is_first(n):
                    pe.wait_ge(o_read, n)
                for hp in range(H // 2):
                    j, c = hp % 4, hp // 4
                    ins = nc.tensor.matmul(ps_o[32 * j:32 * j + 32, c * P:(c + 1) * P],
                                           vn[0:rows, i, 2 * DH * hp:2 * DH * (hp + 1)],
                                           prob[0:rows, slot, 2 * hp:2 * hp + 2, :].rearrange("p h l -> p (h l)"),
                                           start=(tile == 0 and c == 0), stop=(tile == NT - 1),
                                           skip_group_check=True)
                ins.then_inc(pv_done, 1)

            def batch(n, par):
                if is_first(n):
                    for j in range(NK):
                        keys(0, 0, j)
                for t in range(NT):
                    g = n * NT + t
                    rows, slot, i = before(t, par, 0)
                    s0 = t * P
                    if not (isinstance(g, int) and g < 2):
                        pe.wait_ge(vb_ready, g - 1)
                    for k in range(KD):
                        ins = nc.tensor.matmul(ps_v[i][0:rows, 0:D], ctxT[par][:, k, s0:s0 + rows],
                                               a["wv"][:, k, :], start=(k == 0), stop=(k == KD - 1))
                    ins.then_inc(v_product, 1)
                    if t == 0:
                        pe.wait_ge(kT_ready, n * NK + NK)
                        pe.wait_ge(qbd_ready, n * KD + KD)
                    if not (isinstance(g, int) and g < 2):
                        pe.wait_ge(sub_ready, g - 1)
                    for c in range(KD):
                        ins = nc.tensor.matmul(ps_s[i][0:rows, c, :], kT[par][:, c, s0:s0 + rows],
                                               qbd[par][:, c, :, :].rearrange("p h l -> p (h l)"),
                                               start=True, stop=True)
                    ins.then_inc(scores_ready, 1)
                    if t < NK and not is_last(n):
                        keys(n + 1, 1 - par, t)
                    if not (isinstance(g, int) and g < LAG):
                        values_product(g - LAG, n - 1 if t < LAG else n, par, t, LAG)

            def tail():
                for k in range(LAG):
                    values_product(NB * NT - LAG + k, NB - 1, 0, k, LAG)

            pairs(pe, batch, tail)

        @block.vector
        def _(dve):
            def sum_tile(g, par, t, back=1):
                rows, slot, i = before(t, par, back)
                dve.wait_ge(half_ready, g + 1)
                if not (isinstance(g, int) and g < 2):
                    dve.wait_ge(rz_ready, g - 1)
                nc.vector.tensor_reduce(z[0:rows, i, :], half[0:rows, i, :, :], AX_X, ALU.add).then_inc(z_ready, 1)

            def invert_tile(g, par, t, back=1):
                rows, slot, i = before(t, par, back)
                dve.wait_ge(z_ready, g + 1)
                if not (isinstance(g, int) and g < 2):
                    dve.wait_ge(vn_ready, g - 1)
                nc.vector.reciprocal(rz[0:rows, i, :], z[0:rows, i, :]).then_inc(rz_ready, 1)

            def take_output(n):
                o = ps_o[:, 0:KD * P].rearrange("p (c i l) -> p c i l", c=KD, i=2)
                dve.wait_ge(pv_done, n * NT + NT)
                if not is_first(n):
                    dve.wait_ge(o_read, n)
                nc.vector.tensor_scalar(otmp[:, :, :], o[:, :, 0, :], sb["pmask"][:, 0:1], None, ALU.mult)\
                    .then_inc(o_half, 1)
                dve.wait_ge(o_half, n + 1)
                nc.vector.scalar_tensor_tensor(out=a["oT"][:, :, bass.ds(n * L, L)], in0=o[:, :, 1, :],
                                               scalar=sb["pmask"][:, 1:2], in1=otmp[:, :, :], op0=ALU.mult,
                                               op1=ALU.add).then_inc(o_read, 1)

            def batch(n, par):
                for t in range(NT):
                    g = n * NT + t
                    rows, slot, i = before(t, par, 0)
                    early = isinstance(g, int) and g < 3
                    dve.wait_ge(v_product, g + 1)
                    if not early:
                        dve.wait_ge(vn_ready, g - 2)
                    nc.vector.tensor_tensor(vb[0:rows, slot, :], ps_v[i][0:rows, 0:D], a["bv"][0:rows, :], ALU.add)\
                        .then_inc(vb_ready, 1)
                    if t == LAG and not is_first(n):
                        take_output(n - 1)
                    scores = ps_s[i][0:rows, :, :].rearrange("p c (h l) -> p (c h) l", h=HC)
                    dve.wait_ge(scores_ready, g + 1)
                    nc.vector.tensor_reduce(mx[0:rows, slot, :], scores, AX_X, ALU.max).then_inc(max_ready, 1)
                    if not (isinstance(g, int) and g < 1):
                        sum_tile(g - 1, par, t)
                    dve.wait_ge(max_ready, g + 1)
                    if not early:
                        dve.wait_ge(pv_done, g - 2)
                    nc.vector.tensor_tensor(prob[0:rows, slot, :, :], scores,
                                            mx[0:rows, slot, :].unsqueeze(2).broadcast_to([rows, H, L]),
                                            ALU.subtract).then_inc(sub_ready, 1)
                    if not (isinstance(g, int) and g < 1):
                        invert_tile(g - 1, par, t)

            def tail():
                sum_tile(NB * NT - 1, 0, 0)
                invert_tile(NB * NT - 1, 0, 0)
                take_output(NB - 1)

            pairs(dve, batch, tail)


def output_projection(nc, sb, a):
    with ExitStack() as ctx:
        ps = ctx.enter_context(nc.psum_tensor("op_ps", [P, TT, 512], F32))
        biased = ctx.enter_context(nc.semaphore("op_biased"))
        done = ctx.enter_context(nc.semaphore("op_done"))
        block = ctx.enter_context(nc.Block())

        @block.tensor
        def _(pe):
            for t in range(TT):
                for c in range(KD):
                    ins = nc.tensor.matmul(ps[:, t, 0:D], a["oT"][:, c, t * P:(t + 1) * P], a["wo"][:, c, :],
                                           start=(c == 0), stop=(c == KD - 1))
                ins.then_inc(done, 1)

        @block.vector
        def _(dve):
            for t in range(TT):
                nc.vector.tensor_tensor(sb["x"][:, t, :], sb["x"][:, t, :], a["bo"][:, :], ALU.add).then_inc(biased, 1)
            for t in range(TT):
                dve.wait_ge(done, t + 1)
                dve.wait_ge(biased, t + 1)
                nc.vector.tensor_tensor(sb["x"][:, t, :], sb["x"][:, t, :], ps[:, t, 0:D], ALU.add)


def ssm_projections(nc, d, sb, m):
    with ExitStack() as ctx:
        def sbuf(name, shape, dt=F32):
            return ctx.enter_context(nc.sbuf_tensor(name, shape, dt))

        def sem(name):
            return ctx.enter_context(nc.semaphore(name))

        wx = sbuf("wx", [P, KD, DI])
        wz = sbuf("wz", [P, KD, DI])
        wb = sbuf("wb", [P, KD, P])
        wc = sbuf("wc", [P, KD, P])
        wdt = sbuf("wdt", [P, KD, NH])
        convw = sbuf("convw", [P, XC, 4])
        convb = sbuf("convb", [P, XC])
        dtb = sbuf("dtb", [NH, 1])
        conv = sbuf("conv", [P, 2, NB, L])
        dt_v = sbuf("dt_v", [NH, NB, L])
        dt_a = sbuf("dt_a", [NH, NB, L])
        part = [sbuf(f"part{i}", [P, 2, TOK], BF16) for i in range(3)]
        left = sbuf("left", [P, 2, TOK])
        alog = sbuf("alog", [P, XC * UNITS])

        ps = [ctx.enter_context(nc.psum_tensor(f"sp_ps{i}", [P, 2, 512], F32)) for i in range(4)]
        loaded = sem("sp_loaded")
        product = sem("sp_product")
        bc_ready = sem("sp_bc_ready")
        z_ready = sem("sp_z_ready")
        made = sem("sp_made")
        a_chain = sem("sp_a_chain")
        conv_bias = sem("sp_conv_bias")
        conv_chain = sem("sp_conv_chain")
        conv_done = sem("sp_conv_done")
        x_ready = sem("sp_x_ready")
        dt_act = sem("sp_dt_act")
        dt_ready = sem("sp_dt_ready")
        hi_ready = sem("sp_hi_ready")
        left_ready = sem("sp_left_ready")
        mid_ready = sem("sp_mid_ready")
        lo_ready = sem("sp_lo_ready")
        moved = [sem("sp_moved0"), sem("sp_moved1")]
        block = ctx.enter_context(nc.Block())

        jobs = [("dt", 0)] + [("x", c) for c in range(XC)] + [("b", 0), ("c", 0)] + [("z", c) for c in range(XC)]

        def out_of(eng, j):
            kind, c = jobs[j]
            if kind == "dt":
                eng.wait_ge(dt_act, 2)
            elif kind == "x":
                eng.wait_ge(conv_done, c + 1)
            elif kind in "bc":
                eng.wait_ge(bc_ready, 1 + (kind == "c"))
            else:
                eng.wait_ge(z_ready, c + 1)

        SPLITS = XC + 1

        @block.sync
        def _(sp):
            w = d["w_inT"].rearrange("(c p) n -> p c n", p=P)
            bcol, ccol = 2 * DI, 2 * DI + NS
            for dst, src in ((wx[:, :, :], w[:, :, DI:2 * DI]), (wz[:, :, :], w[:, :, 0:DI]),
                             (wb[:, :, 0:NS], w[:, :, bcol:bcol + NS]), (wb[:, :, NS:P], w[:, :, bcol:bcol + NS]),
                             (wc[:, :, 0:NS], w[:, :, ccol:ccol + NS]), (wc[:, :, NS:P], w[:, :, ccol:ccol + NS]),
                             (wdt[:, :, :], w[:, :, ccol + NS:ccol + NS + NH]),
                             (convw[:, :, :], d["w_conv"]),
                             (convb[:, :], d["b_conv"]),
                             (dtb[:, :], d["dt_bias"].rearrange("(h a) -> h a", a=1)),
                             (alog[:, :], d["a_log"]),
                             (m["dskip"][:, :], d["dskip"]),
                             (m["nw"][:, :], d["norm_w"]),
                             (m["w_out"][:, :, :], d["w_outT"].rearrange("(c p) n -> p c n", p=P))):
                sp.dma_start(dst, src).then_inc(loaded, 16)
            sp.wait_ge(loaded, 14 * 16)
            for c in range(XC):
                sp.wait_ge(lo_ready, c + 1)
                for q in range(4):
                    for i in range(3):
                        sp.dma_start(m["xs3"][32 * i:32 * i + 32, 4 * c + q, :],
                                     part[i][32 * q:32 * q + 32, c % 2, :]).then_inc(moved[c % 2], 16)
            sp.wait_ge(lo_ready, SPLITS)
            for i in range(3):
                sp.dma_start(m["dt3"][NH * i:NH * (i + 1), :], part[i][0:NH, XC % 2, :]).then_inc(moved[XC % 2], 16)
            sp.wait_ge(moved[0], 16 * (12 * XC // 2 + 3))
            sp.wait_ge(moved[1], 16 * 12 * XC // 2)

        @block.gpsimd
        def _(pool):
            c = Chain(pool, made)
            c.link(pool.memset(m["sel"][:, :, :, :], 0.0))
            c.link(pool.memset(m["seldt"][:, :, :], 0.0))
            c.link(pool.memset(m["fold"][:, :, :], 0.0))
            c.link(pool.memset(m["ones"][:, :], 1.0))
            for i in range(3):
                v = m["sel"][32 * i:32 * i + 32, :, :, :]
                c.link(pool.affine_select(out=v, in_=v, compare_op=ALU.not_equal, fill=1.0, base=0,
                                         pattern=[[-2, 16], [-1, 2], [0, NS]], channel_multiplier=1))
            flat = m["fold"][:, :, :].rearrange("p j k -> p (j k)")
            for e in range(2):
                c.link(pool.memset(flat[NS * e:NS * (e + 1), e::34], 1.0))
            for i in range(3):
                c.link(pool.affine_select(out=m["seldt"][:, :, :], in_=m["seldt"][:, :, :], compare_op=ALU.not_equal,
                                          fill=1.0, base=-NH * i, pattern=[[-1, NH], [0, P]], channel_multiplier=1))

        @block.tensor
        def _(pe):
            pe.wait_ge(loaded, 14 * 16)
            for j, (kind, c) in enumerate(jobs):
                if j >= 4:
                    out_of(pe, j - 4)
                w = {"x": wx[:, :, c * P:(c + 1) * P], "z": wz[:, :, c * P:(c + 1) * P], "b": wb[:, :, :],
                     "c": wc[:, :, :], "dt": wdt[:, :, :]}[kind]
                rows = NH if kind == "dt" else P
                for n in range(2):
                    for k in range(KD):
                        ins = nc.tensor.matmul(ps[j % 4][0:rows, n, :], w[:, k, :],
                                               sb["xlnT"][:, k, n * 512:(n + 1) * 512],
                                               start=(k == 0), stop=(k == KD - 1))
                ins.then_inc(product, 1)

        def banks(j, rows=P):
            return ps[j % 4][0:rows, :, :].rearrange("p a s -> p (a s)")

        @block.scalar
        def _(act):
            ac = Chain(act, a_chain)
            act.wait_ge(loaded, 14 * 16)
            ac.did(nc.scalar.activation(alog[:, :], alog[:, :], ACT.Exp))
            act.wait_ge(product, 1)
            v = dt_v[:, :, :].rearrange("p b l -> p (b l)")
            e = dt_a[:, :, :].rearrange("p b l -> p (b l)")
            dc = Chain(act, dt_act)
            dc.did(nc.scalar.activation(v, banks(0, NH), ACT.Identity, bias=dtb[:, 0:1]))
            dc.link(nc.scalar.activation(e, banks(0, NH), ACT.Abs, bias=dtb[:, 0:1]))
            dc.link(nc.scalar.activation(e, e, ACT.Exp, scale=-1.0))
            dc.link(nc.scalar.activation(e, e, ACT.Ln, bias=1.0))
            for c in range(XC):
                act.wait_ge(product, c + 2)
                if c >= 2:
                    act.wait_ge(x_ready, c - 1)
                nc.scalar.activation(conv[:, c % 2, :, :].rearrange("p b l -> p (b l)"), banks(c + 1), ACT.Identity,
                                     bias=convb[:, c:c + 1], scale=convw[:, c, 3:4]).then_inc(conv_bias, 1)
                if c >= 1:
                    act.wait_ge(conv_done, c)
                    nc.scalar.activation(m["xs"][:, c - 1, :],
                                         conv[:, (c - 1) % 2, :, :].rearrange("p b l -> p (b l)"),
                                         ACT.Silu).then_inc(x_ready, 1)
            act.wait_ge(conv_done, XC)
            nc.scalar.activation(m["xs"][:, XC - 1, :], conv[:, (XC - 1) % 2, :, :].rearrange("p b l -> p (b l)"),
                                 ACT.Silu).then_inc(x_ready, 1)
            for j, (kind, c) in enumerate(jobs):
                if kind == "z":
                    act.wait_ge(product, j + 1)
                    nc.scalar.activation(m["yg"][:, c, :], banks(j), ACT.Silu).then_inc(z_ready, 1)
            for s in range(SPLITS):
                rows = NH if s == XC else P
                src = dt_a[:, :, :].rearrange("p b l -> p (b l)") if s == XC else m["xs"][:, s, :]
                if s == XC:
                    act.wait_ge(dt_ready, 2)
                else:
                    act.wait_ge(x_ready, s + 1)
                if s >= 2:
                    act.wait_ge(moved[s % 2], 16 * 12 * (s // 2))
                nc.scalar.copy(part[0][0:rows, s % 2, :], src).then_inc(hi_ready, 1)
                act.wait_ge(left_ready, s + 1)
                nc.scalar.copy(part[1][0:rows, s % 2, :], left[0:rows, s % 2, :]).then_inc(mid_ready, 1)

        @block.vector
        def _(dve):
            cc = Chain(dve, conv_chain)
            for c in range(XC):
                dve.wait_ge(conv_bias, c + 1)
                x4 = banks(c + 1).rearrange("p (b l) -> p b l", b=NB)
                for k in range(1, 4):
                    out = conv[:, c % 2, :, k:L]
                    ins = nc.vector.scalar_tensor_tensor(out=out, in0=x4[:, :, 0:L - k],
                                                         scalar=convw[:, c, 3 - k:4 - k], in1=out,
                                                         op0=ALU.mult, op1=ALU.add)
                    if k < 3:
                        cc.link(ins)
                ins.then_inc(conv_done, 1)
            dve.wait_ge(dt_act, 4)
            nc.vector.scalar_tensor_tensor(out=dt_a[:, :, :], in0=dt_v[:, :, :], scalar=0.0, in1=dt_a[:, :, :],
                                           op0=ALU.max, op1=ALU.add).then_inc(dt_ready, 1)
            dve.wait_ge(dt_ready, 1)
            nc.vector.memset(dt_a[:, :, 0:1], FAR).then_inc(dt_ready, 1)
            for j, name in ((XC + 1, "BT"), (XC + 2, "CT")):
                dve.wait_ge(product, j + 1)
                nc.vector.tensor_copy(m[name][:, :], banks(j)).then_inc(bc_ready, 1)
            dve.wait_ge(a_chain, 1)
            nc.vector.tensor_scalar(m["A"][:, :], alog[:, :], -1.0, -A_MIN, ALU.mult, ALU.min)
            for s in range(SPLITS):
                rows = NH if s == XC else P
                src = dt_a[:, :, :].rearrange("p b l -> p (b l)") if s == XC else m["xs"][:, s, :]
                dve.wait_ge(hi_ready, s + 1)
                if s >= 2:
                    dve.wait_ge(lo_ready, s - 1)
                nc.vector.tensor_tensor(left[0:rows, s % 2, :], src, part[0][0:rows, s % 2, :], ALU.subtract)\
                    .then_inc(left_ready, 1)
                dve.wait_ge(mid_ready, s + 1)
                nc.vector.tensor_tensor(part[2][0:rows, s % 2, :], left[0:rows, s % 2, :],
                                        part[1][0:rows, s % 2, :], ALU.subtract).then_inc(lo_ready, 1)


def state_space(nc, sb, m):
    with ExitStack() as ctx:
        def sbuf(name, shape, dt=F32):
            return ctx.enter_context(nc.sbuf_tensor(name, shape, dt))

        def sem(name):
            return ctx.enter_context(nc.semaphore(name))

        decay = sbuf("decay", [P, 2, TOK])
        inp = sbuf("inp", [P, 4, TOK])
        state = sbuf("state", [P, 2, TOK])
        seen = sbuf("seen", [P, 2, TOK])
        ps_dt = ctx.enter_context(nc.psum_tensor("ps_dt", [P, 2, 512], F32))
        ps_x = [ctx.enter_context(nc.psum_tensor(f"ps_x{i}", [P, 2, 512], F32)) for i in range(2)]
        ps_y = ctx.enter_context(nc.psum_tensor("ps_y", [P, 2, 512], F32))
        dt_ready = sem("m_dt_ready")
        xb_ready = sem("m_xb_ready")
        decay_ready = sem("m_decay_ready")
        inp_ready = sem("m_inp_ready")
        state_ready = sem("m_state_ready")
        seen_ready = sem("m_seen_ready")
        folded = sem("m_folded")
        y_skip = sem("m_y_skip")
        y_out = sem("m_y_out")
        block = ctx.enter_context(nc.Block())

        order = [(2 * (k // 32) + k % 2, (k % 32) // 2) for k in range(UNITS)]

        def flat(t):
            return t[:, :, :].rearrange("p a s -> p (a s)")

        def after(chunk, k):
            return chunk * UNITS + k + 1

        @block.tensor
        def _(pe):
            def fold(c, k):
                q, j = order[k]
                pe.wait_ge(seen_ready, after(c, k))
                for n in range(2):
                    ins = nc.tensor.matmul(ps_y[32 * q:32 * q + 32, n, :], m["fold"][:, j, :],
                                           seen[:, k % 2, n * 512:(n + 1) * 512],
                                           start=(j == 0), stop=(j == 15), skip_group_check=True)
                ins.then_inc(folded, 1)

            with pe.Fori(0, XC) as c:
                for k in range(UNITS):
                    q, j = order[k]
                    if k % 32 == 0:
                        if k:
                            pe.wait_ge(decay_ready, after(c, k) - 1)
                        for n in range(2):
                            ins = nc.tensor.matmul(ps_dt[:, n, :], m["seldt"][:, c * 2 + k // 32, :],
                                                   m["dt3"][:, n * 512:(n + 1) * 512], start=True, stop=True)
                        ins.then_inc(dt_ready, 1)
                    if k >= 2:
                        pe.wait_ge(inp_ready, after(c, k) - 2)
                    for n in range(2):
                        ins = nc.tensor.matmul(ps_x[k % 2][:, n, :],
                                               m["sel"][:, j, :, :].rearrange("p e s -> p (e s)"),
                                               m["xs3"][:, c * 4 + q, n * 512:(n + 1) * 512], start=True, stop=True)
                    ins.then_inc(xb_ready, 1)
                    if k >= 3:
                        fold(c, k - 3)
                for k in range(UNITS - 3, UNITS):
                    fold(c, k)
                pe.wait_ge(y_skip, c + 1)

        @block.scalar
        def _(act):
            with act.Fori(0, XC) as c:
                for k in range(UNITS):
                    q, j = order[k]
                    if k % 32 == 0:
                        act.wait_ge(dt_ready, c * 2 + k // 32 + 1)
                    if k >= 2:
                        act.wait_ge(state_ready, after(c, k) - 2)
                    nc.scalar.activation(decay[:, k % 2, :], flat(ps_dt), ACT.Exp,
                                         scale=m["A"][:, bass.ds(c * UNITS + 16 * q + j, 1)]).then_inc(decay_ready, 1)

        @block.vector
        def _(dve):
            def scan(c, k):
                dve.wait_ge(inp_ready, after(c, k))
                dve.wait_ge(decay_ready, after(c, k))
                if k >= 2:
                    dve.wait_ge(seen_ready, after(c, k) - 2)
                nc.vector.tensor_tensor_scan(state[:, k % 2, :], decay[:, k % 2, :], inp[:, k % 4, :], 0.0,
                                             ALU.mult, ALU.add).then_inc(state_ready, 1)

            with dve.Fori(0, XC) as c:
                for k in range(UNITS):
                    dve.wait_ge(xb_ready, after(c, k))
                    if k >= 4:
                        dve.wait_ge(state_ready, after(c, k) - 4)
                    nc.vector.tensor_tensor(inp[:, k % 4, :], flat(ps_x[k % 2]), m["BT"][:, :], ALU.mult)\
                        .then_inc(inp_ready, 1)
                    if k >= 1:
                        scan(c, k - 1)
                scan(c, UNITS - 1)
                dve.wait_ge(folded, after(c, UNITS - 1))
                x = m["xs"][:, bass.ds(c, 1), :].rearrange("p a s -> p (a s)")
                nc.vector.scalar_tensor_tensor(out=x, in0=x, scalar=m["dskip"][:, bass.ds(c, 1)], in1=flat(ps_y),
                                               op0=ALU.mult, op1=ALU.add).then_inc(y_skip, 1)
                dve.wait_ge(y_skip, c + 1)
                y = m["yg"][:, bass.ds(c, 1), :].rearrange("p a s -> p (a s)")
                nc.vector.tensor_tensor(y, x, y, ALU.mult).then_inc(y_out, 1)

        @block.gpsimd
        def _(pool):
            with pool.Fori(0, XC) as c:
                for k in range(UNITS):
                    pool.wait_ge(state_ready, after(c, k))
                    if k >= 2:
                        pool.wait_ge(folded, after(c, k) - 2)
                    pool.tensor_tensor(seen[:, k % 2, :], state[:, k % 2, :], m["CT"][:, :], ALU.mult)\
                        .then_inc(seen_ready, 1)


def ssm_output(nc, sb, m):
    with ExitStack() as ctx:
        ms = ctx.enter_context(nc.sbuf_tensor("so_ms", [P, TT], F32))
        rr = ctx.enter_context(nc.sbuf_tensor("so_rr", [P, TT], F32))
        ps_m = ctx.enter_context(nc.psum_tensor("so_ps_m", [P, 512], F32))
        ps = ctx.enter_context(nc.psum_tensor("so_ps", [P, 4, 512], F32))
        squared = ctx.enter_context(nc.semaphore("so_squared"))
        scaled = ctx.enter_context(nc.semaphore("so_scaled"))
        summed = ctx.enter_context(nc.semaphore("so_summed"))
        mean_ready = ctx.enter_context(nc.semaphore("so_mean_ready"))
        rr_ready = ctx.enter_context(nc.semaphore("so_rr_ready"))
        product = ctx.enter_context(nc.semaphore("so_product"))
        added = ctx.enter_context(nc.semaphore("so_added"))
        block = ctx.enter_context(nc.Block())

        @block.scalar
        def _(act):
            for c in range(XC):
                nc.scalar.activation(m["xs"][:, c, :], m["yg"][:, c, :], ACT.Square).then_inc(squared, 1)

        @block.tensor
        def _(pe):
            pe.wait_ge(squared, XC)
            for t in range(TT):
                for c in range(XC):
                    ins = nc.tensor.matmul(ps_m[:, t:t + 1], m["xs"][:, c, t * P:(t + 1) * P], m["ones"][:, :],
                                           start=(c == 0), stop=(c == XC - 1))
            ins.then_inc(summed, 1)
            pe.wait_ge(scaled, XC)
            for t in range(TT):
                if t >= 4:
                    pe.wait_ge(added, t - 3)
                for c in range(XC):
                    ins = nc.tensor.matmul(ps[:, t % 4, 0:D], m["yg"][:, c, t * P:(t + 1) * P], m["w_out"][:, c, :],
                                           start=(c == 0), stop=(c == XC - 1))
                ins.then_inc(product, 1)

        @block.vector
        def _(dve):
            for c in range(XC):
                nc.vector.tensor_scalar(m["w_out"][:, c, :], m["w_out"][:, c, :], m["nw"][:, c:c + 1], None, ALU.mult)\
                    .then_inc(scaled, 1)
            dve.wait_ge(summed, 1)
            nc.vector.tensor_scalar(ms[:, :], ps_m[:, 0:TT], 1.0 / DI, RMS_EPS, ALU.mult, ALU.add)\
                .then_inc(mean_ready, 1)
            dve.wait_ge(rr_ready, 1)
            for t in range(TT):
                dve.wait_ge(product, t + 1)
                nc.vector.scalar_tensor_tensor(out=sb["x"][:, t, :], in0=ps[:, t % 4, 0:D], scalar=rr[:, t:t + 1],
                                               in1=sb["x"][:, t, :], op0=ALU.mult, op1=ALU.add).then_inc(added, 1)

        @block.gpsimd
        def _(pool):
            pool.wait_ge(mean_ready, 1)
            pool.tensor_tensor(rr[:, :], ms[:, :], sb["minus_half"][:, :], ALU.pow).then_inc(rr_ready, 1)


def router(nc, d, sb, f):
    with ExitStack() as ctx:
        def sbuf(name, shape, dt=F32):
            return ctx.enter_context(nc.sbuf_tensor(name, shape, dt))

        def sem(name):
            return ctx.enter_context(nc.semaphore(name))

        wr = sbuf("wr", [P, KD, E])
        br = sbuf("br", [P, E])
        be2 = sbuf("be2", [E, D])
        bs2 = sbuf("bs2", [P, D])
        logit = sbuf("logit", [P, TT, E])
        top = sbuf("top", [P, TT, 8])
        at = sbuf("at", [P, TT, 8], U32)
        atf = sbuf("atf", [P, TT, 2])
        diff = sbuf("diff", [P, TT])
        ex = sbuf("ex", [P, TT])
        den = sbuf("den", [P, TT])
        w2 = sbuf("w2", [P, TT, 2])
        iot = sbuf("iot", [P, E])
        pick = sbuf("pick", [P, TT, 2, E])
        wT = sbuf("wT", [E, TOK])
        ps_l = ctx.enter_context(nc.psum_tensor("r_ps_l", [P, 512], F32))
        ps_t = ctx.enter_context(nc.psum_tensor("r_ps_t", [P, 2, 512], F32))
        ps_b = ctx.enter_context(nc.psum_tensor("r_ps_b", [P, 4, 512], F32))
        loaded, chain, product = sem("r_loaded"), sem("r_chain"), sem("r_product")
        diff_ready, ex_ready, iota_ready = sem("r_diff_ready"), sem("r_ex_ready"), sem("r_iota_ready")
        w_ready, turned, wT_ready = sem("r_w_ready"), sem("r_turned"), sem("r_wT_ready")
        bias_product, added = sem("r_bias_product"), sem("r_added")
        block = ctx.enter_context(nc.Block())

        @block.sync
        def _(sp):
            sp.dma_start(wr[:, :, :], d["wr"].rearrange("(c p) n -> p c n", p=P)).then_inc(loaded, 16)
            sp.dma_start(br[:, :], d["br"].partition_broadcast(P)).then_inc(loaded, 16)
            sp.dma_start(be2[:, :], d["be2"]).then_inc(loaded, 16)
            sp.dma_start(bs2[:, :], d["bs2"].partition_broadcast(P)).then_inc(loaded, 16)
            sp.wait_ge(loaded, 64)

        @block.gpsimd
        def _(pool):
            pool.iota(iot[:, :], pattern=[[1, E]], base=0, channel_multiplier=0,
                      allow_small_or_imprecise_dtypes=True).then_inc(iota_ready, 1)

        @block.tensor
        def _(pe):
            pe.wait_ge(loaded, 64)
            for t in range(TT):
                for k in range(KD):
                    ins = nc.tensor.matmul(ps_l[:, t * E:(t + 1) * E], sb["xlnT"][:, k, t * P:(t + 1) * P],
                                           wr[:, k, :], start=(k == 0), stop=(k == KD - 1))
            ins.then_inc(product, 1)
            pe.wait_ge(w_ready, 1)
            for t in range(TT):
                ins = nc.tensor.transpose(ps_t[0:E, t // 4, (t % 4) * P:(t % 4 + 1) * P], f["w"][:, t, :],
                                          sb["ident"][:, :])
            ins.then_inc(turned, 1)
            pe.wait_ge(wT_ready, 1)
            for t in range(TT):
                if t >= 4:
                    pe.wait_ge(added, t - 3)
                nc.tensor.matmul(ps_b[:, t % 4, 0:D], wT[:, t * P:(t + 1) * P], be2[:, :], start=True, stop=True)\
                    .then_inc(bias_product, 1)

        @block.scalar
        def _(act):
            act.wait_ge(diff_ready, 1)
            nc.scalar.activation(ex[:, :], diff[:, :], ACT.Exp).then_inc(ex_ready, 1)
            act.wait_ge(turned, 1)
            nc.scalar.copy(wT[:, :], ps_t[0:E, :, :].rearrange("p a s -> p (a s)")).then_inc(wT_ready, 1)

        @block.vector
        def _(dve):
            c = Chain(dve, chain)
            dve.wait_ge(loaded, 64)
            for t in range(TT):
                c.did(nc.vector.tensor_tensor(sb["x"][:, t, :], sb["x"][:, t, :], bs2[:, :], ALU.add))
            dve.wait_ge(product, 1)
            c.link(nc.vector.tensor_tensor(logit[:, :, :], ps_l[:, 0:TT * E].rearrange("p (t e) -> p t e", t=TT),
                                           br[:, :].unsqueeze(1).broadcast_to([P, TT, E]), ALU.add))
            c.link(nc.vector.tensor_scalar(logit[:, :, :], logit[:, :, :], 1.0 / TAU, None, ALU.mult))
            for t in range(TT):
                c.did(nc.vector.max(top[:, t, :], logit[:, t, :]))
            c.wait()
            nc.vector.tensor_tensor(diff[:, :], top[:, :, 1], top[:, :, 0], ALU.subtract).then_inc(diff_ready, 1)
            for t in range(TT):
                c.did(nc.vector.max_index(at[:, t, :], top[:, t, :], logit[:, t, :]))
            c.wait()
            c.link(nc.vector.tensor_copy(atf[:, :, :], at[:, :, 0:2]))
            dve.wait_ge(ex_ready, 1)
            c.link(nc.vector.tensor_scalar(den[:, :], ex[:, :], 1.0, None, ALU.add))
            c.link(nc.vector.reciprocal(w2[:, :, 0], den[:, :]))
            c.link(nc.vector.tensor_tensor(w2[:, :, 1], ex[:, :], w2[:, :, 0], ALU.mult))
            dve.wait_ge(iota_ready, 1)
            for t in range(TT):
                for i in range(2):
                    c.did(nc.vector.tensor_scalar(pick[:, t, i, :], iot[:, :], atf[:, t, i:i + 1], w2[:, t, i:i + 1],
                                                  ALU.is_equal, ALU.mult))
            c.wait()
            nc.vector.tensor_tensor(f["w"][:, :, :], pick[:, :, 0, :], pick[:, :, 1, :], ALU.add).then_inc(w_ready, 1)
            for t in range(TT):
                dve.wait_ge(bias_product, t + 1)
                nc.vector.tensor_tensor(sb["x"][:, t, :], sb["x"][:, t, :], ps_b[:, t % 4, 0:D], ALU.add)\
                    .then_inc(added, 1)


def experts(nc, d, sb, f):
    with ExitStack() as ctx:
        def sbuf(name, shape, dt=F32):
            return ctx.enter_context(nc.sbuf_tensor(name, shape, dt))

        def sem(name):
            return ctx.enter_context(nc.semaphore(name))

        CH, CS = HR // P, HS // P
        w1 = [sbuf(f"w1_{b}", [P, KD, 2 * HR]) for b in range(2)]
        w2 = [sbuf(f"w2_{b}", [P, CH, D]) for b in range(2)]
        b1 = [sbuf(f"b1_{b}", [P, 2 * CH]) for b in range(2)]
        gel = sbuf("gel", [P, 2, 512])
        hid = sbuf("hid", [P, 2, CH, 512])
        ps_a = [ctx.enter_context(nc.psum_tensor(f"e_ps_a{i}", [P, 512], F32)) for i in range(2)]
        ps_g = [ctx.enter_context(nc.psum_tensor(f"e_ps_g{i}", [P, 512], F32)) for i in range(2)]
        ps_y = [ctx.enter_context(nc.psum_tensor(f"e_ps_y{i}", [P, 2, 512], F32)) for i in range(2)]
        loaded = [sem("e_loaded0"), sem("e_loaded1")]
        up_done = sem("e_up_done")
        gelu_done = sem("e_gelu_done")
        hid_done = sem("e_hid_done")
        down_done = sem("e_down_done")
        added = sem("e_added")
        stored = sem("e_stored")
        block = ctx.enter_context(nc.Block())

        def chunks_before(step):
            return 2 * CS + (step - 2) * CH

        def experts_of(eng, one, tail=None):
            one(None, 0)
            one(0, 1)
            with eng.Fori(0, E // 2 - 1) as it:
                for b in range(2):
                    one(it * 2 + b + 1, b)
            one(E - 1, 0)
            if tail:
                tail()

        @block.sync
        def _(sp):
            def load(e, b):
                if e is None:
                    sp.dma_start(w1[0][:, :, 0:2 * HS], d["ws1"].rearrange("(c p) n -> p c n", p=P)).then_inc(loaded[0], 16)
                    sp.dma_start(w2[0][:, 0:CS, :], d["ws2"].rearrange("(c p) n -> p c n", p=P)).then_inc(loaded[0], 16)
                    sp.dma_start(b1[0][:, 0:2 * CS], d["bs1"]).then_inc(loaded[0], 16)
                    return
                if not (isinstance(e, int) and e == 0):
                    sp.wait_ge(down_done, e * 2)
                sp.dma_start(w1[b][:, :, :], d["we1"][e].rearrange("(c p) n -> p c n", p=P)).then_inc(loaded[b], 16)
                sp.dma_start(w2[b][:, :, :], d["we2"][e].rearrange("(c p) n -> p c n", p=P)).then_inc(loaded[b], 16)
                sp.dma_start(b1[b][:, :], d["be1"][e]).then_inc(loaded[b], 16)

            experts_of(sp, load)
            sp.wait_ge(added, 2 * (E + 1) * 4)
            sp.dma_start(d["out"].rearrange("(t p) d -> p t d", p=P), sb["x"][:, :, :]).then_inc(stored, 16)
            sp.wait_ge(stored, 16)

        def step_of(e, half):
            return half if e is None else e * 2 + 2 + half

        @block.tensor
        def _(pe):
            def down(e, half, b):
                step, ch = step_of(e, half), CS if e is None else CH
                first = half * CS if e is None else chunks_before(step)
                for i in range(ch):
                    pe.wait_ge(hid_done, first + i + 1)
                    for tt in range(4):
                        ins = nc.tensor.matmul(ps_y[half][:, tt // 2, (tt % 2) * D:(tt % 2 + 1) * D],
                                               hid[:, half, i, tt * P:(tt + 1) * P], w2[b][:, i, :],
                                               start=(i == 0 and tt % 2 == 0), stop=(i == ch - 1),
                                               skip_group_check=True)
                ins.then_inc(down_done, 1)

            def up(e, half, b):
                step, ch = step_of(e, half), CS if e is None else CH
                first = half * CS if e is None else chunks_before(step)
                for i in range(ch):
                    k2 = i % 2
                    if not (e is None and half == 0 and i < 2):
                        pe.wait_ge(hid_done, first + i - 1)
                    for ps, col in ((ps_g, (ch + i) * P), (ps_a, i * P)):
                        for k in range(KD):
                            ins = nc.tensor.matmul(ps[k2][:, :], w1[b][:, k, col:col + P],
                                                   sb["xlnT"][:, k, half * 512:(half + 1) * 512],
                                                   start=(k == 0), stop=(k == KD - 1))
                    ins.then_inc(up_done, 1)

            def one(e, b):
                pe.wait_ge(loaded[b], 48 if e is None else (e + 1 - b) * 24 + 48)
                up(e, 0, b)
                up(e, 1, b)
                for half in range(2):
                    step = step_of(e, half)
                    if e is not None:
                        pe.wait_ge(added, (step - 1) * 4)
                    down(e, half, b)

            experts_of(pe, one)

        @block.scalar
        def _(act):
            def one(e, b):
                for half in range(2):
                    step, ch = step_of(e, half), CS if e is None else CH
                    first = half * CS if e is None else chunks_before(step)
                    for i in range(ch):
                        act.wait_ge(up_done, first + i + 1)
                        if not (e is None and half == 0 and i < 2):
                            act.wait_ge(hid_done, first + i - 1)
                        nc.scalar.activation(gel[:, i % 2, :], ps_g[i % 2][:, :], ACT.Gelu,
                                             bias=b1[b][:, ch + i:ch + i + 1]).then_inc(gelu_done, 1)

            experts_of(act, one)

        @block.vector
        def _(dve):
            def one(e, b):
                for half in range(2):
                    step, ch = step_of(e, half), CS if e is None else CH
                    first = half * CS if e is None else chunks_before(step)
                    if e is not None:
                        dve.wait_ge(down_done, step - 1)
                    for i in range(ch):
                        dve.wait_ge(gelu_done, first + i + 1)
                        nc.vector.scalar_tensor_tensor(out=hid[:, half, i, :], in0=ps_a[i % 2][:, :],
                                                       scalar=b1[b][:, i:i + 1], in1=gel[:, i % 2, :],
                                                       op0=ALU.add, op1=ALU.mult).then_inc(hid_done, 1)
                for half in range(2):
                    step = step_of(e, half)
                    dve.wait_ge(down_done, step + 1)
                    for tt in range(4):
                        t = 4 * half + tt
                        if e is not None:
                            dve.wait_ge(added, (step - 2) * 4 + tt + 1)
                        y = ps_y[half][:, tt // 2, (tt % 2) * D:(tt % 2 + 1) * D]
                        if e is None:
                            ins = nc.vector.tensor_tensor(sb["x"][:, t, :], sb["x"][:, t, :], y, ALU.add)
                        else:
                            ins = nc.vector.scalar_tensor_tensor(
                                out=sb["x"][:, t, :], in0=y,
                                scalar=f["w"][:, t, bass.ds(e, 1)], in1=sb["x"][:, t, :],
                                op0=ALU.mult, op1=ALU.add)
                        ins.then_inc(added, 1)

            experts_of(dve, one)


def perceiver_layer(nc, d):
    with ExitStack() as ctx:
        def sbuf(name, shape, dt=F32, to=ctx):
            return to.enter_context(nc.sbuf_tensor(name, shape, dt))

        sb = {"x": sbuf("x_sb", [P, TT, D]), "xlnT": sbuf("xlnT", [P, KD, TOK]), "ident": sbuf("ident", [P, P]),
              "hmask": sbuf("hmask", [P, HC]), "pmask": sbuf("pmask", [P, 2]),
              "minus_half": sbuf("minus_half", [P, TT])}
        load_inputs(nc, d, sb)
        layer_norm(nc, sb, "ln1")
        with ExitStack() as part:
            a = {n: sbuf(n, s, to=part) for n, s in (
                ("qT", [P, KD, TOK]), ("oT", [P, KD, TOK]), ("wk", [P, KD, D]), ("wv", [P, KD, D]),
                ("wo", [P, KD, D]), ("bk", [P, KD]), ("bv", [P, D]), ("bo", [P, D]))}
            query_projection(nc, d, sb, a)
            attention(nc, d, sb, a)
            output_projection(nc, sb, a)
        layer_norm(nc, sb, "ln2")
        with ExitStack() as part:
            m = {n: sbuf(n, s, dt, to=part) for n, s, dt in (
                ("xs", [P, XC, TOK], F32), ("yg", [P, XC, TOK], F32), ("BT", [P, TOK], F32), ("CT", [P, TOK], F32),
                ("A", [P, XC * UNITS], F32), ("xs3", [96, 4 * XC, TOK], BF16), ("dt3", [3 * NH, TOK], BF16),
                ("sel", [96, 16, 2, NS], BF16), ("seldt", [3 * NH, NH, P], BF16), ("fold", [P, 16, 32], F32),
                ("ones", [P, 1], F32), ("dskip", [P, XC], F32), ("nw", [P, XC], F32), ("w_out", [P, XC, D], F32))}
            ssm_projections(nc, d, sb, m)
            state_space(nc, sb, m)
            ssm_output(nc, sb, m)
        layer_norm(nc, sb, "ln3")
        with ExitStack() as part:
            f = {"w": sbuf("w_tok", [P, TT, E], to=part)}
            router(nc, d, sb, f)
            experts(nc, d, sb, f)


def kernel(**inputs):
    import numpy as _np
    import concourse.bacc as _bacc
    from concourse import mybir as _mybir
    from concourse.bass_utils import run_bass_kernel_spmd as _run

    g = {k: _np.asarray(v) for k, v in inputs.items()}

    def by_feature(v):
        return v.reshape(-1, P).T

    lay = {
        "x": g["x"].reshape(TOK, D),
        "ctxT": g["ctx_1024"].transpose(0, 2, 1),
        "wq": g["L0_xattn_Wq"], "bq": by_feature(g["L0_xattn_bq"]), "wk": g["L0_xattn_Wk"], "bk": by_feature(g["L0_xattn_bk"]),
        "wv": g["L0_xattn_Wv"], "bv": g["L0_xattn_bv"], "wo": g["L0_xattn_Wo"], "bo": g["L0_xattn_bo"],
        "w_inT": g["L0_attn_W_in"].T,
        "w_conv": g["L0_attn_W_conv"].reshape(XC, P, 4).transpose(1, 0, 2),
        "b_conv": by_feature(g["L0_attn_b_conv"]),
        "a_log": g["L0_attn_A_log"].reshape(NH, HD // 2, 2, NS).transpose(2, 3, 0, 1).reshape(P, XC * UNITS),
        "dskip": by_feature(g["L0_attn_D"]), "dt_bias": g["L0_attn_dt_bias"],
        "norm_w": by_feature(g["L0_attn_norm_w"]),
        "w_outT": g["L0_attn_W_out"].T,
        "ws1": g["L0_ffn_Ws1"], "bs1": by_feature(g["L0_ffn_bs1"]), "ws2": g["L0_ffn_Ws2"], "bs2": g["L0_ffn_bs2"],
        "we1": g["L0_ffn_We1"], "be1": g["L0_ffn_be1"].reshape(E, 2 * HR // P, P).transpose(0, 2, 1),
        "we2": g["L0_ffn_We2"], "be2": g["L0_ffn_be2"], "wr": g["L0_ffn_Wr"], "br": g["L0_ffn_br"],
    }
    nc = _bacc.Bacc("TRN2", target_bir_lowering=False, num_devices=1)
    arrays, d = {}, {}
    for name, v in lay.items():
        v = _np.ascontiguousarray(v)
        arrays[f"in_{name}_dram"] = v
        d[name] = nc.dram_tensor(f"in_{name}_dram", v.shape, _mybir.dt.from_np(v.dtype), kind="ExternalInput").ap()
    d["out"] = nc.dram_tensor("out_0_dram", (TOK, D), _mybir.dt.float32, kind="ExternalOutput").ap()
    perceiver_layer(nc, d)
    r = _run(nc, [arrays], core_ids=[0])
    return r.results[0]["out_0_dram"].reshape(NB, L, D)
```

```python
from contextlib import ExitStack

import numpy as np

import concourse.bass as bass
from concourse import mybir

F32 = mybir.dt.float32
F32R = mybir.dt.float32r
BF16 = mybir.dt.bfloat16
U32 = mybir.dt.uint32
ALU = mybir.AluOpType
ACT = mybir.ActivationFunctionType
AX_X = mybir.AxisListType.X

P = 128
NB, L, D = 16, 64, 256
TOK = NB * L
TT = TOK // P
KD = D // P
LN_EPS = 1e-5

S = 1601
H, DH = 16, 16
ROWS = [P] * (S // P) + [S % P]
NT = len(ROWS)
HC = P // DH
HQ = 4
KCH = [(0, 401), (401, 400), (801, 400), (1201, 400)]
NK = KD * len(KCH)
SLOTS = 5
SLOT = [k for _ in range(4) for k in range(4)] + [k for _ in range(2) for k in range(5)]
SUM_LAG = 2
LAG = 3

DI, NS, NH, HD = 512, 64, 8, 64
XC = DI // P
UNITS = P // 2
RMS_EPS = 1e-6
FAR = 2.0 ** 100
A_MIN = 1e-25

E, HR, HS = 12, 768, 512
TAU = 1.5


class Chain:

    def __init__(self, eng, sem):
        self.eng, self.sem, self.n = eng, sem, 0

    def did(self, ins):
        self.n += 1
        ins.then_inc(self.sem, 1)
        return self.n

    def wait(self):
        self.eng.wait_ge(self.sem, self.n)

    def link(self, ins):
        self.did(ins)
        self.wait()


def load_inputs(nc, d, sb):
    with ExitStack() as ctx:
        loaded = ctx.enter_context(nc.semaphore("l_loaded"))
        made = ctx.enter_context(nc.semaphore("l_made"))
        chain = ctx.enter_context(nc.semaphore("l_chain"))
        block = ctx.enter_context(nc.Block())

        @block.sync
        def _(sp):
            sp.dma_start(sb["x"][:, :, :], d["x"].rearrange("(t p) d -> p t d", p=P)).then_inc(loaded, 16)
            sp.wait_ge(loaded, 16)

        @block.gpsimd
        def _(pool):
            c = Chain(pool, made)
            c.link(pool.memset(sb["ident"][:, :], 0.0))
            c.link(pool.memset(sb["hmask"][:, :], 1.0))
            c.link(pool.memset(sb["minus_half"][:, :], -0.5))
            c.link(pool.affine_select(out=sb["ident"][:, :], in_=sb["ident"][:, :], compare_op=ALU.not_equal,
                                     fill=1.0, base=0, pattern=[[-1, P]], channel_multiplier=1))
            c.link(pool.affine_select(out=sb["hmask"][:, :], in_=sb["hmask"][:, :], compare_op=ALU.is_ge,
                                      fill=0.0, base=0, pattern=[[-DH, HC]], channel_multiplier=1))
            c.link(pool.affine_select(out=sb["hmask"][:, :], in_=sb["hmask"][:, :], compare_op=ALU.is_ge,
                                      fill=0.0, base=DH - 1, pattern=[[DH, HC]], channel_multiplier=-1))

        @block.vector
        def _(dve):
            dve.wait_ge(made, 6)
            for i in range(HQ):
                for c in range(KD):
                    ins = nc.vector.tensor_reduce(sb["qmask"][:, c * HQ + i:c * HQ + i + 1], sb["hmask"][:, i::HQ],
                                                  AX_X, ALU.add)
            ins.then_inc(chain, 1)


def layer_norm(nc, sb, tag):
    with ExitStack() as ctx:
        stats = ctx.enter_context(nc.sbuf_tensor(f"{tag}_stats", [P, TT, 6], F32))
        mv = ctx.enter_context(nc.sbuf_tensor(f"{tag}_mv", [P, TT, 2], F32))
        vare = ctx.enter_context(nc.sbuf_tensor(f"{tag}_vare", [P, TT], F32))
        rstd = ctx.enter_context(nc.sbuf_tensor(f"{tag}_rstd", [P, TT], F32))
        xln = ctx.enter_context(nc.sbuf_tensor(f"{tag}_xln", [P, TT, D], F32))
        ps = ctx.enter_context(nc.psum_tensor(f"{tag}_ps", [P, 4, 512], F32))
        chain = ctx.enter_context(nc.semaphore(f"{tag}_chain"))
        var_ready = ctx.enter_context(nc.semaphore(f"{tag}_var_ready"))
        rstd_ready = ctx.enter_context(nc.semaphore(f"{tag}_rstd_ready"))
        xln_ready = ctx.enter_context(nc.semaphore(f"{tag}_xln_ready"))
        turned = ctx.enter_context(nc.semaphore(f"{tag}_turned"))
        copied = ctx.enter_context(nc.semaphore(f"{tag}_copied"))
        block = ctx.enter_context(nc.Block())

        @block.vector
        def _(dve):
            c = Chain(dve, chain)
            for t in range(TT):
                c.did(nc.vector.bn_stats(stats[:, t, :], sb["x"][:, t, :]))
            c.wait()
            for t in range(TT):
                c.did(nc.vector.bn_aggr(mv[:, t, :], stats[:, t, :]))
            c.wait()
            nc.vector.tensor_scalar(vare[:, :], mv[:, :, 1], LN_EPS, None, ALU.add).then_inc(var_ready, 1)
            dve.wait_ge(rstd_ready, 1)
            for t in range(TT):
                nc.vector.tensor_scalar(xln[:, t, :], sb["x"][:, t, :], mv[:, t, 0:1], rstd[:, t:t + 1],
                                        ALU.subtract, ALU.mult).then_inc(xln_ready, 1)

        @block.gpsimd
        def _(pool):
            pool.wait_ge(var_ready, 1)
            pool.tensor_tensor(rstd[:, :], vare[:, :], sb["minus_half"][:, :], ALU.pow).then_inc(rstd_ready, 1)

        @block.tensor
        def _(pe):
            for t in range(TT):
                pe.wait_ge(xln_ready, t + 1)
                if t >= 4:
                    pe.wait_ge(copied, t - 3)
                for c in range(KD):
                    ins = nc.tensor.transpose(ps[:, t % 4, c * P:(c + 1) * P], xln[:, t, c * P:(c + 1) * P],
                                              sb["ident"][:, :])
                ins.then_inc(turned, 1)

        @block.scalar
        def _(act):
            for t in range(TT):
                act.wait_ge(turned, t + 1)
                nc.scalar.copy(sb["xlnT"][:, :, t * P:(t + 1) * P],
                               ps[:, t % 4, 0:KD * P].rearrange("p (c s) -> p c s", c=KD)).then_inc(copied, 1)


def query_projection(nc, d, sb, a):
    with ExitStack() as ctx:
        wq = ctx.enter_context(nc.sbuf_tensor("wq", [P, KD, D], F32))
        bq = ctx.enter_context(nc.sbuf_tensor("bq", [P, KD], F32))
        q = ctx.enter_context(nc.sbuf_tensor("q", [P, KD, TOK], F32))
        bqs = ctx.enter_context(nc.sbuf_tensor("bqs", [P, KD], F32))
        ps = ctx.enter_context(nc.psum_tensor("q_ps", [P, 4, 512], F32))
        loaded = ctx.enter_context(nc.semaphore("q_loaded"))
        rest = ctx.enter_context(nc.semaphore("q_rest"))
        scaled = ctx.enter_context(nc.semaphore("q_scaled"))
        done = ctx.enter_context(nc.semaphore("q_done"))
        high = ctx.enter_context(nc.semaphore("q_high"))
        block = ctx.enter_context(nc.Block())

        @block.sync
        def _(sp):
            sp.dma_start(wq[:, :, :], d["wq"].rearrange("(c p) n -> p c n", p=P)).then_inc(loaded, 16)
            sp.dma_start(bq[:, :], d["bq"]).then_inc(loaded, 16)
            for name, t in (("wk", a["wk"]), ("wv", a["wv"]), ("wo", a["wo"])):
                sp.dma_start(t[:, :, :], d[name].rearrange("(c p) n -> p c n", p=P)).then_inc(rest, 16)
            sp.dma_start(a["bk"][:, :], d["bk"]).then_inc(rest, 16)
            sp.dma_start(a["bv"][:, :], d["bv"].partition_broadcast(P)).then_inc(rest, 16)
            sp.dma_start(a["bo"][:, :], d["bo"].partition_broadcast(P)).then_inc(rest, 16)
            sp.wait_ge(rest, 96)

        @block.tensor
        def _(pe):
            pe.wait_ge(loaded, 32)
            for m in range(KD):
                for n in range(2):
                    for k in range(KD):
                        ins = nc.tensor.matmul(ps[:, 2 * m + n, :], wq[:, k, m * P:(m + 1) * P],
                                               sb["xlnT"][:, k, n * 512:(n + 1) * 512],
                                               start=(k == 0), stop=(k == KD - 1))
                    ins.then_inc(done, 1)

        @block.scalar
        def _(act):
            act.wait_ge(loaded, 32)
            nc.scalar.mul(bqs[:, :], bq[:, :], DH ** -0.5).then_inc(scaled, 1)
            act.wait_ge(scaled, 1)
            for j in range(2 * KD):
                m, n = j // 2, j % 2
                act.wait_ge(done, j + 1)
                nc.scalar.activation(q[:, m, n * 512:(n + 1) * 512], ps[:, j, :], ACT.Identity,
                                     bias=bqs[:, m:m + 1], scale=DH ** -0.5).then_inc(scaled, 1)
                act.wait_ge(scaled, j + 2)
                nc.scalar.copy(a["qTh"][:, m, n * 512:(n + 1) * 512], q[:, m, n * 512:(n + 1) * 512])\
                    .then_inc(high, 1)

        @block.vector
        def _(dve):
            for j in range(2 * KD):
                m, n = j // 2, j % 2
                dve.wait_ge(high, j + 1)
                part = a["qTh"][:, m, n * 512:(n + 1) * 512].bitcast(F32)
                nc.vector.tensor_tensor(a["qTl"][:, m, n * 512:(n + 1) * 512], q[:, m, n * 512:(n + 1) * 512],
                                        part, ALU.subtract)


def attention(nc, d, sb, a):
    with ExitStack() as ctx:
        def sbuf(name, shape, dt=F32):
            return ctx.enter_context(nc.sbuf_tensor(name, shape, dt))

        def sem(name):
            return ctx.enter_context(nc.semaphore(name))

        ctxT = [sbuf(f"ctxT{b}", [P, KD, S]) for b in range(2)]
        kT = [[sbuf(f"kT{b}{part}", [P, KD, S], F32R) for part in "hl"] for b in range(2)]
        qbd = [[sbuf(f"qbd{b}{part}", [P, KD, HC, L], F32R) for part in "hl"] for b in range(2)]
        prob = sbuf("prob", [P, SLOTS, H, L])
        mx = sbuf("mx", [P, SLOTS, H])
        vb = sbuf("vb", [P, SLOTS, D])
        half = sbuf("half", [P, 2, H, L // 2])
        z = sbuf("z", [P, 2, H])
        rz = sbuf("rz", [P, 2, H])
        vn = sbuf("vn", [P, SLOTS, D])
        otmp = sbuf("otmp", [P, KD, HQ, L])

        ps_s = [ctx.enter_context(nc.psum_tensor(f"ps_s{i}", [P, 2, 512], F32)) for i in range(2)]
        ps_v = ctx.enter_context(nc.psum_tensor("ps_v", [P, 512], F32))
        ps_k = [ctx.enter_context(nc.psum_tensor(f"ps_k{i}", [P, 512], F32)) for i in range(2)]
        ps_o = ctx.enter_context(nc.psum_tensor("ps_o", [P, 512], F32))

        ctx_loaded = [sem("ctx_loaded0"), sem("ctx_loaded1")]
        qbd_ready = sem("qbd_ready")
        k_product = sem("k_product")
        kh_ready = sem("kh_ready")
        kT_ready = sem("kT_ready")
        v_product = sem("v_product")
        vb_ready = sem("vb_ready")
        scores_ready = sem("scores_ready")
        max_ready = sem("max_ready")
        sub_ready = sem("sub_ready")
        exp_ready = sem("exp_ready")
        half_ready = sem("half_ready")
        z_ready = sem("z_ready")
        rz_ready = sem("rz_ready")
        vn_ready = sem("vn_ready")
        pv_done = sem("pv_done")
        o_ready = sem("o_ready")
        o_half = sem("o_half")
        o_read = sem("o_read")
        block = ctx.enter_context(nc.Block())

        def pairs(eng, batch, tail=None):
            for par in range(2):
                batch(par, par)
            with eng.Fori(1, NB // 2 - 1) as it:
                for par in range(2):
                    batch(it * 2 + par, par)
            for par in range(2):
                batch(NB - 2 + par, par)
            if tail:
                tail()

        def is_first(n):
            return isinstance(n, int) and n == 0

        def is_last(n):
            return isinstance(n, int) and n == NB - 1

        def before(t, par, back):
            i = (NT * par + t - back) % (2 * NT)
            return ROWS[i % NT], SLOT[i], i % 2

        @block.sync
        def _(sp):
            def batch(n, par):
                if not (isinstance(n, int) and n < 2):
                    sp.wait_ge(v_product, (n - 1) * NT)
                sp.dma_start(ctxT[par][:, :, :], d["ctxT"][n].rearrange("(c p) s -> p c s", p=P))\
                  .then_inc(ctx_loaded[par], 16)

            pairs(sp, batch)

        @block.gpsimd
        def _(pool):
            def spread_part(n, par, j):
                c, part = j // 2, j % 2
                src = (a["qTh"], a["qTl"])[part]
                pool.tensor_tensor(
                    qbd[par][part][:, c, :, :],
                    src[:, c, bass.ds(n * L, L)].bitcast(F32).unsqueeze(1).broadcast_to([P, HC, L]),
                    sb["hmask"][:, :].unsqueeze(2).broadcast_to([P, HC, L]), ALU.mult).then_inc(qbd_ready, 1)

            def scale_values(g, par, t):
                rows, slot, i = before(t, par, SUM_LAG)
                pool.wait_ge(rz_ready, g + 1)
                pool.wait_ge(vb_ready, g + 1)
                if not (isinstance(g, int) and g < 4):
                    pool.wait_ge(pv_done, g - 3)
                pool.tensor_tensor(vn[0:rows, slot, :].rearrange("p (h e) -> p h e", h=H),
                                   vb[0:rows, slot, :].rearrange("p (h e) -> p h e", h=H),
                                   rz[0:rows, i, :].unsqueeze(2).broadcast_to([rows, H, DH]), ALU.mult)\
                    .then_inc(vn_ready, 1)

            def batch(n, par):
                if is_first(n):
                    for j in range(2 * KD):
                        spread_part(0, 0, j)
                for t in range(NT):
                    g = n * NT + t
                    rows, slot, i = before(t, par, 0)
                    if not (isinstance(g, int) and g < SUM_LAG):
                        scale_values(g - SUM_LAG, par, t)
                    pool.wait_ge(exp_ready, g + 1)
                    if not (isinstance(g, int) and g < 2):
                        pool.wait_ge(z_ready, g - 1)
                    pool.tensor_tensor(half[0:rows, i, :, :], prob[0:rows, slot, :, 0:L // 2],
                                       prob[0:rows, slot, :, L // 2:L], ALU.add).then_inc(half_ready, 1)
                    if t in (5, 7, 9, 11) and not is_last(n):
                        spread_part(n + 1, 1 - par, (t - 5) // 2)

            def tail():
                for k in range(SUM_LAG):
                    scale_values(NB * NT - SUM_LAG + k, 0, k)

            pairs(pool, batch, tail)

        @block.scalar
        def _(act):
            def keys(n, par, j):
                m, (s0, w) = j % KD, KCH[j // KD]
                act.wait_ge(k_product, n * NK + j + 1)
                nc.scalar.activation(kT[par][0][:, m, s0:s0 + w], ps_k[j % 2][:, 0:w], ACT.Identity,
                                     bias=a["bk"][:, m:m + 1]).then_inc(kh_ready, 1)

            def batch(n, par):
                if is_first(n):
                    for j in range(NK):
                        keys(0, 0, j)
                for t in range(NT):
                    g = n * NT + t
                    rows, slot, _ = before(t, par, 0)
                    if t < NK and not is_last(n):
                        keys(n + 1, 1 - par, t)
                    act.wait_ge(sub_ready, g + 1)
                    nc.scalar.activation(prob[0:rows, slot, :, :], prob[0:rows, slot, :, :], ACT.Exp)\
                        .then_inc(exp_ready, 1)

            pairs(act, batch)

        @block.tensor
        def _(pe):
            def keys(n, par, j):
                m, (s0, w) = j % KD, KCH[j // KD]
                if j == 0:
                    pe.wait_ge(ctx_loaded[par], (n - par) * 8 + 16)
                if not (is_first(n) and j < 2):
                    pe.wait_ge(kT_ready, n * NK + j - 1)
                for k in range(KD):
                    ins = nc.tensor.matmul(ps_k[j % 2][:, 0:w], a["wk"][:, k, m * P:(m + 1) * P],
                                           ctxT[par][:, k, s0:s0 + w], start=(k == 0), stop=(k == KD - 1))
                ins.then_inc(k_product, 1)

            def values_product(g, n, par, t, back):
                rows, slot, i = before(t, par, back)
                tile = (NT * par + t - back) % NT
                pe.wait_ge(vn_ready, g + 1)
                if tile == 0 and not is_first(n):
                    pe.wait_ge(o_read, n)
                for q in range(H // HQ):
                    j, c = q % 2, q // 2
                    ins = nc.tensor.matmul(ps_o[64 * j:64 * j + 64, c * HQ * L:(c + 1) * HQ * L],
                                           vn[0:rows, slot, HQ * DH * q:HQ * DH * (q + 1)],
                                           prob[0:rows, slot, HQ * q:HQ * (q + 1), :].rearrange("p h l -> p (h l)"),
                                           start=(tile == 0 and c == 0), stop=(tile == NT - 1),
                                           skip_group_check=True)
                ins.then_inc(pv_done, 1)

            def batch(n, par):
                if is_first(n):
                    for j in range(NK):
                        keys(0, 0, j)
                for t in range(NT):
                    g = n * NT + t
                    rows, slot, i = before(t, par, 0)
                    s0 = t * P
                    if not (isinstance(g, int) and g < 1):
                        pe.wait_ge(vb_ready, g)
                    for k in range(KD):
                        ins = nc.tensor.matmul(ps_v[0:rows, 0:D], ctxT[par][:, k, s0:s0 + rows],
                                               a["wv"][:, k, :], start=(k == 0), stop=(k == KD - 1))
                    ins.then_inc(v_product, 1)
                    if t == 0:
                        pe.wait_ge(kT_ready, n * NK + NK)
                        pe.wait_ge(qbd_ready, (n + 1) * 2 * KD)
                    if not (isinstance(g, int) and g < 2):
                        pe.wait_ge(sub_ready, g - 1)
                    for c in range(KD):
                        for kp, qp in ((0, 0), (0, 1), (1, 0)):
                            ins = nc.tensor.matmul(ps_s[i][0:rows, c, :], kT[par][kp][:, c, s0:s0 + rows],
                                                   qbd[par][qp][:, c, :, :].rearrange("p h l -> p (h l)"),
                                                   start=(kp == qp), stop=(kp == 1))
                    ins.then_inc(scores_ready, 1)
                    if t < NK and not is_last(n):
                        keys(n + 1, 1 - par, t)
                    if not (isinstance(g, int) and g < LAG):
                        values_product(g - LAG, n - 1 if t < LAG else n, par, t, LAG)

            def tail():
                for k in range(LAG):
                    values_product(NB * NT - LAG + k, NB - 1, 0, k, LAG)

            pairs(pe, batch, tail)

        @block.vector
        def _(dve):
            def sum_tile(g, par, t):
                rows, slot, i = before(t, par, SUM_LAG)
                dve.wait_ge(half_ready, g + 1)
                if not (isinstance(g, int) and g < 2):
                    dve.wait_ge(rz_ready, g - 1)
                nc.vector.tensor_reduce(z[0:rows, i, :], half[0:rows, i, :, :], AX_X, ALU.add).then_inc(z_ready, 1)

            def invert_tile(g, par, t):
                rows, slot, i = before(t, par, SUM_LAG)
                dve.wait_ge(z_ready, g + 1)
                if not (isinstance(g, int) and g < 2):
                    dve.wait_ge(vn_ready, g - 1)
                nc.vector.reciprocal(rz[0:rows, i, :], z[0:rows, i, :]).then_inc(rz_ready, 1)

            def take_output(n):
                o = ps_o[:, :].rearrange("p (c i l) -> p (c i) l", c=KD, i=HQ)
                dve.wait_ge(pv_done, n * NT + NT)
                if not is_first(n):
                    dve.wait_ge(o_read, n)
                nc.vector.tensor_tensor(
                    otmp[:, :, :, :].rearrange("p c i l -> p (c i) l"), o,
                    sb["qmask"][:, :].unsqueeze(2).broadcast_to([P, KD * HQ, L]), ALU.mult).then_inc(o_half, 1)
                dve.wait_ge(o_half, n + 1)
                nc.vector.tensor_reduce(a["oT"][:, :, bass.ds(n * L, L)],
                                        otmp[:, :, :, :].rearrange("p c i l -> p c l i"), AX_X, ALU.add)\
                    .then_inc(o_read, 1)

            def low_keys(n, par, j):
                m, (s0, w) = j % KD, KCH[j // KD]
                dve.wait_ge(kh_ready, n * NK + j + 1)
                nc.vector.scalar_tensor_tensor(out=kT[par][1][:, m, s0:s0 + w], in0=ps_k[j % 2][:, 0:w],
                                               scalar=a["bk"][:, m:m + 1],
                                               in1=kT[par][0][:, m, s0:s0 + w].bitcast(F32),
                                               op0=ALU.add, op1=ALU.subtract).then_inc(kT_ready, 1)

            def batch(n, par):
                if is_first(n):
                    for j in range(NK):
                        low_keys(0, 0, j)
                for t in range(NT):
                    g = n * NT + t
                    rows, slot, i = before(t, par, 0)
                    early = isinstance(g, int) and g < 4
                    summed = not (isinstance(g, int) and g < SUM_LAG)
                    if summed:
                        sum_tile(g - SUM_LAG, par, t)
                    dve.wait_ge(v_product, g + 1)
                    if not early:
                        dve.wait_ge(vn_ready, g - 3)
                    nc.vector.tensor_tensor(vb[0:rows, slot, :], ps_v[0:rows, 0:D], a["bv"][0:rows, :], ALU.add)\
                        .then_inc(vb_ready, 1)
                    if summed:
                        invert_tile(g - SUM_LAG, par, t)
                    scores = ps_s[i][0:rows, :, :].rearrange("p c (h l) -> p (c h) l", h=HC)
                    dve.wait_ge(scores_ready, g + 1)
                    nc.vector.tensor_reduce(mx[0:rows, slot, :], scores, AX_X, ALU.max).then_inc(max_ready, 1)
                    if t < NK and not is_last(n):
                        low_keys(n + 1, 1 - par, t)
                    dve.wait_ge(max_ready, g + 1)
                    if not early:
                        dve.wait_ge(pv_done, g - 3)
                    nc.vector.tensor_tensor(prob[0:rows, slot, :, :], scores,
                                            mx[0:rows, slot, :].unsqueeze(2).broadcast_to([rows, H, L]),
                                            ALU.subtract).then_inc(sub_ready, 1)
                    if t == LAG - 1 and not is_first(n):
                        take_output(n - 1)

            def tail():
                for k in range(SUM_LAG):
                    g = NB * NT - SUM_LAG + k
                    sum_tile(g, 0, k)
                    invert_tile(g, 0, k)
                take_output(NB - 1)

            pairs(dve, batch, tail)


def output_projection(nc, sb, a):
    with ExitStack() as ctx:
        ps = ctx.enter_context(nc.psum_tensor("op_ps", [P, TT, 512], F32))
        biased = ctx.enter_context(nc.semaphore("op_biased"))
        done = ctx.enter_context(nc.semaphore("op_done"))
        block = ctx.enter_context(nc.Block())

        @block.tensor
        def _(pe):
            for t in range(TT):
                for c in range(KD):
                    ins = nc.tensor.matmul(ps[:, t, 0:D], a["oT"][:, c, t * P:(t + 1) * P], a["wo"][:, c, :],
                                           start=(c == 0), stop=(c == KD - 1))
                ins.then_inc(done, 1)

        @block.vector
        def _(dve):
            for t in range(TT):
                nc.vector.tensor_tensor(sb["x"][:, t, :], sb["x"][:, t, :], a["bo"][:, :], ALU.add).then_inc(biased, 1)
            for t in range(TT):
                dve.wait_ge(done, t + 1)
                dve.wait_ge(biased, t + 1)
                nc.vector.tensor_tensor(sb["x"][:, t, :], sb["x"][:, t, :], ps[:, t, 0:D], ALU.add)


def ssm_projections(nc, d, sb, m):
    with ExitStack() as ctx:
        def sbuf(name, shape, dt=F32):
            return ctx.enter_context(nc.sbuf_tensor(name, shape, dt))

        def sem(name):
            return ctx.enter_context(nc.semaphore(name))

        wx = sbuf("wx", [P, KD, DI])
        wz = sbuf("wz", [P, KD, DI])
        wb = sbuf("wb", [P, KD, P])
        wc = sbuf("wc", [P, KD, P])
        wdt = sbuf("wdt", [P, KD, NH])
        convw = sbuf("convw", [P, XC, 4])
        convb = sbuf("convb", [P, XC])
        dtb = sbuf("dtb", [NH, 1])
        conv = sbuf("conv", [P, 2, NB, L])
        dt_v = sbuf("dt_v", [NH, NB, L])
        dt_a = sbuf("dt_a", [NH, NB, L])
        part = [sbuf(f"part{i}", [P, 2, TOK], BF16) for i in range(3)]
        left = sbuf("left", [P, 2, TOK])
        alog = sbuf("alog", [P, XC * UNITS])

        ps = [ctx.enter_context(nc.psum_tensor(f"sp_ps{i}", [P, 2, 512], F32)) for i in range(4)]
        loaded = sem("sp_loaded")
        product = sem("sp_product")
        bc_ready = sem("sp_bc_ready")
        z_ready = sem("sp_z_ready")
        made = sem("sp_made")
        a_chain = sem("sp_a_chain")
        conv_bias = sem("sp_conv_bias")
        conv_chain = sem("sp_conv_chain")
        conv_done = sem("sp_conv_done")
        x_ready = sem("sp_x_ready")
        dt_act = sem("sp_dt_act")
        dt_ready = sem("sp_dt_ready")
        hi_ready = sem("sp_hi_ready")
        left_ready = sem("sp_left_ready")
        mid_ready = sem("sp_mid_ready")
        lo_ready = sem("sp_lo_ready")
        moved = [sem("sp_moved0"), sem("sp_moved1")]
        block = ctx.enter_context(nc.Block())

        jobs = [("dt", 0)] + [("x", c) for c in range(XC)] + [("b", 0), ("c", 0)] + [("z", c) for c in range(XC)]

        def out_of(eng, j):
            kind, c = jobs[j]
            if kind == "dt":
                eng.wait_ge(dt_act, 2)
            elif kind == "x":
                eng.wait_ge(conv_done, c + 1)
            elif kind in "bc":
                eng.wait_ge(bc_ready, 1 + (kind == "c"))
            else:
                eng.wait_ge(z_ready, c + 1)

        SPLITS = XC + 1

        @block.sync
        def _(sp):
            w = d["w_inT"].rearrange("(c p) n -> p c n", p=P)
            bcol, ccol = 2 * DI, 2 * DI + NS
            for dst, src in ((wx[:, :, :], w[:, :, DI:2 * DI]), (wz[:, :, :], w[:, :, 0:DI]),
                             (wb[:, :, 0:NS], w[:, :, bcol:bcol + NS]), (wb[:, :, NS:P], w[:, :, bcol:bcol + NS]),
                             (wc[:, :, 0:NS], w[:, :, ccol:ccol + NS]), (wc[:, :, NS:P], w[:, :, ccol:ccol + NS]),
                             (wdt[:, :, :], w[:, :, ccol + NS:ccol + NS + NH]),
                             (convw[:, :, :], d["w_conv"]),
                             (convb[:, :], d["b_conv"]),
                             (dtb[:, :], d["dt_bias"].rearrange("(h a) -> h a", a=1)),
                             (alog[:, :], d["a_log"]),
                             (m["dskip"][:, :], d["dskip"]),
                             (m["nw"][:, :], d["norm_w"]),
                             (m["w_out"][:, :, :], d["w_outT"].rearrange("(c p) n -> p c n", p=P))):
                sp.dma_start(dst, src).then_inc(loaded, 16)
            sp.wait_ge(loaded, 14 * 16)
            for c in range(XC):
                sp.wait_ge(lo_ready, c + 1)
                for q in range(4):
                    for i in range(3):
                        sp.dma_start(m["xs3"][32 * i:32 * i + 32, 4 * c + q, :],
                                     part[i][32 * q:32 * q + 32, c % 2, :]).then_inc(moved[c % 2], 16)
            sp.wait_ge(lo_ready, SPLITS)
            for i in range(3):
                sp.dma_start(m["dt3"][NH * i:NH * (i + 1), :], part[i][0:NH, XC % 2, :]).then_inc(moved[XC % 2], 16)
            sp.wait_ge(moved[0], 16 * (12 * XC // 2 + 3))
            sp.wait_ge(moved[1], 16 * 12 * XC // 2)

        @block.gpsimd
        def _(pool):
            c = Chain(pool, made)
            c.link(pool.memset(m["sel"][:, :, :, :], 0.0))
            c.link(pool.memset(m["seldt"][:, :, :], 0.0))
            c.link(pool.memset(m["fold"][:, :, :], 0.0))
            c.link(pool.memset(m["ones"][:, :], 1.0))
            for i in range(3):
                v = m["sel"][32 * i:32 * i + 32, :, :, :]
                c.link(pool.affine_select(out=v, in_=v, compare_op=ALU.not_equal, fill=1.0, base=0,
                                         pattern=[[-2, 16], [-1, 2], [0, NS]], channel_multiplier=1))
            flat = m["fold"][:, :, :].rearrange("p j k -> p (j k)")
            for e in range(2):
                c.link(pool.memset(flat[NS * e:NS * (e + 1), e::34], 1.0))
            for i in range(3):
                c.link(pool.affine_select(out=m["seldt"][:, :, :], in_=m["seldt"][:, :, :], compare_op=ALU.not_equal,
                                          fill=1.0, base=-NH * i, pattern=[[-1, NH], [0, P]], channel_multiplier=1))

        @block.tensor
        def _(pe):
            pe.wait_ge(loaded, 14 * 16)
            for j, (kind, c) in enumerate(jobs):
                if j >= 4:
                    out_of(pe, j - 4)
                w = {"x": wx[:, :, c * P:(c + 1) * P], "z": wz[:, :, c * P:(c + 1) * P], "b": wb[:, :, :],
                     "c": wc[:, :, :], "dt": wdt[:, :, :]}[kind]
                rows = NH if kind == "dt" else P
                for n in range(2):
                    for k in range(KD):
                        ins = nc.tensor.matmul(ps[j % 4][0:rows, n, :], w[:, k, :],
                                               sb["xlnT"][:, k, n * 512:(n + 1) * 512],
                                               start=(k == 0), stop=(k == KD - 1))
                ins.then_inc(product, 1)

        def banks(j, rows=P):
            return ps[j % 4][0:rows, :, :].rearrange("p a s -> p (a s)")

        @block.scalar
        def _(act):
            ac = Chain(act, a_chain)
            act.wait_ge(loaded, 14 * 16)
            ac.did(nc.scalar.activation(alog[:, :], alog[:, :], ACT.Exp))
            act.wait_ge(product, 1)
            v = dt_v[:, :, :].rearrange("p b l -> p (b l)")
            e = dt_a[:, :, :].rearrange("p b l -> p (b l)")
            dc = Chain(act, dt_act)
            dc.did(nc.scalar.activation(v, banks(0, NH), ACT.Identity, bias=dtb[:, 0:1]))
            dc.link(nc.scalar.activation(e, banks(0, NH), ACT.Abs, bias=dtb[:, 0:1]))
            dc.link(nc.scalar.activation(e, e, ACT.Exp, scale=-1.0))
            dc.link(nc.scalar.activation(e, e, ACT.Ln, bias=1.0))
            for c in range(XC):
                act.wait_ge(product, c + 2)
                if c >= 2:
                    act.wait_ge(x_ready, c - 1)
                nc.scalar.activation(conv[:, c % 2, :, :].rearrange("p b l -> p (b l)"), banks(c + 1), ACT.Identity,
                                     bias=convb[:, c:c + 1], scale=convw[:, c, 3:4]).then_inc(conv_bias, 1)
                if c >= 1:
                    act.wait_ge(conv_done, c)
                    nc.scalar.activation(m["xs"][:, c - 1, :],
                                         conv[:, (c - 1) % 2, :, :].rearrange("p b l -> p (b l)"),
                                         ACT.Silu).then_inc(x_ready, 1)
            act.wait_ge(conv_done, XC)
            nc.scalar.activation(m["xs"][:, XC - 1, :], conv[:, (XC - 1) % 2, :, :].rearrange("p b l -> p (b l)"),
                                 ACT.Silu).then_inc(x_ready, 1)
            for j, (kind, c) in enumerate(jobs):
                if kind == "z":
                    act.wait_ge(product, j + 1)
                    nc.scalar.activation(m["yg"][:, c, :], banks(j), ACT.Silu).then_inc(z_ready, 1)
            for s in range(SPLITS):
                rows = NH if s == XC else P
                src = dt_a[:, :, :].rearrange("p b l -> p (b l)") if s == XC else m["xs"][:, s, :]
                if s == XC:
                    act.wait_ge(dt_ready, 2)
                else:
                    act.wait_ge(x_ready, s + 1)
                if s >= 2:
                    act.wait_ge(moved[s % 2], 16 * 12 * (s // 2))
                nc.scalar.copy(part[0][0:rows, s % 2, :], src).then_inc(hi_ready, 1)
                act.wait_ge(left_ready, s + 1)
                nc.scalar.copy(part[1][0:rows, s % 2, :], left[0:rows, s % 2, :]).then_inc(mid_ready, 1)

        @block.vector
        def _(dve):
            cc = Chain(dve, conv_chain)
            for c in range(XC):
                dve.wait_ge(conv_bias, c + 1)
                x4 = banks(c + 1).rearrange("p (b l) -> p b l", b=NB)
                for k in range(1, 4):
                    out = conv[:, c % 2, :, k:L]
                    ins = nc.vector.scalar_tensor_tensor(out=out, in0=x4[:, :, 0:L - k],
                                                         scalar=convw[:, c, 3 - k:4 - k], in1=out,
                                                         op0=ALU.mult, op1=ALU.add)
                    if k < 3:
                        cc.link(ins)
                ins.then_inc(conv_done, 1)
            dve.wait_ge(dt_act, 4)
            nc.vector.scalar_tensor_tensor(out=dt_a[:, :, :], in0=dt_v[:, :, :], scalar=0.0, in1=dt_a[:, :, :],
                                           op0=ALU.max, op1=ALU.add).then_inc(dt_ready, 1)
            dve.wait_ge(dt_ready, 1)
            nc.vector.memset(dt_a[:, :, 0:1], FAR).then_inc(dt_ready, 1)
            for j, name in ((XC + 1, "BT"), (XC + 2, "CT")):
                dve.wait_ge(product, j + 1)
                nc.vector.tensor_copy(m[name][:, :], banks(j)).then_inc(bc_ready, 1)
            dve.wait_ge(a_chain, 1)
            nc.vector.tensor_scalar(m["A"][:, :], alog[:, :], -1.0, -A_MIN, ALU.mult, ALU.min)
            for s in range(SPLITS):
                rows = NH if s == XC else P
                src = dt_a[:, :, :].rearrange("p b l -> p (b l)") if s == XC else m["xs"][:, s, :]
                dve.wait_ge(hi_ready, s + 1)
                if s >= 2:
                    dve.wait_ge(lo_ready, s - 1)
                nc.vector.tensor_tensor(left[0:rows, s % 2, :], src, part[0][0:rows, s % 2, :], ALU.subtract)\
                    .then_inc(left_ready, 1)
                dve.wait_ge(mid_ready, s + 1)
                nc.vector.tensor_tensor(part[2][0:rows, s % 2, :], left[0:rows, s % 2, :],
                                        part[1][0:rows, s % 2, :], ALU.subtract).then_inc(lo_ready, 1)


def state_space(nc, sb, m):
    with ExitStack() as ctx:
        def sbuf(name, shape, dt=F32):
            return ctx.enter_context(nc.sbuf_tensor(name, shape, dt))

        def sem(name):
            return ctx.enter_context(nc.semaphore(name))

        DECAYS, INPS, STATES, SEEN = 2, 4, 4, 4
        decay = sbuf("decay", [P, DECAYS, TOK])
        inp = sbuf("inp", [P, INPS, TOK])
        state = sbuf("state", [P, STATES, TOK])
        seen = sbuf("seen", [P, SEEN, TOK])
        ps_dt = ctx.enter_context(nc.psum_tensor("ps_dt", [P, 2, 512], F32))
        ps_x = [ctx.enter_context(nc.psum_tensor(f"ps_x{i}", [P, 2, 512], F32)) for i in range(2)]
        ps_y = ctx.enter_context(nc.psum_tensor("ps_y", [P, 2, 512], F32))
        dt_ready = sem("m_dt_ready")
        xb_ready = sem("m_xb_ready")
        decay_ready = sem("m_decay_ready")
        inp_ready = sem("m_inp_ready")
        state_ready = sem("m_state_ready")
        seen_ready = sem("m_seen_ready")
        folded = sem("m_folded")
        y_skip = sem("m_y_skip")
        y_out = sem("m_y_out")
        block = ctx.enter_context(nc.Block())

        order = [(2 * (k // 32) + k % 2, (k % 32) // 2) for k in range(UNITS)]
        FOLD_LAG = 4

        def flat(t):
            return t[:, :, :].rearrange("p a s -> p (a s)")

        def chunks(eng, chunk, tail=None):
            chunk(0)
            with eng.Fori(1, XC) as c:
                chunk(c)
            if tail:
                tail()

        def has(c, k, back):
            return k >= back or not isinstance(c, int)

        @block.tensor
        def _(pe):
            def fold(c, k, g):
                q, j = order[k]
                pe.wait_ge(seen_ready, g + 1)
                if k == 0 and not isinstance(c, int):
                    pe.wait_ge(y_skip, c)
                for n in range(2):
                    ins = nc.tensor.matmul(ps_y[32 * q:32 * q + 32, n, :], m["fold"][:, j, :],
                                           seen[:, k % SEEN, n * 512:(n + 1) * 512],
                                           start=(j == 0), stop=(j == 15), skip_group_check=True)
                ins.then_inc(folded, 1)

            def chunk(c):
                for k in range(UNITS):
                    q, j = order[k]
                    g = c * UNITS + k
                    if k % 32 == 0:
                        if has(c, k, 1):
                            pe.wait_ge(decay_ready, g)
                        for n in range(2):
                            ins = nc.tensor.matmul(ps_dt[:, n, :], m["seldt"][:, c * 2 + k // 32, :],
                                                   m["dt3"][:, n * 512:(n + 1) * 512], start=True, stop=True)
                        ins.then_inc(dt_ready, 1)
                    if has(c, k, 2):
                        pe.wait_ge(inp_ready, g - 1)
                    for n in range(2):
                        ins = nc.tensor.matmul(ps_x[k % 2][:, n, :],
                                               m["sel"][:, j, :, :].rearrange("p e s -> p (e s)"),
                                               m["xs3"][:, c * 4 + q, n * 512:(n + 1) * 512], start=True, stop=True)
                    ins.then_inc(xb_ready, 1)
                    if has(c, k, FOLD_LAG):
                        fold(c, (k - FOLD_LAG) % UNITS, g - FOLD_LAG)

            def tail():
                for k in range(UNITS - FOLD_LAG, UNITS):
                    fold(XC - 1, k, (XC - 1) * UNITS + k)

            chunks(pe, chunk, tail)

        @block.scalar
        def _(act):
            def chunk(c):
                for k in range(UNITS):
                    q, j = order[k]
                    g = c * UNITS + k
                    if k % 32 == 0:
                        act.wait_ge(dt_ready, c * 2 + k // 32 + 1)
                    if has(c, k, DECAYS):
                        act.wait_ge(state_ready, g - DECAYS + 1)
                    nc.scalar.activation(decay[:, k % DECAYS, :], flat(ps_dt), ACT.Exp,
                                         scale=m["A"][:, bass.ds(c * UNITS + 16 * q + j, 1)]).then_inc(decay_ready, 1)

            chunks(act, chunk)

        @block.vector
        def _(dve):
            def scan(c, k, g):
                dve.wait_ge(inp_ready, g + 1)
                dve.wait_ge(decay_ready, g + 1)
                if k >= STATES or not isinstance(c, int):
                    dve.wait_ge(seen_ready, g - STATES + 1)
                nc.vector.tensor_tensor_scan(state[:, k % STATES, :], decay[:, k % DECAYS, :], inp[:, k % INPS, :],
                                             0.0, ALU.mult, ALU.add).then_inc(state_ready, 1)

            def take_output(c):
                dve.wait_ge(folded, c * UNITS + UNITS)
                x = m["xs"][:, bass.ds(c, 1), :].rearrange("p a s -> p (a s)")
                nc.vector.scalar_tensor_tensor(out=x, in0=x, scalar=m["dskip"][:, bass.ds(c, 1)], in1=flat(ps_y),
                                               op0=ALU.mult, op1=ALU.add).then_inc(y_skip, 1)

            def gate_output(c):
                dve.wait_ge(y_skip, c + 1)
                x = m["xs"][:, bass.ds(c, 1), :].rearrange("p a s -> p (a s)")
                y = m["yg"][:, bass.ds(c, 1), :].rearrange("p a s -> p (a s)")
                nc.vector.tensor_tensor(y, x, y, ALU.mult).then_inc(y_out, 1)

            def chunk(c):
                for k in range(UNITS):
                    g = c * UNITS + k
                    dve.wait_ge(xb_ready, g + 1)
                    if has(c, k, INPS):
                        dve.wait_ge(state_ready, g - INPS + 1)
                    nc.vector.tensor_tensor(inp[:, k % INPS, :], flat(ps_x[k % 2]), m["BT"][:, :], ALU.mult)\
                        .then_inc(inp_ready, 1)
                    if has(c, k, 1):
                        scan(c, (k - 1) % UNITS, g - 1)
                    if not isinstance(c, int):
                        if k == FOLD_LAG - 1:
                            take_output(c - 1)
                        if k == FOLD_LAG:
                            gate_output(c - 1)

            def tail():
                scan(XC - 1, UNITS - 1, XC * UNITS - 1)
                take_output(XC - 1)
                gate_output(XC - 1)

            chunks(dve, chunk, tail)

        @block.gpsimd
        def _(pool):
            def chunk(c):
                for k in range(UNITS):
                    g = c * UNITS + k
                    pool.wait_ge(state_ready, g + 1)
                    if has(c, k, SEEN):
                        pool.wait_ge(folded, g - SEEN + 1)
                    pool.tensor_tensor(seen[:, k % SEEN, :], state[:, k % STATES, :], m["CT"][:, :], ALU.mult)\
                        .then_inc(seen_ready, 1)

            chunks(pool, chunk)


def ssm_output(nc, sb, m):
    with ExitStack() as ctx:
        ms = ctx.enter_context(nc.sbuf_tensor("so_ms", [P, TT], F32))
        rr = ctx.enter_context(nc.sbuf_tensor("so_rr", [P, TT], F32))
        ps_m = ctx.enter_context(nc.psum_tensor("so_ps_m", [P, 512], F32))
        ps = ctx.enter_context(nc.psum_tensor("so_ps", [P, 4, 512], F32))
        squared = ctx.enter_context(nc.semaphore("so_squared"))
        scaled = ctx.enter_context(nc.semaphore("so_scaled"))
        summed = ctx.enter_context(nc.semaphore("so_summed"))
        mean_ready = ctx.enter_context(nc.semaphore("so_mean_ready"))
        rr_ready = ctx.enter_context(nc.semaphore("so_rr_ready"))
        product = ctx.enter_context(nc.semaphore("so_product"))
        added = ctx.enter_context(nc.semaphore("so_added"))
        block = ctx.enter_context(nc.Block())

        @block.scalar
        def _(act):
            for c in range(XC):
                nc.scalar.activation(m["xs"][:, c, :], m["yg"][:, c, :], ACT.Square).then_inc(squared, 1)

        @block.tensor
        def _(pe):
            pe.wait_ge(squared, XC)
            for t in range(TT):
                for c in range(XC):
                    ins = nc.tensor.matmul(ps_m[:, t:t + 1], m["xs"][:, c, t * P:(t + 1) * P], m["ones"][:, :],
                                           start=(c == 0), stop=(c == XC - 1))
            ins.then_inc(summed, 1)
            pe.wait_ge(scaled, XC)
            for t in range(TT):
                if t >= 4:
                    pe.wait_ge(added, t - 3)
                for c in range(XC):
                    ins = nc.tensor.matmul(ps[:, t % 4, 0:D], m["yg"][:, c, t * P:(t + 1) * P], m["w_out"][:, c, :],
                                           start=(c == 0), stop=(c == XC - 1))
                ins.then_inc(product, 1)

        @block.vector
        def _(dve):
            for c in range(XC):
                nc.vector.tensor_scalar(m["w_out"][:, c, :], m["w_out"][:, c, :], m["nw"][:, c:c + 1], None, ALU.mult)\
                    .then_inc(scaled, 1)
            dve.wait_ge(summed, 1)
            nc.vector.tensor_scalar(ms[:, :], ps_m[:, 0:TT], 1.0 / DI, RMS_EPS, ALU.mult, ALU.add)\
                .then_inc(mean_ready, 1)
            dve.wait_ge(rr_ready, 1)
            for t in range(TT):
                dve.wait_ge(product, t + 1)
                nc.vector.scalar_tensor_tensor(out=sb["x"][:, t, :], in0=ps[:, t % 4, 0:D], scalar=rr[:, t:t + 1],
                                               in1=sb["x"][:, t, :], op0=ALU.mult, op1=ALU.add).then_inc(added, 1)

        @block.gpsimd
        def _(pool):
            pool.wait_ge(mean_ready, 1)
            pool.tensor_tensor(rr[:, :], ms[:, :], sb["minus_half"][:, :], ALU.pow).then_inc(rr_ready, 1)


def router(nc, d, sb, f):
    with ExitStack() as ctx:
        def sbuf(name, shape, dt=F32):
            return ctx.enter_context(nc.sbuf_tensor(name, shape, dt))

        def sem(name):
            return ctx.enter_context(nc.semaphore(name))

        wr = sbuf("wr", [P, KD, E])
        br = sbuf("br", [P, E])
        be2 = sbuf("be2", [E, D])
        bs2 = sbuf("bs2", [P, D])
        logit = sbuf("logit", [P, TT, E])
        top = sbuf("top", [P, TT, 8])
        at = sbuf("at", [P, TT, 8], U32)
        atf = sbuf("atf", [P, TT, 2])
        diff = sbuf("diff", [P, TT])
        ex = sbuf("ex", [P, TT])
        den = sbuf("den", [P, TT])
        w2 = sbuf("w2", [P, TT, 2])
        iot = sbuf("iot", [P, E])
        pick = sbuf("pick", [P, TT, 2, E])
        wT = sbuf("wT", [E, TOK])
        ps_l = ctx.enter_context(nc.psum_tensor("r_ps_l", [P, 512], F32))
        ps_t = ctx.enter_context(nc.psum_tensor("r_ps_t", [P, 2, 512], F32))
        ps_b = ctx.enter_context(nc.psum_tensor("r_ps_b", [P, 4, 512], F32))
        loaded, chain, product = sem("r_loaded"), sem("r_chain"), sem("r_product")
        diff_ready, ex_ready, iota_ready = sem("r_diff_ready"), sem("r_ex_ready"), sem("r_iota_ready")
        w_ready, turned, wT_ready = sem("r_w_ready"), sem("r_turned"), sem("r_wT_ready")
        bias_product, added = sem("r_bias_product"), sem("r_added")
        high = sem("r_high")
        block = ctx.enter_context(nc.Block())

        @block.sync
        def _(sp):
            sp.dma_start(wr[:, :, :], d["wr"].rearrange("(c p) n -> p c n", p=P)).then_inc(loaded, 16)
            sp.dma_start(br[:, :], d["br"].partition_broadcast(P)).then_inc(loaded, 16)
            sp.dma_start(be2[:, :], d["be2"]).then_inc(loaded, 16)
            sp.dma_start(bs2[:, :], d["bs2"].partition_broadcast(P)).then_inc(loaded, 16)
            sp.wait_ge(loaded, 64)

        @block.gpsimd
        def _(pool):
            pool.iota(iot[:, :], pattern=[[1, E]], base=0, channel_multiplier=0,
                      allow_small_or_imprecise_dtypes=True).then_inc(iota_ready, 1)
            pool.wait_ge(high, 1)
            pool.tensor_tensor(f["xl"][:, :, :], sb["xlnT"][:, :, :], f["xh"][:, :, :].bitcast(F32), ALU.subtract)

        @block.tensor
        def _(pe):
            pe.wait_ge(loaded, 64)
            for t in range(TT):
                for k in range(KD):
                    ins = nc.tensor.matmul(ps_l[:, t * E:(t + 1) * E], sb["xlnT"][:, k, t * P:(t + 1) * P],
                                           wr[:, k, :], start=(k == 0), stop=(k == KD - 1))
            ins.then_inc(product, 1)
            pe.wait_ge(w_ready, 1)
            for t in range(TT):
                ins = nc.tensor.transpose(ps_t[0:E, t // 4, (t % 4) * P:(t % 4 + 1) * P], f["w"][:, t, :],
                                          sb["ident"][:, :])
            ins.then_inc(turned, 1)
            pe.wait_ge(wT_ready, 1)
            for t in range(TT):
                if t >= 4:
                    pe.wait_ge(added, t - 3)
                nc.tensor.matmul(ps_b[:, t % 4, 0:D], wT[:, t * P:(t + 1) * P], be2[:, :], start=True, stop=True)\
                    .then_inc(bias_product, 1)

        @block.scalar
        def _(act):
            nc.scalar.copy(f["xh"][:, :, :], sb["xlnT"][:, :, :]).then_inc(high, 1)
            act.wait_ge(diff_ready, 1)
            nc.scalar.activation(ex[:, :], diff[:, :], ACT.Exp).then_inc(ex_ready, 1)
            act.wait_ge(turned, 1)
            nc.scalar.copy(wT[:, :], ps_t[0:E, :, :].rearrange("p a s -> p (a s)")).then_inc(wT_ready, 1)

        @block.vector
        def _(dve):
            c = Chain(dve, chain)
            dve.wait_ge(loaded, 64)
            for t in range(TT):
                c.did(nc.vector.tensor_tensor(sb["x"][:, t, :], sb["x"][:, t, :], bs2[:, :], ALU.add))
            dve.wait_ge(product, 1)
            c.link(nc.vector.tensor_tensor(logit[:, :, :], ps_l[:, 0:TT * E].rearrange("p (t e) -> p t e", t=TT),
                                           br[:, :].unsqueeze(1).broadcast_to([P, TT, E]), ALU.add))
            c.link(nc.vector.tensor_scalar(logit[:, :, :], logit[:, :, :], 1.0 / TAU, None, ALU.mult))
            for t in range(TT):
                c.did(nc.vector.max(top[:, t, :], logit[:, t, :]))
            c.wait()
            nc.vector.tensor_tensor(diff[:, :], top[:, :, 1], top[:, :, 0], ALU.subtract).then_inc(diff_ready, 1)
            for t in range(TT):
                c.did(nc.vector.max_index(at[:, t, :], top[:, t, :], logit[:, t, :]))
            c.wait()
            c.link(nc.vector.tensor_copy(atf[:, :, :], at[:, :, 0:2]))
            dve.wait_ge(ex_ready, 1)
            c.link(nc.vector.tensor_scalar(den[:, :], ex[:, :], 1.0, None, ALU.add))
            c.link(nc.vector.reciprocal(w2[:, :, 0], den[:, :]))
            c.link(nc.vector.tensor_tensor(w2[:, :, 1], ex[:, :], w2[:, :, 0], ALU.mult))
            dve.wait_ge(iota_ready, 1)
            for t in range(TT):
                for i in range(2):
                    c.did(nc.vector.tensor_scalar(pick[:, t, i, :], iot[:, :], atf[:, t, i:i + 1], w2[:, t, i:i + 1],
                                                  ALU.is_equal, ALU.mult))
            c.wait()
            nc.vector.tensor_tensor(f["w"][:, :, :], pick[:, :, 0, :], pick[:, :, 1, :], ALU.add).then_inc(w_ready, 1)
            for t in range(TT):
                dve.wait_ge(bias_product, t + 1)
                nc.vector.tensor_tensor(sb["x"][:, t, :], sb["x"][:, t, :], ps_b[:, t % 4, 0:D], ALU.add)\
                    .then_inc(added, 1)


def experts(nc, d, sb, f):
    with ExitStack() as ctx:
        def sbuf(name, shape, dt=F32):
            return ctx.enter_context(nc.sbuf_tensor(name, shape, dt))

        def sem(name):
            return ctx.enter_context(nc.semaphore(name))

        CH, CS = HR // P, HS // P
        w1 = [sbuf(f"w1_{b}", [P, KD, 2 * HR]) for b in range(2)]
        w1h = [sbuf(f"w1h_{b}", [P, KD, 2 * HR], F32R) for b in range(2)]
        w1l = [sbuf(f"w1l_{b}", [P, KD, 2 * HR], F32R) for b in range(2)]
        w2 = [sbuf(f"w2_{b}", [P, CH, D]) for b in range(2)]
        b1 = [sbuf(f"b1_{b}", [P, 2 * CH]) for b in range(2)]
        gel = sbuf("gel", [P, 2, 512])
        hid = sbuf("hid", [P, 2, CH, 512])
        ps_a = [ctx.enter_context(nc.psum_tensor(f"e_ps_a{i}", [P, 512], F32)) for i in range(2)]
        ps_g = [ctx.enter_context(nc.psum_tensor(f"e_ps_g{i}", [P, 512], F32)) for i in range(2)]
        ps_y = [ctx.enter_context(nc.psum_tensor(f"e_ps_y{i}", [P, 2, 512], F32)) for i in range(2)]
        w1_loaded = [sem("e_w1_loaded0"), sem("e_w1_loaded1")]
        loaded = [sem("e_loaded0"), sem("e_loaded1")]
        high_done = sem("e_high_done")
        split_done = sem("e_split_done")
        up_done = sem("e_up_done")
        gelu_done = sem("e_gelu_done")
        hid_done = sem("e_hid_done")
        down_done = sem("e_down_done")
        added = sem("e_added")
        stored = sem("e_stored")
        block = ctx.enter_context(nc.Block())

        def experts_of(eng, one, tail=None):
            one(None, 0)
            one(0, 1)
            with eng.Fori(0, E // 2 - 1) as it:
                for b in range(2):
                    one(it * 2 + b + 1, b)
            one(E - 1, 0)
            if tail:
                tail()

        def step_of(e, half):
            return half if e is None else e * 2 + 2 + half

        def chunks_before(e, half):
            return half * CS if e is None else 2 * CS + (e * 2 + half) * CH

        def pieces_before(e):
            return 0 if e is None else 2 * CS + e * 2 * CH

        def piece(i, ch):
            return ((ch if i % 2 == 0 else 0) + i // 2) * P

        def next_expert(e):
            ch = CS if e is None else CH
            return (0 if e is None else e + 1), [range(i * 2 * CH // ch, (i + 1) * 2 * CH // ch) for i in range(ch)]

        def is_last(e):
            return isinstance(e, int) and e == E - 1

        def loads_before(e, b, n):
            return 16 * n if e is None else (e + 1 - b) * 8 * n + 16 * n

        @block.sync
        def _(sp):
            def load_w1(e, b):
                if e is None:
                    src, dst = d["ws1"], w1[0][:, :, 0:2 * HS]
                else:
                    src, dst = d["we1"][e], w1[b][:, :, :]
                    if not (isinstance(e, int) and e == 0):
                        sp.wait_ge(split_done, pieces_before(e - 1))
                sp.dma_start(dst, src.rearrange("(c p) n -> p c n", p=P)).then_inc(w1_loaded[b], 16)

            def load_rest(e, b):
                if e is None:
                    sp.dma_start(w2[0][:, 0:CS, :], d["ws2"].rearrange("(c p) n -> p c n", p=P)).then_inc(loaded[0], 16)
                    sp.dma_start(b1[0][:, 0:2 * CS], d["bs1"]).then_inc(loaded[0], 16)
                    return
                if not (isinstance(e, int) and e == 0):
                    sp.wait_ge(down_done, e * 2)
                sp.dma_start(w2[b][:, :, :], d["we2"][e].rearrange("(c p) n -> p c n", p=P)).then_inc(loaded[b], 16)
                sp.dma_start(b1[b][:, :], d["be1"][e]).then_inc(loaded[b], 16)

            def load(e, b):
                if e is None:
                    load_w1(None, 0)
                load_rest(e, b)
                if not is_last(e):
                    load_w1(next_expert(e)[0], 1 - b)

            experts_of(sp, load)
            sp.wait_ge(added, 2 * (E + 1) * 4)
            sp.dma_start(d["out"].rearrange("(t p) d -> p t d", p=P), sb["x"][:, :, :]).then_inc(stored, 16)
            sp.wait_ge(stored, 16)

        @block.tensor
        def _(pe):
            def down(e, half, b):
                ch, first = CS if e is None else CH, chunks_before(e, half)
                for i in range(ch):
                    pe.wait_ge(hid_done, first + i + 1)
                    for tt in range(4):
                        ins = nc.tensor.matmul(ps_y[half][:, tt // 2, (tt % 2) * D:(tt % 2 + 1) * D],
                                               hid[:, half, i, tt * P:(tt + 1) * P], w2[b][:, i, :],
                                               start=(i == 0 and tt % 2 == 0), stop=(i == ch - 1),
                                               skip_group_check=True)
                ins.then_inc(down_done, 1)

            def up(e, half, b):
                ch, first = CS if e is None else CH, chunks_before(e, half)
                for i in range(ch):
                    k2 = i % 2
                    if half == 0:
                        pe.wait_ge(split_done, pieces_before(e) + 2 * i + 2)
                    if not (e is None and half == 0 and i < 2):
                        pe.wait_ge(hid_done, first + i - 1)
                    for ps, col in ((ps_g, (ch + i) * P), (ps_a, i * P)):
                        passes = [(k, w, x) for k in range(KD) for w, x in ((w1h, "xh"), (w1h, "xl"), (w1l, "xh"))]
                        for j, (k, w, x) in enumerate(passes):
                            ins = nc.tensor.matmul(ps[k2][:, :], w[b][:, k, col:col + P],
                                                   f[x][:, k, half * 512:(half + 1) * 512],
                                                   start=(j == 0), stop=(j == len(passes) - 1))
                    ins.then_inc(up_done, 1)

            def one(e, b):
                up(e, 0, b)
                up(e, 1, b)
                pe.wait_ge(loaded[b], loads_before(e, b, 2))
                for half in range(2):
                    if e is not None:
                        pe.wait_ge(added, (step_of(e, half) - 1) * 4)
                    down(e, half, b)

            experts_of(pe, one)

        @block.scalar
        def _(act):
            def split_high(e, b, i, ch):
                if i == 0:
                    act.wait_ge(w1_loaded[b], loads_before(e, b, 1))
                col = piece(i, ch)
                nc.scalar.copy(w1h[b][:, :, col:col + P], w1[b][:, :, col:col + P]).then_inc(high_done, 1)

            def one(e, b):
                ch = CS if e is None else CH
                if e is None:
                    for i in range(2 * CS):
                        split_high(None, 0, i, CS)
                nxt, pieces = next_expert(e)
                act.wait_ge(loaded[b], loads_before(e, b, 2))
                for half in range(2):
                    first = chunks_before(e, half)
                    for i in range(ch):
                        act.wait_ge(up_done, first + i + 1)
                        if not (e is None and half == 0 and i < 2):
                            act.wait_ge(hid_done, first + i - 1)
                        nc.scalar.activation(gel[:, i % 2, :], ps_g[i % 2][:, :], ACT.Gelu,
                                             bias=b1[b][:, ch + i:ch + i + 1]).then_inc(gelu_done, 1)
                        if half == 1 and not is_last(e):
                            for j in pieces[i]:
                                split_high(nxt, 1 - b, j, CH)

            experts_of(act, one)

        @block.gpsimd
        def _(pool):
            def split_low(e, b, i, ch):
                pool.wait_ge(high_done, pieces_before(e) + i + 1)
                col = piece(i, ch)
                pool.tensor_tensor(w1l[b][:, :, col:col + P], w1[b][:, :, col:col + P],
                                   w1h[b][:, :, col:col + P].bitcast(F32), ALU.subtract).then_inc(split_done, 1)

            def one(e, b):
                if e is None:
                    for i in range(2 * CS):
                        split_low(None, 0, i, CS)
                if not is_last(e):
                    nxt, pieces = next_expert(e)
                    for i in range(2 * CH):
                        split_low(nxt, 1 - b, i, CH)

            experts_of(pool, one)

        @block.vector
        def _(dve):
            def one(e, b):
                for half in range(2):
                    step, ch, first = step_of(e, half), CS if e is None else CH, chunks_before(e, half)
                    if e is not None:
                        dve.wait_ge(down_done, step - 1)
                    for i in range(ch):
                        dve.wait_ge(gelu_done, first + i + 1)
                        nc.vector.scalar_tensor_tensor(out=hid[:, half, i, :], in0=ps_a[i % 2][:, :],
                                                       scalar=b1[b][:, i:i + 1], in1=gel[:, i % 2, :],
                                                       op0=ALU.add, op1=ALU.mult).then_inc(hid_done, 1)
                for half in range(2):
                    step = step_of(e, half)
                    dve.wait_ge(down_done, step + 1)
                    for tt in range(4):
                        t = 4 * half + tt
                        if e is not None:
                            dve.wait_ge(added, (step - 2) * 4 + tt + 1)
                        y = ps_y[half][:, tt // 2, (tt % 2) * D:(tt % 2 + 1) * D]
                        if e is None:
                            ins = nc.vector.tensor_tensor(sb["x"][:, t, :], sb["x"][:, t, :], y, ALU.add)
                        else:
                            ins = nc.vector.scalar_tensor_tensor(
                                out=sb["x"][:, t, :], in0=y,
                                scalar=f["w"][:, t, bass.ds(e, 1)], in1=sb["x"][:, t, :],
                                op0=ALU.mult, op1=ALU.add)
                        ins.then_inc(added, 1)

            experts_of(dve, one)


def perceiver_layer(nc, d):
    with ExitStack() as ctx:
        def sbuf(name, shape, dt=F32, to=ctx):
            return to.enter_context(nc.sbuf_tensor(name, shape, dt))

        sb = {"x": sbuf("x_sb", [P, TT, D]), "xlnT": sbuf("xlnT", [P, KD, TOK]), "ident": sbuf("ident", [P, P]),
              "hmask": sbuf("hmask", [P, HC]), "qmask": sbuf("qmask", [P, KD * HQ]),
              "minus_half": sbuf("minus_half", [P, TT])}
        load_inputs(nc, d, sb)
        layer_norm(nc, sb, "ln1")
        with ExitStack() as part:
            a = {n: sbuf(n, s, F32R if n[:2] == "qT" else F32, to=part) for n, s in (
                ("qTh", [P, KD, TOK]), ("qTl", [P, KD, TOK]), ("oT", [P, KD, TOK]), ("wk", [P, KD, D]), ("wv", [P, KD, D]),
                ("wo", [P, KD, D]), ("bk", [P, KD]), ("bv", [P, D]), ("bo", [P, D]))}
            query_projection(nc, d, sb, a)
            attention(nc, d, sb, a)
            output_projection(nc, sb, a)
        layer_norm(nc, sb, "ln2")
        with ExitStack() as part:
            m = {n: sbuf(n, s, dt, to=part) for n, s, dt in (
                ("xs", [P, XC, TOK], F32), ("yg", [P, XC, TOK], F32), ("BT", [P, TOK], F32), ("CT", [P, TOK], F32),
                ("A", [P, XC * UNITS], F32), ("xs3", [96, 4 * XC, TOK], BF16), ("dt3", [3 * NH, TOK], BF16),
                ("sel", [96, 16, 2, NS], BF16), ("seldt", [3 * NH, NH, P], BF16), ("fold", [P, 16, 32], F32),
                ("ones", [P, 1], F32), ("dskip", [P, XC], F32), ("nw", [P, XC], F32), ("w_out", [P, XC, D], F32))}
            ssm_projections(nc, d, sb, m)
            state_space(nc, sb, m)
            ssm_output(nc, sb, m)
        layer_norm(nc, sb, "ln3")
        with ExitStack() as part:
            f = {"w": sbuf("w_tok", [P, TT, E], to=part),
                 "xh": sbuf("xh", [P, KD, TOK], F32R, to=part), "xl": sbuf("xl", [P, KD, TOK], F32R, to=part)}
            router(nc, d, sb, f)
            experts(nc, d, sb, f)


def kernel(**inputs):
    import numpy as _np
    import concourse.bacc as _bacc
    from concourse import mybir as _mybir
    from concourse.bass_utils import run_bass_kernel_spmd as _run

    g = {k: _np.asarray(v) for k, v in inputs.items()}

    def by_feature(v):
        return v.reshape(-1, P).T

    lay = {
        "x": g["x"].reshape(TOK, D),
        "ctxT": g["ctx_1024"].transpose(0, 2, 1),
        "wq": g["L0_xattn_Wq"], "bq": by_feature(g["L0_xattn_bq"]), "wk": g["L0_xattn_Wk"], "bk": by_feature(g["L0_xattn_bk"]),
        "wv": g["L0_xattn_Wv"], "bv": g["L0_xattn_bv"], "wo": g["L0_xattn_Wo"], "bo": g["L0_xattn_bo"],
        "w_inT": g["L0_attn_W_in"].T,
        "w_conv": g["L0_attn_W_conv"].reshape(XC, P, 4).transpose(1, 0, 2),
        "b_conv": by_feature(g["L0_attn_b_conv"]),
        "a_log": g["L0_attn_A_log"].reshape(NH, HD // 2, 2, NS).transpose(2, 3, 0, 1).reshape(P, XC * UNITS),
        "dskip": by_feature(g["L0_attn_D"]), "dt_bias": g["L0_attn_dt_bias"],
        "norm_w": by_feature(g["L0_attn_norm_w"]),
        "w_outT": g["L0_attn_W_out"].T,
        "ws1": g["L0_ffn_Ws1"], "bs1": by_feature(g["L0_ffn_bs1"]), "ws2": g["L0_ffn_Ws2"], "bs2": g["L0_ffn_bs2"],
        "we1": g["L0_ffn_We1"], "be1": g["L0_ffn_be1"].reshape(E, 2 * HR // P, P).transpose(0, 2, 1),
        "we2": g["L0_ffn_We2"], "be2": g["L0_ffn_be2"], "wr": g["L0_ffn_Wr"], "br": g["L0_ffn_br"],
    }
    nc = _bacc.Bacc("TRN2", target_bir_lowering=False, num_devices=1)
    arrays, d = {}, {}
    for name, v in lay.items():
        v = _np.ascontiguousarray(v)
        arrays[f"in_{name}_dram"] = v
        d[name] = nc.dram_tensor(f"in_{name}_dram", v.shape, _mybir.dt.from_np(v.dtype), kind="ExternalInput").ap()
    d["out"] = nc.dram_tensor("out_0_dram", (TOK, D), _mybir.dt.float32, kind="ExternalOutput").ap()
    perceiver_layer(nc, d)
    r = _run(nc, [arrays], core_ids=[0])
    return r.results[0]["out_0_dram"].reshape(NB, L, D)
```

```python
from contextlib import ExitStack

import numpy as np

import concourse.bass as bass
from concourse import mybir

F32 = mybir.dt.float32
F32R = mybir.dt.float32r
BF16 = mybir.dt.bfloat16
U32 = mybir.dt.uint32
ALU = mybir.AluOpType
ACT = mybir.ActivationFunctionType
AX_X = mybir.AxisListType.X

P = 128
NB, L, D = 16, 64, 256
TOK = NB * L
TT = TOK // P
KD = D // P
LN_EPS = 1e-5

S = 1601
H, DH = 16, 16
ROWS = [P] * (S // P) + [S % P]
NT = len(ROWS)
HC = P // DH
HQ = 4
KW = 267
KCH = [(s0, min(KW, S - s0)) for s0 in range(0, S, KW)]
S_FIRST = len(KCH) // 2 * KW
NK = KD * len(KCH)
SLOTS = 5
SLOT = [k for _ in range(4) for k in range(4)] + [k for _ in range(2) for k in range(5)]
SUM_LAG = 2
LAG = 3

DI, NS, NH, HD = 512, 64, 8, 64
XC = DI // P
UNITS = P // 2
RMS_EPS = 1e-6
PARTS = 3
FAR = 2.0 ** 100
A_MIN = 1e-25

E, HR, HS = 12, 768, 512
TAU = 1.5
RTILES = (2 * TOK + E * (P - 1)) // P
BUFS = 3


class Chain:

    def __init__(self, eng, sem):
        self.eng, self.sem, self.n = eng, sem, 0

    def did(self, ins):
        self.n += 1
        ins.then_inc(self.sem, 1)
        return self.n

    def wait(self):
        self.eng.wait_ge(self.sem, self.n)

    def link(self, ins):
        self.did(ins)
        self.wait()


def load_context(sp, d, a, n, par, h):
    s0, s1 = ((0, S_FIRST), (S_FIRST, S))[h]
    sp.dma_start(a["ctxT"][par][:, :, s0:s1], d["ctxT"][n].rearrange("(c p) s -> p c s", p=P)[:, :, s0:s1])\
      .then_inc(a["ctx_loaded"][par][h], 16)


def load_weights(sp, d, sb, a, m, ssm_loaded, slots_cleared):
    sp.dma_start(a["wq"][:, :, :], d["wq"].rearrange("(c p) n -> p c n", p=P)).then_inc(a["q_loaded"], 16)
    sp.dma_start(a["bq"][:, :], d["bq"]).then_inc(a["q_loaded"], 16)
    sp.dma_start(a["wk"][:, :, :], d["wk"].rearrange("(c p) n -> p c n", p=P)).then_inc(a["loaded"], 16)
    load_context(sp, d, a, 0, 0, 0)
    for name in ("wv", "wo"):
        sp.dma_start(a[name][:, :, :], d[name].rearrange("(c p) n -> p c n", p=P)).then_inc(a["loaded"], 16)
    sp.dma_start(a["bk"][:, :], d["bk"]).then_inc(a["loaded"], 16)
    sp.dma_start(a["bv"][:, :], d["bv"].partition_broadcast(P)).then_inc(a["loaded"], 16)
    sp.dma_start(a["bo"][:, :], d["bo"].partition_broadcast(P)).then_inc(a["loaded"], 16)
    load_context(sp, d, a, 0, 0, 1)
    for h in range(2):
        load_context(sp, d, a, 1, 1, h)
    load_ssm(sp, d, m, ssm_loaded)
    sp.dma_start(d["x_slots"].rearrange("(t p) d -> p t d", p=P),
                 sb["zeros"][:, :].unsqueeze(1).broadcast_to([P, RTILES, D])).then_inc(slots_cleared, 16)


def load_inputs(nc, d, sb):
    with ExitStack() as ctx:
        loaded = ctx.enter_context(nc.semaphore("l_loaded"))
        made = ctx.enter_context(nc.semaphore("l_made"))
        chain = ctx.enter_context(nc.semaphore("l_chain"))
        block = ctx.enter_context(nc.Block())

        @block.sync
        def _(sp):
            sp.dma_start(sb["x"][:, :, :], d["x"].rearrange("(t p) d -> p t d", p=P)).then_inc(loaded, 16)
            sp.wait_ge(loaded, 16)

        @block.gpsimd
        def _(pool):
            c = Chain(pool, made)
            c.link(pool.memset(sb["ident"][:, :], 0.0))
            c.link(pool.memset(sb["hmask"][:, :], 1.0))
            c.link(pool.memset(sb["minus_half"][:, :], -0.5))
            c.link(pool.memset(sb["zeros"][:, :], 0.0))
            c.link(pool.affine_select(out=sb["ident"][:, :], in_=sb["ident"][:, :], compare_op=ALU.not_equal,
                                     fill=1.0, base=0, pattern=[[-1, P]], channel_multiplier=1))
            c.link(pool.affine_select(out=sb["hmask"][:, :], in_=sb["hmask"][:, :], compare_op=ALU.is_ge,
                                      fill=0.0, base=0, pattern=[[-DH, HC]], channel_multiplier=1))
            c.link(pool.affine_select(out=sb["hmask"][:, :], in_=sb["hmask"][:, :], compare_op=ALU.is_ge,
                                      fill=0.0, base=DH - 1, pattern=[[DH, HC]], channel_multiplier=-1))

        @block.vector
        def _(dve):
            dve.wait_ge(made, 7)
            for i in range(HQ):
                for c in range(KD):
                    ins = nc.vector.tensor_reduce(sb["qmask"][:, c * HQ + i:c * HQ + i + 1], sb["hmask"][:, i::HQ],
                                                  AX_X, ALU.add)
            ins.then_inc(chain, 1)


def layer_norm(nc, sb, tag, xln=None, loads=None):
    with ExitStack() as ctx:
        stats = ctx.enter_context(nc.sbuf_tensor(f"{tag}_stats", [P, TT, 6], F32))
        mv = ctx.enter_context(nc.sbuf_tensor(f"{tag}_mv", [P, TT, 2], F32))
        vare = ctx.enter_context(nc.sbuf_tensor(f"{tag}_vare", [P, TT], F32))
        rstd = ctx.enter_context(nc.sbuf_tensor(f"{tag}_rstd", [P, TT], F32))
        if xln is None:
            xln = ctx.enter_context(nc.sbuf_tensor(f"{tag}_xln", [P, TT, D], F32))
        ps = ctx.enter_context(nc.psum_tensor(f"{tag}_ps", [P, 4, 512], F32))
        chain = ctx.enter_context(nc.semaphore(f"{tag}_chain"))
        var_ready = ctx.enter_context(nc.semaphore(f"{tag}_var_ready"))
        rstd_ready = ctx.enter_context(nc.semaphore(f"{tag}_rstd_ready"))
        xln_ready = ctx.enter_context(nc.semaphore(f"{tag}_xln_ready"))
        turned = ctx.enter_context(nc.semaphore(f"{tag}_turned"))
        copied = ctx.enter_context(nc.semaphore(f"{tag}_copied"))
        block = ctx.enter_context(nc.Block())

        if loads:
            @block.sync
            def _(sp):
                loads(sp)

        @block.vector
        def _(dve):
            c = Chain(dve, chain)
            for t in range(TT):
                c.did(nc.vector.bn_stats(stats[:, t, :], sb["x"][:, t, :]))
            c.wait()
            for t in range(TT):
                c.did(nc.vector.bn_aggr(mv[:, t, :], stats[:, t, :]))
            c.wait()
            nc.vector.tensor_scalar(vare[:, :], mv[:, :, 1], LN_EPS, None, ALU.add).then_inc(var_ready, 1)
            dve.wait_ge(rstd_ready, 1)
            for t in range(TT):
                nc.vector.tensor_scalar(xln[:, t, :], sb["x"][:, t, :], mv[:, t, 0:1], rstd[:, t:t + 1],
                                        ALU.subtract, ALU.mult).then_inc(xln_ready, 1)

        @block.gpsimd
        def _(pool):
            pool.wait_ge(var_ready, 1)
            pool.tensor_tensor(rstd[:, :], vare[:, :], sb["minus_half"][:, :], ALU.pow).then_inc(rstd_ready, 1)

        @block.tensor
        def _(pe):
            for t in range(TT):
                pe.wait_ge(xln_ready, t + 1)
                if t >= 4:
                    pe.wait_ge(copied, t - 3)
                for c in range(KD):
                    ins = nc.tensor.transpose(ps[:, t % 4, c * P:(c + 1) * P], xln[:, t, c * P:(c + 1) * P],
                                              sb["ident"][:, :])
                ins.then_inc(turned, 1)

        @block.scalar
        def _(act):
            for t in range(TT):
                act.wait_ge(turned, t + 1)
                nc.scalar.copy(sb["xlnT"][:, :, t * P:(t + 1) * P],
                               ps[:, t % 4, 0:KD * P].rearrange("p (c s) -> p c s", c=KD)).then_inc(copied, 1)


def load_ssm(sp, d, m, loaded):
    w = d["w_inT"].rearrange("(c p) n -> p c n", p=P)
    bcol, ccol = 2 * DI, 2 * DI + NS
    for dst, src in ((m["wzx"][:, :, :], w[:, :, 0:2 * DI]),
                     (m["wb"][:, :, 0:NS], w[:, :, bcol:bcol + NS]), (m["wb"][:, :, NS:P], w[:, :, bcol:bcol + NS]),
                     (m["wc"][:, :, 0:NS], w[:, :, ccol:ccol + NS]), (m["wc"][:, :, NS:P], w[:, :, ccol:ccol + NS]),
                     (m["wdt"][:, :, :], w[:, :, ccol + NS:ccol + NS + NH]),
                     (m["convw"][:, :, :], d["w_conv"]), (m["convb"][:, :], d["b_conv"]),
                     (m["dtb"][:, :], d["dt_bias"].rearrange("(h a) -> h a", a=1)), (m["A"][:, :], d["a_log"]),
                     (m["dskip"][:, :], d["dskip"]), (m["nw"][:, :], d["norm_w"]),
                     (m["w_out"][:, :, :], d["w_outT"].rearrange("(c p) n -> p c n", p=P))):
        sp.dma_start(dst, src).then_inc(loaded, 16)


SSM_LOADS = 13
A_LOADS = 6


def build_selectors(pool, m, made):
    c = Chain(pool, made)
    c.link(pool.memset(m["sel"][:, :, :, :], 0.0))
    c.link(pool.memset(m["seldt"][:, :, :], 0.0))
    c.link(pool.memset(m["fold"][:, :, :], 0.0))
    c.link(pool.memset(m["ones"][:, :], 1.0))
    for i in range(3):
        v = m["sel"][32 * i:32 * i + 32, :, :, :]
        c.link(pool.affine_select(out=v, in_=v, compare_op=ALU.not_equal, fill=1.0, base=0,
                                  pattern=[[-2, 16], [-1, 2], [0, NS]], channel_multiplier=1))
    flat = m["fold"][:, :, :].rearrange("p j k -> p (j k)")
    for e in range(2):
        c.link(pool.memset(flat[NS * e:NS * (e + 1), e::34], 1.0))
    for i in range(3):
        c.link(pool.affine_select(out=m["seldt"][:, :, :], in_=m["seldt"][:, :, :], compare_op=ALU.not_equal,
                                  fill=1.0, base=-NH * i, pattern=[[-1, NH], [0, P]], channel_multiplier=1))


def query_projection(nc, sb, a):
    with ExitStack() as ctx:
        wq, bq, loaded = a["wq"], a["bq"], a["q_loaded"]
        q = ctx.enter_context(nc.sbuf_tensor("q", [P, KD, TOK], F32))
        bqs = ctx.enter_context(nc.sbuf_tensor("bqs", [P, KD], F32))
        ps = ctx.enter_context(nc.psum_tensor("q_ps", [P, 4, 512], F32))
        scaled = ctx.enter_context(nc.semaphore("q_scaled"))
        done = ctx.enter_context(nc.semaphore("q_done"))
        high = ctx.enter_context(nc.semaphore("q_high"))
        block = ctx.enter_context(nc.Block())

        @block.tensor
        def _(pe):
            pe.wait_ge(loaded, 32)
            for m in range(KD):
                for n in range(2):
                    for k in range(KD):
                        ins = nc.tensor.matmul(ps[:, 2 * m + n, :], wq[:, k, m * P:(m + 1) * P],
                                               sb["xlnT"][:, k, n * 512:(n + 1) * 512],
                                               start=(k == 0), stop=(k == KD - 1))
                    ins.then_inc(done, 1)

        @block.scalar
        def _(act):
            act.wait_ge(loaded, 32)
            nc.scalar.mul(bqs[:, :], bq[:, :], DH ** -0.5).then_inc(scaled, 1)
            act.wait_ge(scaled, 1)
            for j in range(2 * KD):
                m, n = j // 2, j % 2
                act.wait_ge(done, j + 1)
                nc.scalar.activation(q[:, m, n * 512:(n + 1) * 512], ps[:, j, :], ACT.Identity,
                                     bias=bqs[:, m:m + 1], scale=DH ** -0.5).then_inc(scaled, 1)
                act.wait_ge(scaled, j + 2)
                nc.scalar.copy(a["qTh"][:, m, n * 512:(n + 1) * 512], q[:, m, n * 512:(n + 1) * 512])\
                    .then_inc(high, 1)

        @block.vector
        def _(dve):
            for j in range(2 * KD):
                m, n = j // 2, j % 2
                dve.wait_ge(high, j + 1)
                part = a["qTh"][:, m, n * 512:(n + 1) * 512].bitcast(F32)
                nc.vector.tensor_tensor(a["qTl"][:, m, n * 512:(n + 1) * 512], q[:, m, n * 512:(n + 1) * 512],
                                        part, ALU.subtract)


def attention(nc, d, sb, a, m):
    with ExitStack() as ctx:
        def sbuf(name, shape, dt=F32):
            return ctx.enter_context(nc.sbuf_tensor(name, shape, dt))

        def sem(name):
            return ctx.enter_context(nc.semaphore(name))

        ctxT, ctx_loaded = a["ctxT"], a["ctx_loaded"]
        kT = [[sbuf(f"kT{b}{part}", [P, KD, S], F32R) for part in "hl"] for b in range(2)]
        qbd = [[sbuf(f"qbd{b}{part}", [P, KD, HC, L], F32R) for part in "hl"] for b in range(2)]
        prob = sbuf("prob", [P, SLOTS, H, L])
        mx = sbuf("mx", [P, SLOTS, H])
        vb = sbuf("vb", [P, SLOTS, D])
        half = sbuf("half", [P, H, L // 2])
        quarter = sbuf("quarter", [P, 2, H, L // 4])
        z = sbuf("z", [P, 2, H])
        rz = sbuf("rz", [P, 2, H])
        vn = sbuf("vn", [P, SLOTS, D])
        otmp = sbuf("otmp", [P, KD, HQ, L])

        ps_s = [ctx.enter_context(nc.psum_tensor(f"ps_s{i}", [P, 2, 512], F32)) for i in range(2)]
        ps_v = ctx.enter_context(nc.psum_tensor("ps_v", [P, 512], F32))
        ps_k = [ctx.enter_context(nc.psum_tensor(f"ps_k{i}", [P, 512], F32)) for i in range(2)]
        ps_o = ctx.enter_context(nc.psum_tensor("ps_o", [P, 512], F32))

        qbd_ready = sem("qbd_ready")
        selectors = sem("selectors")
        k_product = sem("k_product")
        kh_ready = sem("kh_ready")
        kT_ready = sem("kT_ready")
        v_product = sem("v_product")
        vb_ready = sem("vb_ready")
        scores_ready = sem("scores_ready")
        max_ready = sem("max_ready")
        sub_ready = sem("sub_ready")
        exp_ready = sem("exp_ready")
        half_ready = sem("half_ready")
        quarter_ready = sem("quarter_ready")
        z_ready = sem("z_ready")
        rz_ready = sem("rz_ready")
        vn_ready = sem("vn_ready")
        pv_done = sem("pv_done")
        o_masked = sem("o_masked")
        o_read = sem("o_read")
        block = ctx.enter_context(nc.Block())

        def pairs(eng, batch, tail=None):
            for par in range(2):
                batch(par, par)
            with eng.Fori(1, NB // 2 - 1) as it:
                for par in range(2):
                    batch(it * 2 + par, par)
            for par in range(2):
                batch(NB - 2 + par, par)
            if tail:
                tail()

        def is_first(n):
            return isinstance(n, int) and n == 0

        def is_last(n):
            return isinstance(n, int) and n == NB - 1

        def before(t, par, back):
            i = (NT * par + t - back) % (2 * NT)
            return ROWS[i % NT], SLOT[i], i % 2

        @block.sync
        def _(sp):
            def batch(n, par):
                if isinstance(n, int) and n < 2:
                    return
                for h, tiles in enumerate((-(-S_FIRST // P), NT)):
                    sp.wait_ge(v_product, (n - 2) * NT + tiles)
                    load_context(sp, d, a, n, par, h)

            pairs(sp, batch)

        @block.gpsimd
        def _(pool):
            def spread_part(n, par, j):
                c, part = j // 2, j % 2
                src = (a["qTh"], a["qTl"])[part]
                pool.tensor_tensor(
                    qbd[par][part][:, c, :, :],
                    src[:, c, bass.ds(n * L, L)].bitcast(F32).unsqueeze(1).broadcast_to([P, HC, L]),
                    sb["hmask"][:, :].unsqueeze(2).broadcast_to([P, HC, L]), ALU.mult).then_inc(qbd_ready, 1)

            def scale_values(g, par, t):
                rows, slot, i = before(t, par, SUM_LAG)
                pool.wait_ge(rz_ready, g + 1)
                pool.wait_ge(vb_ready, g + 1)
                if not (isinstance(g, int) and g < 4):
                    pool.wait_ge(pv_done, g - 3)
                pool.tensor_tensor(vn[0:rows, slot, :].rearrange("p (h e) -> p h e", h=H),
                                   vb[0:rows, slot, :].rearrange("p (h e) -> p h e", h=H),
                                   rz[0:rows, i, :].unsqueeze(2).broadcast_to([rows, H, DH]), ALU.mult)\
                    .then_inc(vn_ready, 1)

            def batch(n, par):
                if is_first(n):
                    for j in range(2 * KD):
                        spread_part(0, 0, j)
                    build_selectors(pool, m, selectors)
                for t in range(NT):
                    g = n * NT + t
                    rows, slot, i = before(t, par, 0)
                    if not (isinstance(g, int) and g < SUM_LAG):
                        scale_values(g - SUM_LAG, par, t)
                    pool.wait_ge(exp_ready, g + 1)
                    if not (isinstance(g, int) and g < 1):
                        pool.wait_ge(quarter_ready, g)
                    pool.tensor_tensor(half[0:rows, :, :], prob[0:rows, slot, :, 0:L // 2],
                                       prob[0:rows, slot, :, L // 2:L], ALU.add).then_inc(half_ready, 1)
                    pool.wait_ge(half_ready, g + 1)
                    if not (isinstance(g, int) and g < 2):
                        pool.wait_ge(z_ready, g - 1)
                    pool.tensor_tensor(quarter[0:rows, i, :, :], half[0:rows, :, 0:L // 4],
                                       half[0:rows, :, L // 4:L // 2], ALU.add).then_inc(quarter_ready, 1)
                    if t in (3, 5, 7, 9) and not is_last(n):
                        spread_part(n + 1, 1 - par, (t - 3) // 2)

            def tail():
                for k in range(SUM_LAG):
                    scale_values(NB * NT - SUM_LAG + k, 0, k)

            pairs(pool, batch, tail)

        @block.scalar
        def _(act):
            def keys(n, par, j):
                m, (s0, w) = j % KD, KCH[j // KD]
                act.wait_ge(k_product, n * NK + j + 1)
                nc.scalar.activation(kT[par][0][:, m, s0:s0 + w], ps_k[j % 2][:, 0:w], ACT.Identity,
                                     bias=a["bk"][:, m:m + 1]).then_inc(kh_ready, 1)

            def batch(n, par):
                if is_first(n):
                    for j in range(NK):
                        keys(0, 0, j)
                for t in range(NT):
                    g = n * NT + t
                    rows, slot, _ = before(t, par, 0)
                    if t >= NT - NK and not is_last(n):
                        keys(n + 1, 1 - par, t - NT + NK)
                    act.wait_ge(sub_ready, g + 1)
                    nc.scalar.activation(prob[0:rows, slot, :, :], prob[0:rows, slot, :, :], ACT.Exp)\
                        .then_inc(exp_ready, 1)

            act.wait_ge(a["loaded"], 16 * A_LOADS)
            pairs(act, batch)

        @block.tensor
        def _(pe):
            def keys(n, par, j):
                m, (s0, w) = j % KD, KCH[j // KD]
                if j % (NK // 2) == 0:
                    pe.wait_ge(ctx_loaded[par][j // (NK // 2)], (n - par) * 8 + 16)
                if not (is_first(n) and j < 2):
                    pe.wait_ge(kT_ready, n * NK + j - 1)
                for k in range(KD):
                    ins = nc.tensor.matmul(ps_k[j % 2][:, 0:w], a["wk"][:, k, m * P:(m + 1) * P],
                                           ctxT[par][:, k, s0:s0 + w], start=(k == 0), stop=(k == KD - 1))
                ins.then_inc(k_product, 1)

            def values_product(g, n, par, t, back):
                rows, slot, i = before(t, par, back)
                tile = (NT * par + t - back) % NT
                pe.wait_ge(vn_ready, g + 1)
                if tile == 0 and not is_first(n):
                    pe.wait_ge(o_masked, n)
                for q in range(H // HQ):
                    j, c = q % 2, q // 2
                    ins = nc.tensor.matmul(ps_o[64 * j:64 * j + 64, c * HQ * L:(c + 1) * HQ * L],
                                           vn[0:rows, slot, HQ * DH * q:HQ * DH * (q + 1)],
                                           prob[0:rows, slot, HQ * q:HQ * (q + 1), :].rearrange("p h l -> p (h l)"),
                                           start=(tile == 0 and c == 0), stop=(tile == NT - 1),
                                           skip_group_check=True)
                ins.then_inc(pv_done, 1)

            def batch(n, par):
                if is_first(n):
                    for j in range(NK):
                        keys(0, 0, j)
                for t in range(NT):
                    g = n * NT + t
                    rows, slot, i = before(t, par, 0)
                    s0 = t * P
                    if not (isinstance(g, int) and g < 1):
                        pe.wait_ge(vb_ready, g)
                    for k in range(KD):
                        ins = nc.tensor.matmul(ps_v[0:rows, 0:D], ctxT[par][:, k, s0:s0 + rows],
                                               a["wv"][:, k, :], start=(k == 0), stop=(k == KD - 1))
                    ins.then_inc(v_product, 1)
                    if t == 0:
                        pe.wait_ge(kT_ready, n * NK + NK)
                        pe.wait_ge(qbd_ready, (n + 1) * 2 * KD)
                    if not (isinstance(g, int) and g < 2):
                        pe.wait_ge(sub_ready, g - 1)
                    for c in range(KD):
                        for kp, qp in ((0, 0), (0, 1), (1, 0)):
                            ins = nc.tensor.matmul(ps_s[i][0:rows, c, :], kT[par][kp][:, c, s0:s0 + rows],
                                                   qbd[par][qp][:, c, :, :].rearrange("p h l -> p (h l)"),
                                                   start=(kp == qp), stop=(kp == 1))
                    ins.then_inc(scores_ready, 1)
                    if t >= NT - NK and not is_last(n):
                        keys(n + 1, 1 - par, t - NT + NK)
                    if not (isinstance(g, int) and g < LAG):
                        values_product(g - LAG, n - 1 if t < LAG else n, par, t, LAG)

            def tail():
                for k in range(LAG):
                    values_product(NB * NT - LAG + k, NB - 1, 0, k, LAG)

            pe.wait_ge(a["loaded"], 16 * A_LOADS)
            pairs(pe, batch, tail)

        @block.vector
        def _(dve):
            def sum_tile(g, par, t):
                rows, slot, i = before(t, par, SUM_LAG)
                dve.wait_ge(quarter_ready, g + 1)
                if not (isinstance(g, int) and g < 2):
                    dve.wait_ge(rz_ready, g - 1)
                nc.vector.tensor_reduce(z[0:rows, i, :], quarter[0:rows, i, :, :], AX_X, ALU.add)\
                    .then_inc(z_ready, 1)

            def invert_tile(g, par, t):
                rows, slot, i = before(t, par, SUM_LAG)
                dve.wait_ge(z_ready, g + 1)
                if not (isinstance(g, int) and g < 2):
                    dve.wait_ge(vn_ready, g - 1)
                nc.vector.reciprocal(rz[0:rows, i, :], z[0:rows, i, :]).then_inc(rz_ready, 1)

            def take_output(n):
                o = ps_o[:, :].rearrange("p (c i l) -> p (c i) l", c=KD, i=HQ)
                dve.wait_ge(pv_done, n * NT + NT)
                if not is_first(n):
                    dve.wait_ge(o_read, n)
                nc.vector.tensor_tensor(
                    otmp[:, :, :, :].rearrange("p c i l -> p (c i) l"), o,
                    sb["qmask"][:, :].unsqueeze(2).broadcast_to([P, KD * HQ, L]), ALU.mult).then_inc(o_masked, 1)

            def fold_output(n):
                dve.wait_ge(o_masked, n + 1)
                nc.vector.tensor_reduce(a["oT"][:, :, bass.ds(n * L, L)],
                                        otmp[:, :, :, :].rearrange("p c i l -> p c l i"), AX_X, ALU.add)\
                    .then_inc(o_read, 1)

            def low_keys(n, par, j):
                m, (s0, w) = j % KD, KCH[j // KD]
                dve.wait_ge(kh_ready, n * NK + j + 1)
                nc.vector.scalar_tensor_tensor(out=kT[par][1][:, m, s0:s0 + w], in0=ps_k[j % 2][:, 0:w],
                                               scalar=a["bk"][:, m:m + 1],
                                               in1=kT[par][0][:, m, s0:s0 + w].bitcast(F32),
                                               op0=ALU.add, op1=ALU.subtract).then_inc(kT_ready, 1)

            def batch(n, par):
                if is_first(n):
                    for j in range(NK):
                        low_keys(0, 0, j)
                for t in range(NT):
                    g = n * NT + t
                    rows, slot, i = before(t, par, 0)
                    early = isinstance(g, int) and g < 4
                    summed = not (isinstance(g, int) and g < SUM_LAG)
                    if summed:
                        sum_tile(g - SUM_LAG, par, t)
                    dve.wait_ge(v_product, g + 1)
                    if not early:
                        dve.wait_ge(vn_ready, g - 3)
                    nc.vector.tensor_tensor(vb[0:rows, slot, :], ps_v[0:rows, 0:D], a["bv"][0:rows, :], ALU.add)\
                        .then_inc(vb_ready, 1)
                    if summed:
                        invert_tile(g - SUM_LAG, par, t)
                    scores = ps_s[i][0:rows, :, :].rearrange("p c (h l) -> p (c h) l", h=HC)
                    dve.wait_ge(scores_ready, g + 1)
                    nc.vector.tensor_reduce(mx[0:rows, slot, :], scores, AX_X, ALU.max).then_inc(max_ready, 1)
                    dve.wait_ge(max_ready, g + 1)
                    if not early:
                        dve.wait_ge(pv_done, g - 3)
                    nc.vector.tensor_tensor(prob[0:rows, slot, :, :], scores,
                                            mx[0:rows, slot, :].unsqueeze(2).broadcast_to([rows, H, L]),
                                            ALU.subtract).then_inc(sub_ready, 1)
                    if t >= NT - NK and not is_last(n):
                        low_keys(n + 1, 1 - par, t - NT + NK)
                    if t == LAG - 1 and not is_first(n):
                        take_output(n - 1)
                    if t == LAG and not is_first(n):
                        fold_output(n - 1)

            def tail():
                for k in range(SUM_LAG):
                    g = NB * NT - SUM_LAG + k
                    sum_tile(g, 0, k)
                    invert_tile(g, 0, k)
                take_output(NB - 1)
                fold_output(NB - 1)

            dve.wait_ge(a["loaded"], 16 * A_LOADS)
            pairs(dve, batch, tail)


def output_projection(nc, sb, a):
    with ExitStack() as ctx:
        ps = ctx.enter_context(nc.psum_tensor("op_ps", [P, TT, 512], F32))
        biased = ctx.enter_context(nc.semaphore("op_biased"))
        done = ctx.enter_context(nc.semaphore("op_done"))
        block = ctx.enter_context(nc.Block())

        @block.tensor
        def _(pe):
            for t in range(TT):
                for c in range(KD):
                    ins = nc.tensor.matmul(ps[:, t, 0:D], a["oT"][:, c, t * P:(t + 1) * P], a["wo"][:, c, :],
                                           start=(c == 0), stop=(c == KD - 1))
                ins.then_inc(done, 1)

        @block.vector
        def _(dve):
            for t in range(TT):
                nc.vector.tensor_tensor(sb["x"][:, t, :], sb["x"][:, t, :], a["bo"][:, :], ALU.add).then_inc(biased, 1)
            for t in range(TT):
                dve.wait_ge(done, t + 1)
                dve.wait_ge(biased, t + 1)
                nc.vector.tensor_tensor(sb["x"][:, t, :], sb["x"][:, t, :], ps[:, t, 0:D], ALU.add)


def move_parts(sp, m, moved, s):
    for i, part in enumerate(m["part"]):
        if s == 0:
            sp.dma_start(m["dt3"][NH * i:NH * (i + 1), :], part[0:NH, 0, :]).then_inc(moved[0], 16)
            continue
        for q in range(4):
            sp.dma_start(m["xs3"][32 * i:32 * i + 32, 4 * (s - 1) + q, :],
                         part[32 * q:32 * q + 32, s % PARTS, :]).then_inc(moved[s % PARTS], 16)


def moves(s):
    return 3 if s == 0 else 12


def ssm_projections(nc, d, sb, m, f, loaded, moved):
    with ExitStack() as ctx:
        def sbuf(name, shape, dt=F32):
            return ctx.enter_context(nc.sbuf_tensor(name, shape, dt))

        def sem(name):
            return ctx.enter_context(nc.semaphore(name))

        conv = sbuf("conv", [P, 2, NB, L])
        dt_v = sbuf("dt_v", [NH, NB, L])
        dt_a = sbuf("dt_a", [NH, NB, L])
        part = m["part"]
        left = sbuf("left", [P, 2, TOK])

        ps = [ctx.enter_context(nc.psum_tensor(f"sp_ps{i}", [P, 2, 512], F32)) for i in range(4)]
        product = sem("sp_product")
        bc_ready = sem("sp_bc_ready")
        z_ready = sem("sp_z_ready")
        a_exp = sem("sp_a_exp")
        conv_bias = sem("sp_conv_bias")
        conv_chain = sem("sp_conv_chain")
        conv_done = sem("sp_conv_done")
        x_ready = sem("sp_x_ready")
        dt_act = sem("sp_dt_act")
        dt_ready = sem("sp_dt_ready")
        hi_ready = sem("sp_hi_ready")
        left_ready = sem("sp_left_ready")
        mid_ready = sem("sp_mid_ready")
        lo_ready = sem("sp_lo_ready")
        cleared, made, left_bias = sem("sp_cleared"), sem("sp_made"), sem("sp_left_bias")
        f["bias"] = sbuf("bias", [96, 2 * HR + D])
        f["rounded"] = sbuf("rounded", [96, 2 * HR + D], BF16)
        block = ctx.enter_context(nc.Block())

        jobs = [("dt", 0)] + [("x", c) for c in range(XC)] + [("b", 0), ("c", 0)] + [("z", c) for c in range(XC)]

        def out_of(eng, j):
            kind, c = jobs[j]
            if kind == "dt":
                eng.wait_ge(dt_act, 2)
            elif kind == "x":
                eng.wait_ge(conv_done, c + 1)
            elif kind in "bc":
                eng.wait_ge(bc_ready, 1 + (kind == "c"))
            else:
                eng.wait_ge(z_ready, c + 1)

        def banks(j, rows=P):
            return ps[j % 4][0:rows, :, :].rearrange("p a s -> p (a s)")

        def source(s):
            return dt_a[:, :, :].rearrange("p b l -> p (b l)") if s == 0 else m["xs"][:, s - 1, :]

        def rows_of(s):
            return NH if s == 0 else P

        @block.gpsimd
        def _(pool):
            clear_biases(pool, f, cleared)
            build_routing(pool, f, made)
            bias_parts(pool, sb, f, left_bias)

        @block.sync
        def _(sp):
            load_experts(sp, d, f, cleared)
            for s in range(PARTS):
                sp.wait_ge(lo_ready, s + 1)
                move_parts(sp, m, moved, s)

        @block.tensor
        def _(pe):
            pe.wait_ge(loaded, SSM_LOADS * 16)
            for j, (kind, c) in enumerate(jobs):
                if j >= 4:
                    out_of(pe, j - 4)
                w = {"x": m["wzx"][:, :, DI + c * P:DI + (c + 1) * P], "z": m["wzx"][:, :, c * P:(c + 1) * P],
                     "b": m["wb"][:, :, :], "c": m["wc"][:, :, :], "dt": m["wdt"][:, :, :]}[kind]
                rows = NH if kind == "dt" else P
                for n in range(2):
                    for k in range(KD):
                        ins = nc.tensor.matmul(ps[j % 4][0:rows, n, :], w[:, k, :],
                                               sb["xlnT"][:, k, n * 512:(n + 1) * 512],
                                               start=(k == 0), stop=(k == KD - 1))
                ins.then_inc(product, 1)

        @block.scalar
        def _(act):
            def conv_first(c):
                act.wait_ge(product, c + 2)
                if c >= 2:
                    act.wait_ge(x_ready, c - 1)
                nc.scalar.activation(conv[:, c % 2, :, :].rearrange("p b l -> p (b l)"), banks(c + 1), ACT.Identity,
                                     bias=m["convb"][:, c:c + 1], scale=m["convw"][:, c, 3:4]).then_inc(conv_bias, 1)

            def silu_x(c):
                act.wait_ge(conv_done, c + 1)
                nc.scalar.activation(m["xs"][:, c, :], conv[:, c % 2, :, :].rearrange("p b l -> p (b l)"),
                                     ACT.Silu).then_inc(x_ready, 1)

            def high(s):
                if s == 0:
                    act.wait_ge(dt_ready, 2)
                else:
                    act.wait_ge(x_ready, s)
                if s >= PARTS:
                    act.wait_ge(moved[s % PARTS], 16 * sum(moves(r) for r in range(s % PARTS, s, PARTS)))
                nc.scalar.copy(part[0][0:rows_of(s), s % PARTS, :], source(s)).then_inc(hi_ready, 1)

            def middle(s):
                act.wait_ge(left_ready, s + 1)
                nc.scalar.copy(part[1][0:rows_of(s), s % PARTS, :], left[0:rows_of(s), s % 2, :]).then_inc(mid_ready, 1)

            act.wait_ge(loaded, SSM_LOADS * 16)
            nc.scalar.activation(m["A"][:, :], m["A"][:, :], ACT.Exp).then_inc(a_exp, 1)
            act.wait_ge(product, 1)
            v = dt_v[:, :, :].rearrange("p b l -> p (b l)")
            e = dt_a[:, :, :].rearrange("p b l -> p (b l)")
            dc = Chain(act, dt_act)
            dc.did(nc.scalar.activation(v, banks(0, NH), ACT.Identity, bias=m["dtb"][:, 0:1]))
            dc.link(nc.scalar.activation(e, banks(0, NH), ACT.Abs, bias=m["dtb"][:, 0:1]))
            dc.link(nc.scalar.activation(e, e, ACT.Exp, scale=-1.0))
            dc.link(nc.scalar.activation(e, e, ACT.Ln, bias=1.0))
            conv_first(0)
            high(0)
            conv_first(1)
            middle(0)
            silu_x(0)
            high(1)
            for c in range(2, XC):
                conv_first(c)
                middle(c - 1)
                silu_x(c - 1)
                high(c)
            middle(XC - 1)
            silu_x(XC - 1)
            high(XC)
            middle(XC)
            for j, (kind, c) in enumerate(jobs):
                if kind == "z":
                    act.wait_ge(product, j + 1)
                    nc.scalar.activation(m["yg"][:, c, :], banks(j), ACT.Silu).then_inc(z_ready, 1)

        @block.vector
        def _(dve):
            cc = Chain(dve, conv_chain)

            def convolve(c):
                dve.wait_ge(conv_bias, c + 1)
                x4 = banks(c + 1).rearrange("p (b l) -> p b l", b=NB)
                for k in range(1, 4):
                    out = conv[:, c % 2, :, k:L]
                    ins = nc.vector.scalar_tensor_tensor(out=out, in0=x4[:, :, 0:L - k],
                                                         scalar=m["convw"][:, c, 3 - k:4 - k], in1=out,
                                                         op0=ALU.mult, op1=ALU.add)
                    if k < 3:
                        cc.link(ins)
                ins.then_inc(conv_done, 1)

            def leave(s):
                dve.wait_ge(hi_ready, s + 1)
                if s >= 2:
                    dve.wait_ge(lo_ready, s - 1)
                nc.vector.tensor_tensor(left[0:rows_of(s), s % 2, :], source(s), part[0][0:rows_of(s), s % PARTS, :],
                                        ALU.subtract).then_inc(left_ready, 1)

            def low(s):
                dve.wait_ge(mid_ready, s + 1)
                nc.vector.tensor_tensor(part[2][0:rows_of(s), s % PARTS, :], left[0:rows_of(s), s % 2, :],
                                        part[1][0:rows_of(s), s % PARTS, :], ALU.subtract).then_inc(lo_ready, 1)

            def keep(name, j):
                dve.wait_ge(product, j + 1)
                nc.vector.tensor_copy(m[name][:, :], banks(j)).then_inc(bc_ready, 1)

            dve.wait_ge(a_exp, 1)
            nc.vector.tensor_scalar(m["A"][:, :], m["A"][:, :], -1.0, -A_MIN, ALU.mult, ALU.min)
            dve.wait_ge(dt_act, 4)
            nc.vector.scalar_tensor_tensor(out=dt_a[:, :, :], in0=dt_v[:, :, :], scalar=0.0, in1=dt_a[:, :, :],
                                           op0=ALU.max, op1=ALU.add).then_inc(dt_ready, 1)
            dve.wait_ge(dt_ready, 1)
            nc.vector.memset(dt_a[:, :, 0:1], FAR).then_inc(dt_ready, 1)
            convolve(0)
            leave(0)
            low(0)
            convolve(1)
            leave(1)
            convolve(2)
            low(1)
            leave(2)
            convolve(3)
            low(2)
            leave(3)
            keep("BT", XC + 1)
            low(3)
            keep("CT", XC + 2)
            leave(4)
            low(4)


def state_space(nc, sb, m, moved):
    with ExitStack() as ctx:
        def sbuf(name, shape, dt=F32):
            return ctx.enter_context(nc.sbuf_tensor(name, shape, dt))

        def sem(name):
            return ctx.enter_context(nc.semaphore(name))

        DECAYS, INPS, STATES, SEEN = 2, 4, 4, 4
        decay = sbuf("decay", [P, DECAYS, TOK])
        inp = sbuf("inp", [P, INPS, TOK])
        state = sbuf("state", [P, STATES, TOK])
        seen = sbuf("seen", [P, SEEN, TOK])
        ps_dt = ctx.enter_context(nc.psum_tensor("ps_dt", [P, 2, 512], F32))
        ps_x = [ctx.enter_context(nc.psum_tensor(f"ps_x{i}", [P, 2, 512], F32)) for i in range(2)]
        ps_y = ctx.enter_context(nc.psum_tensor("ps_y", [P, 2, 512], F32))
        dt_ready = sem("m_dt_ready")
        xb_ready = sem("m_xb_ready")
        decay_ready = sem("m_decay_ready")
        inp_ready = sem("m_inp_ready")
        state_ready = sem("m_state_ready")
        seen_ready = sem("m_seen_ready")
        folded = sem("m_folded")
        y_skip = sem("m_y_skip")
        y_out = sem("m_y_out")
        block = ctx.enter_context(nc.Block())

        order = [(2 * (k // 32) + k % 2, (k % 32) // 2) for k in range(UNITS)]
        FOLD_LAG = 4

        def flat(t):
            return t[:, :, :].rearrange("p a s -> p (a s)")

        def chunks(eng, chunk, tail=None):
            chunk(0)
            with eng.Fori(1, XC) as c:
                chunk(c)
            if tail:
                tail()

        def has(c, k, back):
            return k >= back or not isinstance(c, int)

        @block.sync
        def _(sp):
            for s in range(PARTS, XC + 1):
                move_parts(sp, m, moved, s)

        @block.tensor
        def _(pe):
            def fold(c, k, g):
                q, j = order[k]
                pe.wait_ge(seen_ready, g + 1)
                if k == 0 and not isinstance(c, int):
                    pe.wait_ge(y_skip, c)
                for n in range(2):
                    ins = nc.tensor.matmul(ps_y[32 * q:32 * q + 32, n, :], m["fold"][:, j, :],
                                           seen[:, k % SEEN, n * 512:(n + 1) * 512],
                                           start=(j == 0), stop=(j == 15), skip_group_check=True)
                ins.then_inc(folded, 1)

            def chunk(c):
                splits = (0, 1) if isinstance(c, int) else range(XC + 1)
                for i in range(PARTS):
                    if sum(moves(s) for s in splits if s % PARTS == i) > 0:
                        pe.wait_ge(moved[i], 16 * sum(moves(s) for s in splits if s % PARTS == i))
                for k in range(UNITS):
                    q, j = order[k]
                    g = c * UNITS + k
                    if k % 32 == 0:
                        if has(c, k, 1):
                            pe.wait_ge(decay_ready, g)
                        for n in range(2):
                            ins = nc.tensor.matmul(ps_dt[:, n, :], m["seldt"][:, c * 2 + k // 32, :],
                                                   m["dt3"][:, n * 512:(n + 1) * 512], start=True, stop=True)
                        ins.then_inc(dt_ready, 1)
                    if has(c, k, 2):
                        pe.wait_ge(inp_ready, g - 1)
                    for n in range(2):
                        ins = nc.tensor.matmul(ps_x[k % 2][:, n, :],
                                               m["sel"][:, j, :, :].rearrange("p e s -> p (e s)"),
                                               m["xs3"][:, c * 4 + q, n * 512:(n + 1) * 512], start=True, stop=True)
                    ins.then_inc(xb_ready, 1)
                    if has(c, k, FOLD_LAG):
                        fold(c, (k - FOLD_LAG) % UNITS, g - FOLD_LAG)

            def tail():
                for k in range(UNITS - FOLD_LAG, UNITS):
                    fold(XC - 1, k, (XC - 1) * UNITS + k)

            chunks(pe, chunk, tail)

        @block.scalar
        def _(act):
            def chunk(c):
                for k in range(UNITS):
                    q, j = order[k]
                    g = c * UNITS + k
                    if k % 32 == 0:
                        act.wait_ge(dt_ready, c * 2 + k // 32 + 1)
                    if has(c, k, DECAYS):
                        act.wait_ge(state_ready, g - DECAYS + 1)
                    nc.scalar.activation(decay[:, k % DECAYS, :], flat(ps_dt), ACT.Exp,
                                         scale=m["A"][:, bass.ds(c * UNITS + 16 * q + j, 1)]).then_inc(decay_ready, 1)

            chunks(act, chunk)

        @block.vector
        def _(dve):
            def scan(c, k, g):
                dve.wait_ge(inp_ready, g + 1)
                dve.wait_ge(decay_ready, g + 1)
                if k >= STATES or not isinstance(c, int):
                    dve.wait_ge(seen_ready, g - STATES + 1)
                nc.vector.tensor_tensor_scan(state[:, k % STATES, :], decay[:, k % DECAYS, :], inp[:, k % INPS, :],
                                             0.0, ALU.mult, ALU.add).then_inc(state_ready, 1)

            def take_output(c):
                dve.wait_ge(folded, c * UNITS + UNITS)
                x = m["xs"][:, bass.ds(c, 1), :].rearrange("p a s -> p (a s)")
                nc.vector.scalar_tensor_tensor(out=x, in0=x, scalar=m["dskip"][:, bass.ds(c, 1)], in1=flat(ps_y),
                                               op0=ALU.mult, op1=ALU.add).then_inc(y_skip, 1)

            def gate_output(c):
                dve.wait_ge(y_skip, c + 1)
                x = m["xs"][:, bass.ds(c, 1), :].rearrange("p a s -> p (a s)")
                y = m["yg"][:, bass.ds(c, 1), :].rearrange("p a s -> p (a s)")
                nc.vector.tensor_tensor(y, x, y, ALU.mult).then_inc(y_out, 1)

            def chunk(c):
                for k in range(UNITS):
                    g = c * UNITS + k
                    dve.wait_ge(xb_ready, g + 1)
                    if has(c, k, INPS):
                        dve.wait_ge(state_ready, g - INPS + 1)
                    nc.vector.tensor_tensor(inp[:, k % INPS, :], flat(ps_x[k % 2]), m["BT"][:, :], ALU.mult)\
                        .then_inc(inp_ready, 1)
                    if has(c, k, 1):
                        scan(c, (k - 1) % UNITS, g - 1)
                    if not isinstance(c, int):
                        if k == FOLD_LAG - 1:
                            take_output(c - 1)
                        if k == FOLD_LAG:
                            gate_output(c - 1)

            def tail():
                scan(XC - 1, UNITS - 1, XC * UNITS - 1)
                take_output(XC - 1)
                gate_output(XC - 1)

            chunks(dve, chunk, tail)

        @block.gpsimd
        def _(pool):
            def chunk(c):
                for k in range(UNITS):
                    g = c * UNITS + k
                    pool.wait_ge(state_ready, g + 1)
                    if has(c, k, SEEN):
                        pool.wait_ge(folded, g - SEEN + 1)
                    pool.tensor_tensor(seen[:, k % SEEN, :], state[:, k % STATES, :], m["CT"][:, :], ALU.mult)\
                        .then_inc(seen_ready, 1)

            chunks(pool, chunk)


def ssm_output(nc, sb, m):
    with ExitStack() as ctx:
        ms = ctx.enter_context(nc.sbuf_tensor("so_ms", [P, TT], F32))
        rr = ctx.enter_context(nc.sbuf_tensor("so_rr", [P, TT], F32))
        ps_m = ctx.enter_context(nc.psum_tensor("so_ps_m", [P, 512], F32))
        ps = ctx.enter_context(nc.psum_tensor("so_ps", [P, TT, D], F32))
        squared = ctx.enter_context(nc.semaphore("so_squared"))
        scaled = ctx.enter_context(nc.semaphore("so_scaled"))
        folded = ctx.enter_context(nc.semaphore("so_folded"))
        summed = ctx.enter_context(nc.semaphore("so_summed"))
        mean_ready = ctx.enter_context(nc.semaphore("so_mean_ready"))
        rr_ready = ctx.enter_context(nc.semaphore("so_rr_ready"))
        product = ctx.enter_context(nc.semaphore("so_product"))
        block = ctx.enter_context(nc.Block())

        @block.scalar
        def _(act):
            for c in range(XC):
                nc.scalar.activation(m["xs"][:, c, :], m["yg"][:, c, :], ACT.Square).then_inc(squared, 1)

        @block.tensor
        def _(pe):
            pe.wait_ge(scaled, XC)
            for t in range(TT):
                for c in range(XC):
                    ins = nc.tensor.matmul(ps[:, t, :], m["yg"][:, c, t * P:(t + 1) * P], m["w_out"][:, c, :],
                                           start=(c == 0), stop=(c == XC - 1))
                ins.then_inc(product, 1)
                if t == TT // 2:
                    pe.wait_ge(folded, XC - 1)
                    for u in range(TT):
                        ins = nc.tensor.matmul(ps_m[:, u:u + 1], m["xs"][:, 0, u * P:(u + 1) * P], m["ones"][:, :],
                                               start=True, stop=True)
                    ins.then_inc(summed, 1)

        @block.vector
        def _(dve):
            for c in range(XC):
                nc.vector.tensor_scalar(m["w_out"][:, c, :], m["w_out"][:, c, :], m["nw"][:, c:c + 1], None, ALU.mult)\
                    .then_inc(scaled, 1)
            for c in range(1, XC):
                dve.wait_ge(squared, c + 1)
                if c > 1:
                    dve.wait_ge(folded, c - 1)
                nc.vector.tensor_tensor(m["xs"][:, 0, :], m["xs"][:, 0, :], m["xs"][:, c, :], ALU.add)\
                    .then_inc(folded, 1)
            dve.wait_ge(summed, 1)
            nc.vector.tensor_scalar(ms[:, :], ps_m[:, 0:TT], 1.0 / DI, RMS_EPS, ALU.mult, ALU.add)\
                .then_inc(mean_ready, 1)
            dve.wait_ge(rr_ready, 1)
            for t in range(TT):
                dve.wait_ge(product, t // 2 * 2 + 2)
                nc.vector.scalar_tensor_tensor(out=sb["x"][:, t, :], in0=ps[:, t, :], scalar=rr[:, t:t + 1],
                                               in1=sb["x"][:, t, :], op0=ALU.mult, op1=ALU.add)

        @block.gpsimd
        def _(pool):
            pool.wait_ge(mean_ready, 1)
            pool.tensor_tensor(rr[:, :], ms[:, :], sb["minus_half"][:, :], ALU.pow).then_inc(rr_ready, 1)


def load_experts(sp, d, f, cleared):
    sp.dma_start(f["wr"][:, :, :], d["wr"].rearrange("(c p) n -> p c n", p=P)).then_inc(f["wr_loaded"], 16)
    sp.dma_start(f["br"][:, :], d["br"].partition_broadcast(P)).then_inc(f["wr_loaded"], 16)
    sp.wait_ge(cleared, 1)
    for i in range(3):
        r = 32 * i
        sp.dma_start(f["bias"][r:r + E, 0:2 * HR], d["be1"]).then_inc(f["bias_loaded"], 16)
        sp.dma_start(f["bias"][r:r + E, 2 * HR:2 * HR + D], d["be2"]).then_inc(f["bias_loaded"], 16)
        sp.dma_start(f["bias"][r + E:r + E + 1, 0:2 * HS], d["bs1"]).then_inc(f["bias_loaded"], 16)
        sp.dma_start(f["bias"][r + E:r + E + 1, 2 * HR:2 * HR + D], d["bs2"]).then_inc(f["bias_loaded"], 16)
    sp.dma_start(f["ws1"][:, :, :], d["ws1"].rearrange("(c p) n -> p c n", p=P)).then_inc(f["ws_loaded"], 16)
    sp.dma_start(f["ws2"][:, :, :], d["ws2"].rearrange("(c p) n -> p c n", p=P)).then_inc(f["ws_loaded"], 16)


def clear_biases(pool, f, cleared):
    pool.memset(f["bias"][:, :], 0.0).then_inc(cleared, 1)


def build_routing(pool, f, made):
    def iota(out, pattern, mult=0):
        return pool.iota(out, pattern=pattern, base=0, channel_multiplier=mult, allow_small_or_imprecise_dtypes=True)

    c = Chain(pool, made)
    c.link(iota(f["experts"][:, :], [[1, E]]))
    c.link(iota(f["row"][:, :], [[0, 1]], 1))
    c.link(iota(f["tile_no"][:, :], [[1, RTILES]]))
    c.link(iota(f["full"][:, :], [[P, TT]]))
    c.link(pool.memset(f["before"][:, :], 1.0))
    c.link(pool.affine_select(out=f["before"][:, :], in_=f["before"][:, :], compare_op=ALU.is_ge, fill=0.0,
                              base=-1, pattern=[[1, P]], channel_multiplier=-1))
    c.link(pool.memset(f["all"][:, :], 1.0))
    c.link(pool.memset(f["one"][:, :], 1.0))
    c.link(pool.memset(f["taken"][:, TT, :], 0.0))
    c.link(pool.memset(f["sel_shared"][:, :], 0.0))
    for i in range(3):
        rows = slice(32 * i, 32 * i + 32)
        c.link(iota(f["part_row"][rows, :], [[0, 1]], 1))
        c.link(pool.affine_select(out=f["sel_shared"][rows, :], in_=f["sel_shared"][rows, :], compare_op=ALU.not_equal,
                                  fill=1.0, base=-E, pattern=[[0, P]], channel_multiplier=1))


def bias_parts(pool, sb, f, chain):
    c = Chain(pool, chain)

    def zero(rows):
        return sb["zeros"][rows, 0:1].broadcast_to([32, 2 * HR + D])

    pool.wait_ge(f["bias_loaded"], 16 * 12)
    for i in range(3):
        rows = [slice(r, r + 32) for r in range(32 * i, 96, 32)]
        c.link(pool.tensor_tensor(f["biases"][rows[0], :], f["bias"][rows[0], :], zero(rows[0]), ALU.add))
        for r in rows[1:]:
            c.link(pool.tensor_tensor(f["rounded"][r, :], f["bias"][r, :], zero(r), ALU.add))
            c.link(pool.tensor_tensor(f["bias"][r, :], f["bias"][r, :], f["rounded"][r, :], ALU.subtract))


def experts(nc, d, sb, f):
    with ExitStack() as ctx:
        def sbuf(name, shape, dt=F32):
            return ctx.enter_context(nc.sbuf_tensor(name, shape, dt))

        def sem(name):
            return ctx.enter_context(nc.semaphore(name))

        logit = sbuf("logit", [P, TT, E])
        top = sbuf("top", [P, TT, 8])
        at = sbuf("at", [P, TT, 8], U32)
        atf = sbuf("atf", [P, TT, 2])
        diff = sbuf("diff", [P, TT])
        ex = sbuf("ex", [P, TT])
        den = sbuf("den", [P, TT])
        share = sbuf("share", [P, TT, 2])
        pick = sbuf("pick", [P, TT, 2, E])
        rank = sbuf("rank", [P, TT + 1, E])
        above = sbuf("above", [P, E, TT])
        tiles = sbuf("tiles", [P, E])
        upto = sbuf("upto", [P, E])
        first = sbuf("first", [P, E])
        place = sbuf("place", [P, TT, E])
        placed = sbuf("placed", [P, TT, 2, E])
        slot_f = sbuf("slot_f", [P, TT, 2])
        slot = sbuf("slot", [P, TT * 2], U32)
        passed = sbuf("passed", [P, RTILES, E])
        owner = sbuf("owner", [P, RTILES])
        weight_row_f = sbuf("weight_row_f", [P, RTILES])
        weight_row = sbuf("weight_row", [P, RTILES], U32)
        mine = sbuf("mine", [96, RTILES])
        sel = sbuf("sel_tile", [96, RTILES, P], BF16)
        w1 = [sbuf(f"w1_{b}", [P, KD * 2 * HR]) for b in range(BUFS)]
        w2 = [sbuf(f"w2_{b}", [P, HR // P * D]) for b in range(BUFS)]
        xg = [sbuf(f"xg_{b}", [P, D]) for b in range(BUFS)]
        w1h = [sbuf(f"w1h_{half}", [P, KD * 2, HR // 2], F32R) for half in range(2)]
        w1l = [sbuf(f"w1l_{half}", [P, KD * 2, HR // 2], F32R) for half in range(2)]
        xTh = [sbuf(f"xTh_{b}", [P, KD, P], F32R) for b in range(BUFS)]
        xTl = [sbuf(f"xTl_{b}", [P, KD, P], F32R) for b in range(BUFS)]
        y = [sbuf(f"y_{b}", [P, D]) for b in range(BUFS)]
        gel = sbuf("gel", [P, 2, HR // 2])
        hid = sbuf("hid", [P, 2, HR // 2])
        hidT = sbuf("hidT", [P, 2, HR // 2])
        back = sbuf("back", [P, TT, 2, D])

        ps_a = [ctx.enter_context(nc.psum_tensor(f"e_ps_a{i}", [P, 512], F32)) for i in range(2)]
        ps_g = [ctx.enter_context(nc.psum_tensor(f"e_ps_g{i}", [P, 512], F32)) for i in range(2)]
        ps_h = [ctx.enter_context(nc.psum_tensor(f"e_ps_h{i}", [P, 512], F32)) for i in range(2)]
        ps_y = ctx.enter_context(nc.psum_tensor("e_ps_y", [P, 512], F32))
        ps_x = ctx.enter_context(nc.psum_tensor("e_ps_x", [P, 512], F32))
        ps_l, ps_r = ps_x[:, D:D + TT * E], ps_x[:, D + TT * E:D + TT * E + (TT + 1) * E]

        chain, logits_ready = sem("e_chain"), sem("e_logits_ready")
        diff_ready, ex_ready = sem("e_diff_ready"), sem("e_ex_ready")
        taken_ready, rank_ready, mine_ready = sem("e_taken_ready"), sem("e_rank_ready"), sem("e_mine_ready")
        owner_ready, slot_ready, sel_ready = sem("e_owner_ready"), sem("e_slot_ready"), sem("e_sel_ready")
        scattered = sem("e_scattered")
        w_loaded = [[sem(f"e_w{m + 1}_loaded{b}") for b in range(BUFS)] for m in range(2)]
        x_loaded = [sem(f"e_x_loaded{b}") for b in range(BUFS)]
        y_stored = [sem(f"e_y_stored{b}") for b in range(BUFS)]
        y_back = [sem(f"e_y_back{t}") for t in range(TT)]
        x_turned, xTh_ready, xT_ready = sem("e_x_turned"), sem("e_xTh_ready"), sem("e_xT_ready")
        high_done, split_done = sem("e_high_done"), sem("e_split_done")
        gates_done, values_done, gelu_done = sem("e_gates_done"), sem("e_values_done"), sem("e_gelu_done")
        hid_done, hid_turned, hidT_ready = sem("e_hid_done"), sem("e_hid_turned"), sem("e_hidT_ready")
        down_done, y_taken, out_ready = sem("e_down_done"), sem("e_y_taken"), sem("e_out_ready")
        stored = sem("e_stored")
        block = ctx.enter_context(nc.Block())

        def all_tiles(eng, one, tail=None, routed_only=False):
            if not routed_only:
                for t in range(TT):
                    one("shared", t, 0, 0)
            for b in range(BUFS):
                one("routed", TT + b, 0, b)
            with eng.Fori(1, RTILES // BUFS - 1) as turn:
                for b in range(BUFS):
                    one("routed", turn * BUFS + (TT + b), turn, b)
            last = RTILES // BUFS - 1
            for b in range(BUFS):
                one("routed", TT + last * BUFS + b, last, b)
            if tail:
                tail()

        def known(v, below):
            return isinstance(v, int) and v < below

        def behind(kind, T, turn, b, half, back):
            if half >= back:
                return kind, T, turn, b, half - back
            if kind == "shared" or known(T, TT + 1):
                return "shared", T - 1, 0, 0, half + 2 - back
            return kind, T - 1, (turn if b else turn - 1), (b - 1) % BUFS, half + 2 - back

        def width(kind):
            return (HS if kind == "shared" else HR) // 2

        def next_tile(kind, T, turn, b):
            if kind == "shared":
                return (TT, 0, 0) if T == TT - 1 else None
            if isinstance(T, int) and T == TT + RTILES - 1:
                return None
            return T + 1, (turn if b < BUFS - 1 else turn + 1), (b + 1) % BUFS

        def columns(w, half):
            return w[:, :].rearrange("p (c n) -> p c n", n=HR)[:, :, half * HR // 2:(half + 1) * HR // 2]

        @block.sync
        def _(sp):
            def load_x(T, turn, b):
                if not known(turn, 1):
                    sp.wait_ge(x_turned, T - TT - BUFS + 1)
                sp.dma_start(xg[b][:, :], d["x_slots"][bass.ds((T - TT) * P, P), :]).then_inc(x_loaded[b], 16)

            def one(kind, T, turn, b):
                if not (isinstance(turn, int) and turn == RTILES // BUFS - 1):
                    load_x(T + BUFS, turn + 1, b)
                sp.wait_ge(y_taken, T + 1)
                sp.dma_start(d["y_slots"][bass.ds((T - TT) * P, P), :], y[b][:, :]).then_inc(y_stored[b], 16)

            sp.wait_ge(scattered, 16 * 2 * TT)
            for b in range(BUFS):
                load_x(TT + b, 0, b)
            all_tiles(sp, one, routed_only=True)
            for t in range(TT):
                sp.wait_ge(out_ready, t + 1)
                sp.dma_start(d["out"][t * P:(t + 1) * P, :], sb["x"][:, t, :]).then_inc(stored, 16)
            sp.wait_ge(stored, 16 * TT)

        @block.gpsimd
        def _(pool):
            pool.wait_ge(f["slots_cleared"], 16)
            pool.wait_ge(slot_ready, 1)
            for t in range(TT):
                for i in range(2):
                    j = 2 * t + i
                    pool.indirect_dma_start(d["x_slots"][:, :],
                                            bass.IndirectOffsetOnAxis(ap=slot[:, j:j + 1], axis=0),
                                            f["xln"][:, t, :], None).then_inc(scattered, 16)
            pool.wait_ge(owner_ready, 1)
            for i in range(RTILES):
                for m, (w, used) in enumerate(((w1, values_done), (w2, down_done))):
                    if i >= BUFS:
                        pool.wait_ge(used, 2 * (TT + i - BUFS + 1))
                    pool.indirect_dma_start(w[i % BUFS][:, :], None, d[("we1", "we2")[m]][:, :],
                                            bass.IndirectOffsetOnAxis(ap=weight_row[:, i:i + 1], axis=0))\
                        .then_inc(w_loaded[m][i % BUFS], 16)
            for b in range(BUFS):
                pool.wait_ge(y_stored[b], 16 * RTILES // BUFS)
            for t in range(TT):
                for i in range(2):
                    j = 2 * t + i
                    pool.indirect_dma_start(back[:, t, i, :], None, d["y_slots"][:, :],
                                            bass.IndirectOffsetOnAxis(ap=slot[:, j:j + 1], axis=0))\
                        .then_inc(y_back[t], 16)

        @block.tensor
        def _(pe):
            def up(kind, T, turn, b, half):
                w, q = width(kind), T * 2 + half
                if kind == "shared":
                    passes = [(sb["xlnT"][:, :, T * P:(T + 1) * P], None)]
                    biases, n = f["sel_shared"][:, :], 2 * HS
                else:
                    passes = [(xTh[b][:, :, :], w1h), (xTl[b][:, :, :], w1h), (xTh[b][:, :, :], w1l)]
                    biases, n = sel[:, bass.ds(T - TT, 1), :].rearrange("p a s -> p (a s)"), 2 * HR
                    if half == 0:
                        pe.wait_ge(xT_ready, T - TT + 1)
                        if known(T, TT + 1):
                            pe.wait_ge(sel_ready, 1)
                    pe.wait_ge(split_done, (T - TT) * 2 + half + 1)
                if not known(q, 2):
                    pe.wait_ge(hid_done, q - 1)
                for j, ps, col, done in ((1, ps_g, n // 2 + half * w, gates_done), (0, ps_a, half * w, values_done)):
                    nc.tensor.matmul(ps[half][:, 0:w], biases, f["biases"][:, col:col + w], start=True, stop=False)
                    for k in range(KD):
                        for i, (rows, part) in enumerate(passes):
                            weights = part[half][:, 2 * k + j, :] if part else f["ws1"][:, k, col:col + w]
                            ins = nc.tensor.matmul(ps[half][:, 0:w], rows[:, k, :], weights,
                                                   start=False, stop=(k == KD - 1 and i == len(passes) - 1))
                    ins.then_inc(done, 1)

            def turn_hidden(kind, T, turn, b, half):
                q = T * 2 + half
                pe.wait_ge(hid_done, q + 1)
                if not known(q, 2):
                    pe.wait_ge(hidT_ready, q - 1)
                for c in range(width(kind) // P):
                    ins = nc.tensor.transpose(ps_h[half][:, c * P:(c + 1) * P], hid[:, half, c * P:(c + 1) * P],
                                              sb["ident"][:, :])
                ins.then_inc(hid_turned, 1)

            def down(kind, T, turn, b, half):
                q, chunks = T * 2 + half, width(kind) // P
                if kind == "shared":
                    weights, biases = f["ws2"][:, :, :], f["sel_shared"][:, :]
                else:
                    weights = w2[b][:, :].rearrange("p (c n) -> p c n", c=HR // P)
                    biases = sel[:, bass.ds(T - TT, 1), :].rearrange("p a s -> p (a s)")
                if half == 0:
                    if kind == "routed":
                        pe.wait_ge(w_loaded[1][b], (turn + 1) * 16)
                    if not known(T, 1):
                        pe.wait_ge(y_taken, T)
                    nc.tensor.matmul(ps_y[:, 0:D], biases, f["biases"][:, 2 * HR:2 * HR + D], start=True, stop=False)
                pe.wait_ge(hidT_ready, q + 1)
                for c in range(chunks):
                    ins = nc.tensor.matmul(ps_y[:, 0:D], hidT[:, half, c * P:(c + 1) * P],
                                           weights[:, half * chunks + c, :], start=False,
                                           stop=(half == 1 and c == chunks - 1))
                ins.then_inc(down_done, 1)

            def turn_x(T, turn, b):
                pe.wait_ge(x_loaded[b], (turn + 1) * 16)
                if not known(T, TT + 1):
                    pe.wait_ge(xT_ready, T - TT)
                for c in range(KD):
                    ins = nc.tensor.transpose(ps_x[:, c * P:(c + 1) * P], xg[b][:, c * P:(c + 1) * P],
                                              sb["ident"][:, :])
                ins.then_inc(x_turned, 1)

            def one(kind, T, turn, b):
                for half in range(2):
                    up(kind, T, turn, b, half)
                    if half == 0:
                        if next_tile(kind, T, turn, b):
                            turn_x(*next_tile(kind, T, turn, b))
                    if not known(T * 2 + half, 1):
                        turn_hidden(*behind(kind, T, turn, b, half, 1))
                    if not known(T * 2 + half, 2):
                        down(*behind(kind, T, turn, b, half, 2))
                if kind == "shared" and T == 0:
                    count()

            def count():
                pe.wait_ge(taken_ready, 1)
                nc.tensor.matmul(ps_r, f["before"][:, :], f["taken"][:, :, :].rearrange("p t e -> p (t e)"),
                                 start=True, stop=False,
                                 skip_group_check=True)
                for t in range(TT):
                    ins = nc.tensor.matmul(
                        ps_r[:, (t + 1) * E:].rearrange("p (t e) -> p t e", e=E), f["all"][:, :],
                        f["taken"][:, t:t + 1, :].broadcast_to([P, TT - t, E]), start=False, stop=(t == TT - 1),
                        skip_group_check=True)
                ins.then_inc(rank_ready, 1)

            def tail():
                last, b = TT + RTILES - 1, BUFS - 1
                turn_hidden("routed", last, RTILES // BUFS - 1, b, 1)
                for half in range(2):
                    down("routed", last, RTILES // BUFS - 1, b, half)

            pe.wait_ge(f["wr_loaded"], 32)
            for t in range(TT):
                for k in range(KD):
                    ins = nc.tensor.matmul(ps_l[:, t * E:(t + 1) * E], sb["xlnT"][:, k, t * P:(t + 1) * P],
                                           f["wr"][:, k, :], start=(k == 0), stop=(k == KD - 1))
            ins.then_inc(logits_ready, 1)
            pe.wait_ge(f["ws_loaded"], 32)
            all_tiles(pe, one, tail)

        @block.scalar
        def _(act):
            def gelu(kind, T, turn, b, half):
                w, q = width(kind), T * 2 + half
                act.wait_ge(gates_done, q + 1)
                if not known(q, 2):
                    act.wait_ge(hid_done, q - 1)
                nc.scalar.activation(gel[:, half, 0:w], ps_g[half][:, 0:w], ACT.Gelu).then_inc(gelu_done, 1)

            def take_turned(kind, T, turn, b, half):
                w, q = width(kind), T * 2 + half
                act.wait_ge(hid_turned, q + 1)
                if not known(q, 2):
                    act.wait_ge(down_done, q - 1)
                nc.scalar.copy(hidT[:, half, 0:w], ps_h[half][:, 0:w]).then_inc(hidT_ready, 1)

            def split_high(T, turn, b, half):
                act.wait_ge(w_loaded[0][b], (turn + 1) * 16)
                if not known(T, TT + 1):
                    act.wait_ge(values_done, T * 2 + half - 1)
                nc.scalar.copy(w1h[half][:, :, :], columns(w1[b], half)).then_inc(high_done, 1)

            def take_x_high(T, turn, b):
                act.wait_ge(x_turned, T - TT + 1)
                nc.scalar.copy(xTh[b][:, :, :].rearrange("p c s -> p (c s)"), ps_x[:, 0:D]).then_inc(xTh_ready, 1)

            def one(kind, T, turn, b):
                after = next_tile(kind, T, turn, b)
                for half in range(2):
                    if kind == "routed" and half == 0:
                        split_high(T, turn, b, 1)
                    elif after and half == 1:
                        split_high(*after, 0)
                    gelu(kind, T, turn, b, half)
                    if not known(T * 2 + half, 1):
                        take_turned(*behind(kind, T, turn, b, half, 1))
                    if after and half == 0:
                        take_x_high(*after)
                if kind == "shared" and T == 1:
                    act.wait_ge(mine_ready, 1)
                    nc.scalar.copy(sel[:, :, :], mine[:, :].unsqueeze(2).broadcast_to([96, RTILES, P]))\
                        .then_inc(sel_ready, 1)

            def tail():
                take_turned("routed", TT + RTILES - 1, RTILES // BUFS - 1, BUFS - 1, 1)

            act.wait_ge(diff_ready, 1)
            nc.scalar.activation(ex[:, :], diff[:, :], ACT.Exp).then_inc(ex_ready, 1)
            all_tiles(act, one, tail)

        @block.vector
        def _(dve):
            c = Chain(dve, chain)

            def choose():
                dve.wait_ge(logits_ready, 1)
                c.link(nc.vector.tensor_tensor(logit[:, :, :], ps_l.rearrange("p (t e) -> p t e", t=TT),
                                               f["br"][:, :].unsqueeze(1).broadcast_to([P, TT, E]), ALU.add))
                c.link(nc.vector.tensor_scalar(logit[:, :, :], logit[:, :, :], 1.0 / TAU, None, ALU.mult))
                for t in range(TT):
                    c.did(nc.vector.max(top[:, t, :], logit[:, t, :]))
                c.wait()
                nc.vector.tensor_tensor(diff[:, :], top[:, :, 1], top[:, :, 0], ALU.subtract).then_inc(diff_ready, 1)
                for t in range(TT):
                    c.did(nc.vector.max_index(at[:, t, :], top[:, t, :], logit[:, t, :]))
                c.wait()
                c.link(nc.vector.tensor_copy(atf[:, :, :], at[:, :, 0:2]))
                c.link(nc.vector.tensor_tensor(
                    pick[:, :, :, :].rearrange("p t i e -> p (t i) e"),
                    f["experts"][:, :].unsqueeze(1).broadcast_to([P, TT * 2, E]),
                    atf[:, :, :].rearrange("p t i -> p (t i)").unsqueeze(2).broadcast_to([P, TT * 2, E]), ALU.is_equal))
                nc.vector.tensor_tensor(f["taken"][:, 0:TT, :], pick[:, :, 0, :], pick[:, :, 1, :], ALU.add)\
                    .then_inc(taken_ready, 1)

            def weigh():
                dve.wait_ge(ex_ready, 1)
                c.link(nc.vector.tensor_scalar(den[:, :], ex[:, :], 1.0, None, ALU.add))
                c.link(nc.vector.reciprocal(share[:, :, 0], den[:, :]))
                c.link(nc.vector.tensor_tensor(share[:, :, 1], ex[:, :], share[:, :, 0], ALU.mult))

            def assign_tiles():
                dve.wait_ge(rank_ready, 1)
                c.link(nc.vector.tensor_copy(rank[:, :, :].rearrange("p t e -> p (t e)"), ps_r))
                c.link(nc.vector.tensor_tensor(above[:, :, :], rank[:, TT, :].unsqueeze(2).broadcast_to([P, E, TT]),
                                               f["full"][:, :].unsqueeze(1).broadcast_to([P, E, TT]), ALU.is_gt))
                c.link(nc.vector.tensor_reduce(tiles[:, :], above[:, :, :], AX_X, ALU.add))
                c.link(nc.vector.tensor_tensor_scan(upto[:, :], f["one"][:, :], tiles[:, :], 0.0, ALU.mult, ALU.add))

            def assign_owners():
                c.link(nc.vector.tensor_tensor(passed[:, :, :],
                                               f["tile_no"][:, :].unsqueeze(2).broadcast_to([P, RTILES, E]),
                                               upto[:, :].unsqueeze(1).broadcast_to([P, RTILES, E]), ALU.is_ge))
                c.link(nc.vector.tensor_reduce(owner[:, :], passed[:, :, :], AX_X, ALU.add))
                c.link(nc.vector.tensor_scalar(owner[:, :], owner[:, :], float(E - 1), None, ALU.min))
                c.link(nc.vector.tensor_scalar(weight_row_f[:, :], owner[:, :], float(P), f["row"][:, 0:1],
                                               ALU.mult, ALU.add))
                nc.vector.tensor_copy(weight_row[:, :], weight_row_f[:, :]).then_inc(owner_ready, 1)
                nc.vector.tensor_scalar(mine[:, :], owner[0:96, :], f["part_row"][:, 0:1], None, ALU.is_equal)\
                    .then_inc(mine_ready, 1)

            def assign_rows():
                c.link(nc.vector.tensor_tensor(first[:, :], upto[:, :], tiles[:, :], ALU.subtract))
                c.link(nc.vector.scalar_tensor_tensor(out=place[:, :, :],
                                                      in0=first[:, :].unsqueeze(1).broadcast_to([P, TT, E]),
                                                      scalar=float(P), in1=rank[:, 0:TT, :], op0=ALU.mult, op1=ALU.add))
                for i in range(2):
                    c.did(nc.vector.tensor_tensor(placed[:, :, i, :], pick[:, :, i, :], place[:, :, :], ALU.mult))
                c.wait()
                c.link(nc.vector.tensor_reduce(slot_f[:, :, :].rearrange("p t i -> p (t i)"),
                                               placed[:, :, :, :].rearrange("p t i e -> p (t i) e"), AX_X, ALU.add))
                nc.vector.tensor_copy(slot[:, :], slot_f[:, :, :].rearrange("p t i -> p (t i)")).then_inc(slot_ready, 1)

            def multiply(kind, T, turn, b, half):
                w, q = width(kind), T * 2 + half
                dve.wait_ge(gelu_done, q + 1)
                dve.wait_ge(values_done, q + 1)
                if not known(q, 2):
                    dve.wait_ge(hid_turned, q - 1)
                nc.vector.tensor_tensor(hid[:, half, 0:w], ps_a[half][:, 0:w], gel[:, half, 0:w], ALU.mult)\
                    .then_inc(hid_done, 1)

            def take_x_low(T, turn, b):
                dve.wait_ge(xTh_ready, T - TT + 1)
                nc.vector.tensor_tensor(xTl[b][:, :, :].rearrange("p c s -> p (c s)"), ps_x[:, 0:D],
                                        xTh[b][:, :, :].rearrange("p c s -> p (c s)").bitcast(F32), ALU.subtract)\
                    .then_inc(xT_ready, 1)

            def split_low(T, turn, b, half):
                dve.wait_ge(high_done, (T - TT) * 2 + half + 1)
                nc.vector.tensor_tensor(w1l[half][:, :, :], columns(w1[b], half), w1h[half][:, :, :].bitcast(F32),
                                        ALU.subtract).then_inc(split_done, 1)

            def take_y(kind, T, turn, b):
                dve.wait_ge(down_done, T * 2 + 2)
                if kind == "shared":
                    nc.vector.tensor_tensor(sb["x"][:, T, :], sb["x"][:, T, :], ps_y[:, 0:D], ALU.add)\
                        .then_inc(y_taken, 1)
                else:
                    if not known(turn, 1):
                        dve.wait_ge(y_stored[b], turn * 16)
                    nc.vector.tensor_copy(y[b][:, :], ps_y[:, 0:D]).then_inc(y_taken, 1)

            def one(kind, T, turn, b):
                after = next_tile(kind, T, turn, b)
                if kind == "routed":
                    split_low(T, turn, b, 1)
                multiply(kind, T, turn, b, 0)
                if after:
                    take_x_low(*after)
                    split_low(*after, 0)
                multiply(kind, T, turn, b, 1)
                if not known(T, 1):
                    take_y(*behind(kind, T, turn, b, 0, 1)[:4])
                if kind == "shared" and T == 0:
                    weigh()
                    assign_tiles()
                    assign_rows()
                    assign_owners()

            def tail():
                take_y("routed", TT + RTILES - 1, RTILES // BUFS - 1, BUFS - 1)
                for t in range(TT):
                    dve.wait_ge(y_back[t], 32)
                    for i in range(2):
                        if i == 1:
                            c.wait()
                        ins = nc.vector.scalar_tensor_tensor(out=sb["x"][:, t, :], in0=back[:, t, i, :],
                                                             scalar=share[:, t, i:i + 1], in1=sb["x"][:, t, :],
                                                             op0=ALU.mult, op1=ALU.add)
                        if i == 0:
                            c.did(ins)
                    ins.then_inc(out_ready, 1)

            choose()
            all_tiles(dve, one, tail)


def perceiver_layer(nc, d):
    with ExitStack() as ctx:
        def sbuf(name, shape, dt=F32, to=ctx):
            return to.enter_context(nc.sbuf_tensor(name, shape, dt))

        sb = {"x": sbuf("x_sb", [P, TT, D]), "xlnT": sbuf("xlnT", [P, KD, TOK]), "ident": sbuf("ident", [P, P]),
              "hmask": sbuf("hmask", [P, HC]), "qmask": sbuf("qmask", [P, KD * HQ]),
              "minus_half": sbuf("minus_half", [P, TT]), "zeros": sbuf("zeros", [P, D])}
        slots_cleared = ctx.enter_context(nc.semaphore("slots_cleared"))
        f = {n: ctx.enter_context(nc.semaphore(n)) for n in ("wr_loaded", "bias_loaded", "ws_loaded")}
        f["slots_cleared"] = slots_cleared
        f.update({n: sbuf(n, s, dt) for n, s, dt in (
            ("wr", [P, KD, E], F32), ("br", [P, E], F32), ("experts", [P, E], F32), ("row", [P, 1], F32),
            ("part_row", [96, 1], F32), ("tile_no", [P, RTILES], F32), ("full", [P, TT], F32), ("one", [P, E], F32),
            ("before", [P, P], BF16), ("all", [P, P], BF16), ("taken", [P, TT + 1, E], BF16),
            ("sel_shared", [96, P], BF16), ("biases", [96, 2 * HR + D], BF16))})
        with ExitStack() as ssm:
            ssm_loaded = ssm.enter_context(nc.semaphore("ssm_loaded"))
            m = {n: sbuf(n, s, dt, to=ssm) for n, s, dt in (
                ("wzx", [P, KD, 2 * DI], F32), ("wb", [P, KD, P], F32), ("wc", [P, KD, P], F32),
                ("wdt", [P, KD, NH], F32), ("convw", [P, XC, 4], F32), ("convb", [P, XC], F32), ("dtb", [NH, 1], F32),
                ("A", [P, XC * UNITS], F32), ("sel", [96, 16, 2, NS], BF16), ("seldt", [3 * NH, NH, P], BF16),
                ("fold", [P, 16, 32], F32), ("ones", [P, 1], F32), ("dskip", [P, XC], F32), ("nw", [P, XC], F32),
                ("w_out", [P, XC, D], F32))}
            with ExitStack() as part:
                a = {n: part.enter_context(nc.semaphore(f"a_{n}")) for n in ("q_loaded", "loaded")}
                a["ctx_loaded"] = [[part.enter_context(nc.semaphore(f"ctx_loaded{b}_{h}")) for h in range(2)]
                                   for b in range(2)]
                a["ctxT"] = [sbuf(f"ctxT{b}", [P, KD, S], to=part) for b in range(2)]
                a.update({n: sbuf(n, s, F32R if n[:2] == "qT" else F32, to=part) for n, s in (
                    ("qTh", [P, KD, TOK]), ("qTl", [P, KD, TOK]), ("oT", [P, KD, TOK]), ("wk", [P, KD, D]),
                    ("wv", [P, KD, D]), ("wo", [P, KD, D]), ("bk", [P, KD]), ("bv", [P, D]), ("bo", [P, D]))})
                with ExitStack() as early:
                    a.update({"wq": sbuf("wq", [P, KD, D], to=early), "bq": sbuf("bq", [P, KD], to=early)})
                    load_inputs(nc, d, sb)
                    layer_norm(nc, sb, "ln1", loads=lambda sp: load_weights(sp, d, sb, a, m, ssm_loaded, slots_cleared))
                    query_projection(nc, sb, a)
                attention(nc, d, sb, a, m)
                output_projection(nc, sb, a)
            layer_norm(nc, sb, "ln2")
            f.update({n: sbuf(n, s, dt, to=ssm) for n, s, dt in (
                ("ws1", [P, KD, 2 * HS], F32), ("ws2", [P, HS // P, D], F32))})
            with ExitStack() as part:
                m.update({n: sbuf(n, s, dt, to=part) for n, s, dt in (
                    ("xs", [P, XC, TOK], F32), ("yg", [P, XC, TOK], F32), ("BT", [P, TOK], F32), ("CT", [P, TOK], F32),
                    ("xs3", [96, 4 * XC, TOK], BF16), ("dt3", [3 * NH, TOK], BF16))})
                m["part"] = [sbuf(f"part{i}", [P, PARTS, TOK], BF16, to=part) for i in range(3)]
                moved = [part.enter_context(nc.semaphore(f"moved{i}")) for i in range(PARTS)]
                ssm_projections(nc, d, sb, m, f, ssm_loaded, moved)
                state_space(nc, sb, m, moved)
                ssm_output(nc, sb, m)
            f["xln"] = m["wzx"][:, :, :].rearrange("p k n -> p (k n)").rearrange("p (t d) -> p t d", t=TT)
            layer_norm(nc, sb, "ln3", f["xln"])
            experts(nc, d, sb, f)


def kernel(**inputs):
    import numpy as _np
    import concourse.bacc as _bacc
    from concourse import mybir as _mybir
    from concourse.bass_utils import run_bass_kernel_spmd as _run

    g = {k: _np.asarray(v) for k, v in inputs.items()}

    def by_feature(v):
        return v.reshape(-1, P).T

    lay = {
        "x": g["x"].reshape(TOK, D),
        "ctxT": g["ctx_1024"].transpose(0, 2, 1),
        "wq": g["L0_xattn_Wq"], "bq": by_feature(g["L0_xattn_bq"]), "wk": g["L0_xattn_Wk"], "bk": by_feature(g["L0_xattn_bk"]),
        "wv": g["L0_xattn_Wv"], "bv": g["L0_xattn_bv"], "wo": g["L0_xattn_Wo"], "bo": g["L0_xattn_bo"],
        "w_inT": g["L0_attn_W_in"].T,
        "w_conv": g["L0_attn_W_conv"].reshape(XC, P, 4).transpose(1, 0, 2),
        "b_conv": by_feature(g["L0_attn_b_conv"]),
        "a_log": g["L0_attn_A_log"].reshape(NH, HD // 2, 2, NS).transpose(2, 3, 0, 1).reshape(P, XC * UNITS),
        "dskip": by_feature(g["L0_attn_D"]), "dt_bias": g["L0_attn_dt_bias"],
        "norm_w": by_feature(g["L0_attn_norm_w"]),
        "w_outT": g["L0_attn_W_out"].T,
        "ws1": g["L0_ffn_Ws1"], "bs1": g["L0_ffn_bs1"].reshape(1, -1), "ws2": g["L0_ffn_Ws2"],
        "bs2": g["L0_ffn_bs2"].reshape(1, -1),
        "we1": g["L0_ffn_We1"].reshape(E, KD, P, 2 * HR).transpose(0, 2, 1, 3).reshape(E * P, KD * 2 * HR),
        "we2": g["L0_ffn_We2"].reshape(E, HR // P, P, D).transpose(0, 2, 1, 3).reshape(E * P, HR // P * D),
        "be1": g["L0_ffn_be1"], "be2": g["L0_ffn_be2"], "wr": g["L0_ffn_Wr"], "br": g["L0_ffn_br"],
    }
    nc = _bacc.Bacc("TRN2", target_bir_lowering=False, num_devices=1)
    arrays, d = {}, {}
    for name, v in lay.items():
        v = _np.ascontiguousarray(v)
        arrays[f"in_{name}_dram"] = v
        d[name] = nc.dram_tensor(f"in_{name}_dram", v.shape, _mybir.dt.from_np(v.dtype), kind="ExternalInput").ap()
    d["out"] = nc.dram_tensor("out_0_dram", (TOK, D), _mybir.dt.float32, kind="ExternalOutput").ap()
    for name in ("x_slots", "y_slots"):
        d[name] = nc.dram_tensor(name, (RTILES * P, D), _mybir.dt.float32, kind="Internal").ap()
    perceiver_layer(nc, d)
    r = _run(nc, [arrays], core_ids=[0])
    return r.results[0]["out_0_dram"].reshape(NB, L, D)
```
